# Optimizing a Trainium2 kernel written in Bass

```python
import numpy as np
import jax
import jax.numpy as jnp

def _softmax(x, axis=-1):
    return jax.nn.softmax(x, axis=axis)

def _gelu(x):
    return jax.nn.gelu(x, approximate=True)

def _silu(x):
    return jax.nn.silu(x)

def _sigmoid(x):
    return jax.nn.sigmoid(x)

def _layernorm(x, axis=-1, eps=1e-05):
    m = jnp.mean(x, axis=axis, keepdims=True)
    v = jnp.var(x, axis=axis, keepdims=True)
    return (x - m) / jnp.sqrt(v + eps)

def _scatter_add(tgt, idx, src, axis=0):
    return tgt.at[idx].add(src)

def _segment_sum(src, seg, n):
    return jax.ops.segment_sum(src, seg, n)
kernel_name = 'mk_decoder_postln_d1_seqx_r4_19af16'

def setup_inputs(seed: int=0):
    np.random.seed(seed)
    _w = jnp.asarray

    def _rec_inputs():
        import jax
        import jax.numpy as jnp
        _rk = jax.random.key(seed)
        x = 2.818e-05 + 1 * jax.random.normal(jax.random.fold_in(_rk, 1), (32, 128, 256), jnp.float32)
        _lenS = 128 - jax.random.randint(jax.random.fold_in(_rk, 7), (32,), 0, max(1, 128 // 4) + 1, jnp.int32)
        _lenS2 = 128 - jax.random.randint(jax.random.fold_in(_rk, 8), (32,), 0, max(1, 128 // 4) + 1, jnp.int32)
        _ctx_2048P = jax.random.normal(jax.random.fold_in(_rk, 11), (32, 16, 512), jnp.float32)
        _ctx_2048c = jax.random.dirichlet(jax.random.fold_in(_rk, 511), 0.3 * jnp.ones((16,), jnp.float32), (32, 128))
        _ctx_2048t = jnp.einsum('bsk,bkd->bsd', _ctx_2048c, _ctx_2048P)
        _ctx_2048t = _ctx_2048t * jax.lax.rsqrt(jnp.mean(jnp.square(_ctx_2048t)) + 1e-12) * 0.953939
        ctx_2048 = -0.000125008 + 0.999885 * (_ctx_2048t + 0.3 * jax.random.normal(jax.random.fold_in(_rk, 611), (32, 128, 512), jnp.float32))
        _validS = jnp.arange(128)[None, :] < _lenS[:, None]
        _validS2 = jnp.arange(128)[None, :] < _lenS2[:, None]
        _causal = jnp.tril(jnp.ones((128, 128), dtype=bool))
        mask_BxS2_fk1 = jnp.where(jnp.broadcast_to(_validS2[:, :], (32, 128)), 1.0, 0.0).astype(jnp.float32)
        return (x, ctx_2048, mask_BxS2_fk1)
    x, ctx_2048, mask_BxS2_fk1 = _rec_inputs()

    def _L0_attn_setup():
        import jax, jax.numpy as jnp
        import numpy as np
        B, L, D, H = (2, 512, 256, 4)
        DV = D // H
        P = 5
        CHUNK = 32
        CONV_K = 4
        FIR_K = (3, 15, 64)

        def _dwconv(x, w):
            K = w.shape[1]
            xt = jnp.pad(jnp.transpose(x, (0, 2, 1)), ((0, 0), (0, 0), (K - 1, 0)))
            y = jax.lax.conv_general_dilated(xt, w[:, None, :], (1,), 'VALID', dimension_numbers=('NCH', 'OIH', 'NCH'), feature_group_count=w.shape[0])
            return jnp.transpose(y, (0, 2, 1))

        def _l2norm(x):
            return x * jax.lax.rsqrt(jnp.sum(x * x, -1, keepdims=True) + 1e-06)

        def _delta_rule_chunkwise(q, k, v, beta, chunk=CHUNK):
            b, h, Lp, dk = q.shape
            dv = v.shape[-1]
            n = Lp // chunk
            q = _l2norm(q)
            k = _l2norm(k)
            v = v * beta[..., None]
            kb = k * beta[..., None]
            r = lambda t: t.reshape(b, h, n, chunk, -1)
            q, k, v, kb = (r(q), r(k), r(v), r(kb))
            sw = lambda t: jnp.swapaxes(t, -1, -2)
            strict = jnp.tril(jnp.ones((chunk, chunk), bool), -1)
            attn = jnp.where(strict, -(kb @ sw(k)), 0.0)
            T = jnp.linalg.inv(jnp.eye(chunk, dtype=q.dtype) - attn)
            u = T @ v
            w = T @ kb
            incl = jnp.tril(jnp.ones((chunk, chunk), bool), 0)
            qs, ks, us, ws = (jnp.moveaxis(t, 2, 0) for t in (q, k, u, w))
            S0 = jnp.zeros((b, h, dk, dv), q.dtype)

            def step(S, inp):
                q_i, k_i, u0, w_i = inp
                local = jnp.where(incl, q_i @ sw(k_i), 0.0)
                u_i = u0 - w_i @ S
                o_i = q_i @ S + local @ u_i
                return (S + sw(k_i) @ u_i, o_i)
            S, o = jax.lax.scan(step, S0, (qs, ks, us, ws))
            return (jnp.moveaxis(o, 0, 2).reshape(b, h, Lp, dv), S)

        def _stats(t):
            m = jnp.mean(t, -1, keepdims=True)
            v = jnp.mean(t * t, -1, keepdims=True)
            a = jnp.mean(jnp.abs(t), -1, keepdims=True)
            nrm = jnp.sqrt(jnp.sum(t * t, -1, keepdims=True))
            s = jnp.concatenate([jnp.broadcast_to(x, t.shape) for x in (m, v, a, nrm)], -1)
            return s.reshape(t.shape[0], t.shape[1], -1)

        def _forward(hs, Wq, Wk, Wv, conv_q, conv_k, conv_v, Wb, fir_s, fir_m, fir_l, gW1, gb1, gW2, gb2, log_tau, eps_logit, norm_w, Wo):
            b, Ln, _ = hs.shape
            q = jax.nn.silu(_dwconv(hs @ Wq, conv_q))
            k = jax.nn.silu(_dwconv(hs @ Wk, conv_k))
            v = jax.nn.silu(_dwconv(hs @ Wv, conv_v))
            beta = jax.nn.sigmoid(hs @ Wb)
            bh = lambda t: jnp.transpose(t.reshape(b, Ln, H, -1), (0, 2, 1, 3))
            o_d, _ = _delta_rule_chunkwise(bh(q), bh(k), bh(v), jnp.transpose(beta, (0, 2, 1)))
            delta_path = jnp.transpose(o_d, (0, 2, 1, 3))
            paths = jnp.stack([_dwconv(v, fir_s).reshape(b, Ln, H, DV), _dwconv(v, fir_m).reshape(b, Ln, H, DV), _dwconv(v, fir_l).reshape(b, Ln, H, DV), delta_path, v.reshape(b, Ln, H, DV)], axis=3)
            stats_flat = jnp.concatenate([_stats(paths[..., p, :]) for p in range(P)], -1)
            gate_in = jnp.concatenate([hs, stats_flat], -1)
            logits = jax.nn.gelu(gate_in @ gW1 + gb1, approximate=False) @ gW2 + gb2
            logits = logits.reshape(b, Ln, H, P)
            tau = jax.nn.softplus(log_tau) + 0.5
            probs = jax.nn.softmax(logits / tau[:, None], -1)
            eps = jax.nn.sigmoid(eps_logit) * 0.2
            probs = probs * (1.0 - jnp.sum(eps, -1, keepdims=True)) + eps
            o = jnp.einsum('blhp,blhpd->blhd', probs, paths)
            o = o * jax.lax.rsqrt(jnp.mean(o * o, -1, keepdims=True) + 1e-05) * norm_w
            return o.reshape(b, Ln, D) @ Wo
        key = jax.random.key(seed)
        ks = jax.random.split(key, 14)
        lin = lambda kk, fan_in, shape: jax.random.normal(kk, shape, jnp.float32) / np.float32(np.sqrt(fan_in))

        def fir(kk, K):
            w = np.zeros((D, K), np.float32)
            w[:, -1] = 1.0
            return jnp.asarray(w) + 0.001 * jax.random.normal(kk, (D, K), jnp.float32)
        in_gate = D + 4 * DV * H * P
        HF = 2 * D
        gb2 = np.zeros((H * P,), np.float32)
        gb2[np.arange(H) * P + P - 1] = 1.0
        return {'hidden_states': jax.random.normal(ks[0], (B, L, D), jnp.float32), 'Wq': lin(ks[1], D, (D, D)), 'Wk': lin(ks[2], D, (D, D)), 'Wv': lin(ks[3], D, (D, D)), 'conv_q': lin(ks[4], CONV_K, (D, CONV_K)), 'conv_k': lin(ks[5], CONV_K, (D, CONV_K)), 'conv_v': lin(ks[6], CONV_K, (D, CONV_K)), 'Wb': lin(ks[7], D, (D, H)), 'fir_s': fir(ks[8], FIR_K[0]), 'fir_m': fir(ks[9], FIR_K[1]), 'fir_l': fir(ks[10], FIR_K[2]), 'gW1': lin(ks[11], in_gate, (in_gate, HF)), 'gb1': jnp.zeros((HF,), jnp.float32), 'gW2': lin(ks[12], HF, (HF, H * P)), 'gb2': jnp.asarray(gb2), 'log_tau': jnp.zeros((H,), jnp.float32), 'eps_logit': jnp.zeros((H, P), jnp.float32), 'norm_w': jnp.ones((DV,), jnp.float32), 'Wo': lin(ks[13], D, (D, D))}
    _L0_attn_all = _L0_attn_setup()
    _L0_attn_in = {k: v for k, v in _L0_attn_all.items() if k in ('Wq', 'Wk', 'Wv', 'conv_q', 'conv_k', 'conv_v', 'Wb', 'fir_s', 'fir_m', 'fir_l', 'gW1', 'gb1', 'gW2', 'gb2', 'log_tau', 'eps_logit', 'norm_w', 'Wo')}
    del _L0_attn_all

    def _L0_xattn_setup():
        import jax, jax.numpy as jnp
        import numpy as np
        B, S, T = (32, 128, 128)
        SRC_SIZE, TGT_SIZE, OUT_SIZE, NUM_HEAD = (512, 256, 256, 8)
        HEAD_DIM = OUT_SIZE // NUM_HEAD
        key = jax.random.key(seed)
        ks = jax.random.split(key, 12)
        src = jax.random.normal(ks[0], (B, S, SRC_SIZE), dtype=jnp.float32)
        tgt = jax.random.normal(ks[1], (B, T, TGT_SIZE), dtype=jnp.float32)
        src_mask = (jax.random.uniform(ks[2], (B, S)) > 0.3).astype(jnp.float32)
        src_mask = src_mask.at[:, 0].set(1.0)
        tgt_mask = (jax.random.uniform(ks[3], (B, T)) > 0.3).astype(jnp.float32)
        tgt_mask = tgt_mask.at[:, 0].set(1.0)

        def lin(k, out_f, in_f):
            return jax.random.normal(k, (out_f, in_f), dtype=jnp.float32) / np.sqrt(in_f)
        W_src = lin(ks[4], 2 * OUT_SIZE, SRC_SIZE)
        b_src = jnp.zeros((2 * OUT_SIZE,), jnp.float32)
        W_tgt = lin(ks[5], OUT_SIZE, TGT_SIZE)
        b_tgt = jnp.zeros((OUT_SIZE,), jnp.float32)
        W_out = lin(ks[6], OUT_SIZE, OUT_SIZE + TGT_SIZE)
        b_out = jnp.zeros((OUT_SIZE,), jnp.float32)
        return {'src': src, 'tgt': tgt, 'src_mask': src_mask, 'tgt_mask': tgt_mask, 'W_src': W_src, 'b_src': b_src, 'W_tgt': W_tgt, 'b_tgt': b_tgt, 'W_out': W_out, 'b_out': b_out}
    _L0_xattn_all = _L0_xattn_setup()
    _L0_xattn_in = {k: v for k, v in _L0_xattn_all.items() if k in ('W_src', 'b_src', 'W_tgt', 'b_tgt', 'W_out', 'b_out')}
    del _L0_xattn_all

    def _L0_ffn_setup():
        import jax, jax.numpy as jnp
        import numpy as np
        H = 256
        E = 8
        K = 2
        I = 352
        B, S = (2, 256)

        def _moe_forward(x, w_router, wg, wu, wd, wg_s, wu_s, wd_s):
            b, s, h = x.shape
            xf = x.reshape(-1, h)
            scores = jax.nn.softmax(xf @ w_router.T, axis=-1)
            topk_w, topk_idx = jax.lax.top_k(scores, K)
            topk_w = topk_w / (topk_w.sum(axis=-1, keepdims=True) + 1e-20)
            cw = (jax.nn.one_hot(topk_idx, E, dtype=xf.dtype) * topk_w[..., None]).sum(axis=1)
            g = jnp.einsum('th,ehi->tei', xf, wg)
            u = jnp.einsum('th,ehi->tei', xf, wu)
            eo = jnp.einsum('tei,eih->teh', jax.nn.silu(g) * u, wd)
            y = jnp.einsum('te,teh->th', cw, eo)
            y = y + jax.nn.silu(xf @ wg_s) * (xf @ wu_s) @ wd_s
            return y.reshape(b, s, h)
        key = jax.random.key(seed)
        ks = jax.random.split(key, 8)
        sc = 0.02
        return {'x': jax.random.normal(ks[0], (B, S, H), dtype=jnp.float32), 'w_router': jax.random.normal(ks[1], (E, H), dtype=jnp.float32) * sc, 'wg': jax.random.normal(ks[2], (E, H, I), dtype=jnp.float32) * sc, 'wu': jax.random.normal(ks[3], (E, H, I), dtype=jnp.float32) * sc, 'wd': jax.random.normal(ks[4], (E, I, H), dtype=jnp.float32) * sc, 'wg_s': jax.random.normal(ks[5], (H, I), dtype=jnp.float32) * sc, 'wu_s': jax.random.normal(ks[6], (H, I), dtype=jnp.float32) * sc, 'wd_s': jax.random.normal(ks[7], (I, H), dtype=jnp.float32) * sc}
    _L0_ffn_all = _L0_ffn_setup()
    _L0_ffn_in = {k: v for k, v in _L0_ffn_all.items() if k in ('w_router', 'wg', 'wu', 'wd', 'wg_s', 'wu_s', 'wd_s')}
    del _L0_ffn_all
    return {'x': x, 'ctx_2048': ctx_2048, 'mask_BxS2_fk1': mask_BxS2_fk1, 'L0_attn_Wq': _L0_attn_in['Wq'], 'L0_attn_Wk': _L0_attn_in['Wk'], 'L0_attn_Wv': _L0_attn_in['Wv'], 'L0_attn_conv_q': _L0_attn_in['conv_q'], 'L0_attn_conv_k': _L0_attn_in['conv_k'], 'L0_attn_conv_v': _L0_attn_in['conv_v'], 'L0_attn_Wb': _L0_attn_in['Wb'], 'L0_attn_fir_s': _L0_attn_in['fir_s'], 'L0_attn_fir_m': _L0_attn_in['fir_m'], 'L0_attn_fir_l': _L0_attn_in['fir_l'], 'L0_attn_gW1': _L0_attn_in['gW1'], 'L0_attn_gb1': _L0_attn_in['gb1'], 'L0_attn_gW2': _L0_attn_in['gW2'], 'L0_attn_gb2': _L0_attn_in['gb2'], 'L0_attn_log_tau': _L0_attn_in['log_tau'], 'L0_attn_eps_logit': _L0_attn_in['eps_logit'], 'L0_attn_norm_w': _L0_attn_in['norm_w'], 'L0_attn_Wo': _L0_attn_in['Wo'], 'L0_xattn_W_src': _L0_xattn_in['W_src'], 'L0_xattn_b_src': _L0_xattn_in['b_src'], 'L0_xattn_W_tgt': _L0_xattn_in['W_tgt'], 'L0_xattn_b_tgt': _L0_xattn_in['b_tgt'], 'L0_xattn_W_out': _L0_xattn_in['W_out'], 'L0_xattn_b_out': _L0_xattn_in['b_out'], 'L0_ffn_w_router': _L0_ffn_in['w_router'], 'L0_ffn_wg': _L0_ffn_in['wg'], 'L0_ffn_wu': _L0_ffn_in['wu'], 'L0_ffn_wd': _L0_ffn_in['wd'], 'L0_ffn_wg_s': _L0_ffn_in['wg_s'], 'L0_ffn_wu_s': _L0_ffn_in['wu_s'], 'L0_ffn_wd_s': _L0_ffn_in['wd_s']}

def reference(x, ctx_2048, mask_BxS2_fk1, L0_attn_Wq, L0_attn_Wk, L0_attn_Wv, L0_attn_conv_q, L0_attn_conv_k, L0_attn_conv_v, L0_attn_Wb, L0_attn_fir_s, L0_attn_fir_m, L0_attn_fir_l, L0_attn_gW1, L0_attn_gb1, L0_attn_gW2, L0_attn_gb2, L0_attn_log_tau, L0_attn_eps_logit, L0_attn_norm_w, L0_attn_Wo, L0_xattn_W_src, L0_xattn_b_src, L0_xattn_W_tgt, L0_xattn_b_tgt, L0_xattn_W_out, L0_xattn_b_out, L0_ffn_w_router, L0_ffn_wg, L0_ffn_wu, L0_ffn_wd, L0_ffn_wg_s, L0_ffn_wu_s, L0_ffn_wd_s):
    import jax
    import jax.numpy as jnp

    def _L0_attn_ref(hidden_states, Wq, Wk, Wv, conv_q, conv_k, conv_v, Wb, fir_s, fir_m, fir_l, gW1, gb1, gW2, gb2, log_tau, eps_logit, norm_w, Wo):
        import jax, jax.numpy as jnp
        import numpy as np
        B, L, D, H = (2, 512, 256, 4)
        DV = D // H
        P = 5
        CHUNK = 32
        CONV_K = 4
        FIR_K = (3, 15, 64)

        def _dwconv(x, w):
            K = w.shape[1]
            xt = jnp.pad(jnp.transpose(x, (0, 2, 1)), ((0, 0), (0, 0), (K - 1, 0)))
            y = jax.lax.conv_general_dilated(xt, w[:, None, :], (1,), 'VALID', dimension_numbers=('NCH', 'OIH', 'NCH'), feature_group_count=w.shape[0])
            return jnp.transpose(y, (0, 2, 1))

        def _l2norm(x):
            return x * jax.lax.rsqrt(jnp.sum(x * x, -1, keepdims=True) + 1e-06)

        def _delta_rule_chunkwise(q, k, v, beta, chunk=CHUNK):
            b, h, Lp, dk = q.shape
            dv = v.shape[-1]
            n = Lp // chunk
            q = _l2norm(q)
            k = _l2norm(k)
            v = v * beta[..., None]
            kb = k * beta[..., None]
            r = lambda t: t.reshape(b, h, n, chunk, -1)
            q, k, v, kb = (r(q), r(k), r(v), r(kb))
            sw = lambda t: jnp.swapaxes(t, -1, -2)
            strict = jnp.tril(jnp.ones((chunk, chunk), bool), -1)
            attn = jnp.where(strict, -(kb @ sw(k)), 0.0)
            T = jnp.linalg.inv(jnp.eye(chunk, dtype=q.dtype) - attn)
            u = T @ v
            w = T @ kb
            incl = jnp.tril(jnp.ones((chunk, chunk), bool), 0)
            qs, ks, us, ws = (jnp.moveaxis(t, 2, 0) for t in (q, k, u, w))
            S0 = jnp.zeros((b, h, dk, dv), q.dtype)

            def step(S, inp):
                q_i, k_i, u0, w_i = inp
                local = jnp.where(incl, q_i @ sw(k_i), 0.0)
                u_i = u0 - w_i @ S
                o_i = q_i @ S + local @ u_i
                return (S + sw(k_i) @ u_i, o_i)
            S, o = jax.lax.scan(step, S0, (qs, ks, us, ws))
            return (jnp.moveaxis(o, 0, 2).reshape(b, h, Lp, dv), S)

        def _stats(t):
            m = jnp.mean(t, -1, keepdims=True)
            v = jnp.mean(t * t, -1, keepdims=True)
            a = jnp.mean(jnp.abs(t), -1, keepdims=True)
            nrm = jnp.sqrt(jnp.sum(t * t, -1, keepdims=True))
            s = jnp.concatenate([jnp.broadcast_to(x, t.shape) for x in (m, v, a, nrm)], -1)
            return s.reshape(t.shape[0], t.shape[1], -1)

        def _forward(hs, Wq, Wk, Wv, conv_q, conv_k, conv_v, Wb, fir_s, fir_m, fir_l, gW1, gb1, gW2, gb2, log_tau, eps_logit, norm_w, Wo):
            b, Ln, _ = hs.shape
            q = jax.nn.silu(_dwconv(hs @ Wq, conv_q))
            k = jax.nn.silu(_dwconv(hs @ Wk, conv_k))
            v = jax.nn.silu(_dwconv(hs @ Wv, conv_v))
            beta = jax.nn.sigmoid(hs @ Wb)
            bh = lambda t: jnp.transpose(t.reshape(b, Ln, H, -1), (0, 2, 1, 3))
            o_d, _ = _delta_rule_chunkwise(bh(q), bh(k), bh(v), jnp.transpose(beta, (0, 2, 1)))
            delta_path = jnp.transpose(o_d, (0, 2, 1, 3))
            paths = jnp.stack([_dwconv(v, fir_s).reshape(b, Ln, H, DV), _dwconv(v, fir_m).reshape(b, Ln, H, DV), _dwconv(v, fir_l).reshape(b, Ln, H, DV), delta_path, v.reshape(b, Ln, H, DV)], axis=3)
            stats_flat = jnp.concatenate([_stats(paths[..., p, :]) for p in range(P)], -1)
            gate_in = jnp.concatenate([hs, stats_flat], -1)
            logits = jax.nn.gelu(gate_in @ gW1 + gb1, approximate=False) @ gW2 + gb2
            logits = logits.reshape(b, Ln, H, P)
            tau = jax.nn.softplus(log_tau) + 0.5
            probs = jax.nn.softmax(logits / tau[:, None], -1)
            eps = jax.nn.sigmoid(eps_logit) * 0.2
            probs = probs * (1.0 - jnp.sum(eps, -1, keepdims=True)) + eps
            o = jnp.einsum('blhp,blhpd->blhd', probs, paths)
            o = o * jax.lax.rsqrt(jnp.mean(o * o, -1, keepdims=True) + 1e-05) * norm_w
            return o.reshape(b, Ln, D) @ Wo
        return _forward(hidden_states, Wq, Wk, Wv, conv_q, conv_k, conv_v, Wb, fir_s, fir_m, fir_l, gW1, gb1, gW2, gb2, log_tau, eps_logit, norm_w, Wo)

    def _L0_xattn_ref(src, tgt, src_mask, tgt_mask, W_src, b_src, W_tgt, b_tgt, W_out, b_out):
        import jax, jax.numpy as jnp
        import numpy as np
        B, S, T = (32, 128, 128)
        SRC_SIZE, TGT_SIZE, OUT_SIZE, NUM_HEAD = (512, 256, 256, 8)
        HEAD_DIM = OUT_SIZE // NUM_HEAD
        b, s, _ = src.shape
        t = tgt.shape[1]
        src_trans = jnp.einsum('bsf,of->bso', src, W_src) + b_src
        tgt_trans = jnp.einsum('btf,of->bto', tgt, W_tgt) + b_tgt
        src_trans = src_trans * src_mask[:, :, None]
        tgt_trans = tgt_trans * tgt_mask[:, :, None]
        src_key, src_val = jnp.split(src_trans, 2, axis=2)
        k = src_key.reshape(b, s, NUM_HEAD, HEAD_DIM)
        v = src_val.reshape(b, s, NUM_HEAD, HEAD_DIM)
        q = tgt_trans.reshape(b, t, NUM_HEAD, HEAD_DIM)
        scores = jnp.einsum('bthd,bshd->bhts', q, k) / np.sqrt(HEAD_DIM)
        scores = jnp.where(src_mask[:, None, None, :] == 0, -jnp.inf, scores)
        attn = jax.nn.softmax(scores, axis=-1)
        tgt_update = jnp.einsum('bhts,bshd->bthd', attn, v).reshape(b, t, OUT_SIZE)
        cat_tgt = jnp.concatenate([tgt, tgt_update], axis=2)
        return jnp.einsum('btf,of->bto', cat_tgt, W_out) + b_out

    def _L0_ffn_ref(x, w_router, wg, wu, wd, wg_s, wu_s, wd_s):
        import jax, jax.numpy as jnp
        import numpy as np
        H = 256
        E = 8
        K = 2
        I = 352
        B, S = (2, 256)

        def _moe_forward(x, w_router, wg, wu, wd, wg_s, wu_s, wd_s):
            b, s, h = x.shape
            xf = x.reshape(-1, h)
            scores = jax.nn.softmax(xf @ w_router.T, axis=-1)
            topk_w, topk_idx = jax.lax.top_k(scores, K)
            topk_w = topk_w / (topk_w.sum(axis=-1, keepdims=True) + 1e-20)
            cw = (jax.nn.one_hot(topk_idx, E, dtype=xf.dtype) * topk_w[..., None]).sum(axis=1)
            g = jnp.einsum('th,ehi->tei', xf, wg)
            u = jnp.einsum('th,ehi->tei', xf, wu)
            eo = jnp.einsum('tei,eih->teh', jax.nn.silu(g) * u, wd)
            y = jnp.einsum('te,teh->th', cw, eo)
            y = y + jax.nn.silu(xf @ wg_s) * (xf @ wu_s) @ wd_s
            return y.reshape(b, s, h)
        return _moe_forward(x, w_router, wg, wu, wd, wg_s, wu_s, wd_s)
    x = _layernorm(x + _L0_attn_ref(x, L0_attn_Wq, L0_attn_Wk, L0_attn_Wv, L0_attn_conv_q, L0_attn_conv_k, L0_attn_conv_v, L0_attn_Wb, L0_attn_fir_s, L0_attn_fir_m, L0_attn_fir_l, L0_attn_gW1, L0_attn_gb1, L0_attn_gW2, L0_attn_gb2, L0_attn_log_tau, L0_attn_eps_logit, L0_attn_norm_w, L0_attn_Wo), axis=-1)
    x = _layernorm(x + _L0_xattn_ref(ctx_2048, x, mask_BxS2_fk1, mask_BxS2_fk1, L0_xattn_W_src, L0_xattn_b_src, L0_xattn_W_tgt, L0_xattn_b_tgt, L0_xattn_W_out, L0_xattn_b_out), axis=-1)
    x = _layernorm(x + _L0_ffn_ref(x, L0_ffn_w_router, L0_ffn_wg, L0_ffn_wu, L0_ffn_wd, L0_ffn_wg_s, L0_ffn_wu_s, L0_ffn_wd_s), axis=-1)
    return x

_drawn_inputs = setup_inputs


def setup_inputs(seed=0):
    import zlib

    import numpy as np

    out = dict(_drawn_inputs(seed))
    spreads = {'L0_attn_gb1': (0.0, 2.0),
     'L0_attn_log_tau': (0.0, 2.0),
     'L0_attn_eps_logit': (0.0, 0.8),
     'L0_attn_norm_w': (1.0, 0.2),
     'L0_xattn_b_src': (0.0, 0.1),
     'L0_xattn_b_tgt': (0.0, 0.71),
     'L0_xattn_b_out': (0.0, 0.1)}
    factors = {'L0_attn_gW1': 10.827,
     'L0_attn_gb2': 5.209,
     'L0_ffn_w_router': 4.682,
     'L0_ffn_wg': 4.042,
     'L0_ffn_wu': 4.012,
     'L0_ffn_wd': 4.005,
     'L0_ffn_wg_s': 2.889,
     'L0_ffn_wu_s': 2.879,
     'L0_ffn_wd_s': 2.879}
    for name, (base, spread) in spreads.items():
        noise = np.random.default_rng([zlib.crc32(name.encode()), seed]).standard_normal(out[name].shape)
        drawn = base * np.exp(spread * noise) if base else spread * noise
        out[name] = jnp.asarray(drawn.astype(out[name].dtype))
    for name, factor in factors.items():
        out[name] = (out[name] * factor).astype(out[name].dtype)
    return out
```

```python
import math

import concourse.bass as bass
from concourse import mybir
from contextlib import ExitStack, contextmanager

B, L, D = 32, 128, 256
H, DV = 4, 64
NP = 5
TAPS = 4
FIRS = (3, 15, 64)
CTX = 512
XH, XD = 8, 32
GH = 512
NE, EH = 8, 352
KD = D // 128
BLK = 512
BB = BLK // L
NBLK = B * L // BLK
CB = 32
NC = L // CB
FC = 8
HALF = L // 2
NFC = D // FC
SLOT_TILES = 2 * B + NE
UNITS = B + SLOT_TILES
FIR_PAD = L + HALF - 1

fp32 = mybir.dt.float32
ALU = mybir.AluOpType
ACT = mybir.ActivationFunctionType
AX = mybir.AxisListType


def pair_loop(eng, count, step):
    with eng.Fori(0, count // 2) as j:
        step(j, 0)
        step(j, 1)


def skewed_pair_loop(eng, count, early, late):
    early(0, 0)
    with eng.Fori(0, count // 2 - 1) as j:
        early(j, 1)
        late(j, 0)
        early(j + 1, 0)
        late(j, 1)
    last = count // 2 - 1
    early(last, 1)
    late(last, 0)
    late(last, 1)


def wide(ap, shape, axis):
    return ap.unsqueeze(axis).broadcast_to(shape)


def staged_pair_loop(eng, count, *stages):
    most = max(lag for _, lag in stages)
    fill = most + most % 2

    def turn(n):
        for step, lag in stages:
            if 0 <= n - lag < count:
                step((n - lag) // 2, (n - lag) % 2)

    for n in range(fill):
        turn(n)
    with eng.Fori(fill // 2, count // 2) as j:
        for u in range(2):
            for step, lag in stages:
                step(j + (u - lag) // 2, (u - lag) % 2)
    for n in range(count, count + most):
        turn(n)


@contextmanager
def signals(nc):
    taken = []

    def signal(name):
        taken.append(nc.alloc_semaphore(name))
        return taken[-1]

    yield signal
    nc.clear_and_free_semaphores(taken)
    nc.all_engine_barrier()


class Memory:
    pass


def build_constants(nc, M):
    with signals(nc) as signal, ExitStack() as ctx:
        logtau = ctx.enter_context(nc.sbuf_tensor("logtau", [128, H], fp32))
        softp = ctx.enter_context(nc.sbuf_tensor("softp", [128, 3, H], fp32))
        epsl = ctx.enter_context(nc.sbuf_tensor("epsl", [128, H, NP], fp32))
        norm_w = ctx.enter_context(nc.sbuf_tensor("norm_w", [128, 1], fp32))
        loaded = signal("const_loaded")
        zeroed = signal("const_zeroed")
        act_step = signal("const_act_step")
        dve_step = signal("const_dve_step")
        block = ctx.enter_context(nc.Block())

        @block.sync
        def _(sp):
            sp.dma_start(logtau[:, :], M.log_tau.partition_broadcast(128)).then_inc(loaded, 16)
            sp.dma_start(epsl[:, :, :], M.eps_logit.partition_broadcast(128)).then_inc(loaded, 16)
            sp.dma_start(M.gb2[:, :], M.gb2_dram.partition_broadcast(128)).then_inc(loaded, 16)
            sp.dma_start(norm_w[0:DV, :], M.norm_w_dram).then_inc(loaded, 16)
            sp.dma_start(norm_w[DV:128, :], M.norm_w_dram).then_inc(loaded, 16)
            sp.dma_start(M.wo[:, :, :], M.wo_dram.rearrange("(k p) n -> p k n", p=128)).then_inc(loaded, 16)
            sp.dma_start(M.gw1x[:, :, :], M.gw1_dram[0:D, :].rearrange("(k p) n -> p k n", p=128)).then_inc(loaded, 16)
            sp.dma_start(M.gw2[:, :, :], M.gw2_dram.rearrange("(k p) n -> p k n", p=128)).then_inc(loaded, 16)
            sp.dma_start(M.gb1[:, :], M.gb1_dram).then_inc(loaded, 16)
            sp.dma_start(M.stat_scale[:, :], M.stat_scale_dram).then_inc(loaded, 16)
            sp.wait_ge(loaded, 160)

        @block.gpsimd
        def _(pool):
            pool.memset(M.ident[:, :], 0.0).then_inc(zeroed, 1)
            pool.memset(M.causal[:, :], 1.0).then_inc(zeroed, 1)
            for m in (M.reverse, M.reverse_first):
                pool.memset(m[:, :], 0.0).then_inc(zeroed, 1)
            pool.memset(M.minus_half[:, :], -0.5)
            pool.memset(M.plus_half[:, :], 0.5)
            pool.memset(M.euler[:, :], 2.718281828459045)
            pool.wait_ge(zeroed, 4)
            pool.affine_select(out=M.ident[:, :], in_=M.ident[:, :], compare_op=ALU.not_equal, fill=1.0,
                               base=0, pattern=[[-1, 128]], channel_multiplier=1)
            for m, last in ((M.reverse, L - 1), (M.reverse_first, HALF - 1)):
                pool.affine_select(out=m[:, :], in_=m[:, :], compare_op=ALU.not_equal, fill=1.0,
                                   base=-last, pattern=[[1, 128]], channel_multiplier=1)
            pool.affine_select(out=M.causal[:, :], in_=M.causal[:, :], compare_op=ALU.is_ge, fill=0.0,
                               base=0, pattern=[[1, 128]], channel_multiplier=-1)

        @block.scalar
        def _(act):
            act.wait_ge(loaded, 160)
            act.activation(softp[:, 0, :], logtau[:, :], ACT.Abs).then_inc(act_step, 1)
            act.wait_ge(act_step, 1)
            act.activation(softp[:, 1, :], softp[:, 0, :], ACT.Exp, scale=-1.0).then_inc(act_step, 1)
            act.wait_ge(act_step, 2)
            act.activation(softp[:, 2, :], softp[:, 1, :], ACT.Ln, bias=1.0).then_inc(act_step, 1)
            act.activation(epsl[:, :, :], epsl[:, :, :], ACT.Exp, scale=-1.0).then_inc(act_step, 1)

        @block.vector
        def _(dve):
            steps = [0]

            def link(ins):
                steps[0] += 1
                ins.then_inc(dve_step, 1)
                dve.wait_ge(dve_step, steps[0])

            for m in (M.off32, M.off64, M.blockdiag):
                link(dve.memset(m[:, :], 0.0))
            dve.memset(M.off32[0:32, 32:64], 1.0)
            dve.memset(M.off32[64:96, 96:128], 1.0)
            dve.memset(M.off64[0:64, 64:128], 1.0)
            for c in range(NC):
                dve.memset(M.blockdiag[c * CB:(c + 1) * CB, c * CB:(c + 1) * CB], 1.0)
            dve.wait_ge(loaded, 160)
            for k in range(KD):
                link(dve.tensor_scalar(M.wo[:, k, :], M.wo[:, k, :], norm_w[:, 0:1], None, ALU.mult))
            dve.wait_ge(act_step, 4)
            link(dve.tensor_scalar(logtau[:, :], logtau[:, :], 0.0, 0.5, ALU.max, ALU.add))
            link(dve.tensor_tensor(logtau[:, :], logtau[:, :], softp[:, 2, :], ALU.add))
            link(dve.reciprocal(M.inv_tau[:, :], logtau[:, :]))
            link(dve.tensor_scalar(epsl[:, :, :], epsl[:, :, :], 1.0, None, ALU.add))
            link(dve.reciprocal(epsl[:, :, :], epsl[:, :, :]))
            link(dve.tensor_scalar(M.floor[:, :, :], epsl[:, :, :], 0.2, None, ALU.mult))
            link(dve.tensor_reduce(M.keep[:, :], M.floor[:, :, :], AX.X, ALU.add))
            link(dve.tensor_scalar(M.keep[:, :], M.keep[:, :], -1.0, 1.0, ALU.mult, ALU.add))


def project(nc, M):
    NT = 3 * KD
    PB = 4
    USES = 2 * NT // PB
    with signals(nc) as signal, ExitStack() as ctx:
        def sb(name, shape):
            return ctx.enter_context(nc.sbuf_tensor(name, shape, fp32))

        def sem(name):
            return signal(name)

        wqkv = sb("wqkv", [128, 3, KD, D])
        taps = sb("conv_taps", [128, 3, KD, TAPS])
        wb = sb("wb", [128, KD, H])
        headsel = sb("headsel", [128, 2])
        xT = sb("xT_block", [128, 2, KD, BLK])
        conv = sb("conv_acc", [128, NT, BLK])
        qkv = sb("qkv_block", [128, 2, NT, BLK])
        squares = sb("qk_squares", [128, 2, 2 * KD, BLK])
        tanh_b = sb("tanh_beta", [128, 2, BB, H])
        ssq = sb("qk_ssq", [128, 2, BB, 2 * H])
        neg_decay = sb("neg_decay", [128, 2, BB, H])
        ndG = sb("decay_gram", [128, 2, H, L])
        GPART = DV // NBLK
        gsum = sb("gate_rows", [80, GPART, GH])
        gpart = sb("gate_part", [80, 2, GPART, GH])
        psum = ctx.enter_context(nc.psum_tensor("proj_psum", [128, 8, BLK], fp32))
        V_BANK, S_BANK, G_BANK = PB, PB + 1, PB + 2

        weights_in = sem("weights_in")
        xT_in = [sem(f"xT_in{u}") for u in range(2)]
        proj_done = sem("proj_done")
        tap3_done = sem("tap3_done")
        conv_done = [sem(f"conv_done{b}") for b in range(PB)]
        silu_done = sem("silu_done")
        qk_stored = [sem(f"qk_stored{u}") for u in range(2)]
        squares_done = sem("squares_done")
        small_done = [sem(f"small_done{u}") for u in range(2)]
        tanh_done = sem("tanh_done")
        ssq_done = sem("ssq_done")
        decay_done = sem("decay_done")
        vT_done = sem("vT_done")
        v_kept = sem("v_kept")
        gram_done = [sem(f"gram_done{u}") for u in range(2)]
        nd_done = [[sem(f"nd_done{u}{p}") for p in range(2)] for u in range(2)]
        nd_stored = [sem(f"nd_stored{u}") for u in range(2)]
        norm_done = sem("norm_done")
        decay_step = sem("decay_step")
        taps_step = sem("taps_step")
        gate_in = [sem(f"gate_in{u}") for u in range(2)]
        gate_step = sem("gate_step")
        sel_set = sem("sel_set")
        block = ctx.enter_context(nc.Block())

        def bank_use(u, m):
            return (NT * u + m) % PB, (NT * u + m) // PB

        @block.sync
        def _(sp):
            for i, w in enumerate((M.wq_dram, M.wk_dram, M.wv_dram)):
                sp.dma_start(wqkv[:, i, :, :], w.rearrange("(k p) n -> p k n", p=128)).then_inc(weights_in, 16)
            for i, w in enumerate((M.conv_q_dram, M.conv_k_dram, M.conv_v_dram)):
                sp.dma_start(taps[:, i, :, :], w.rearrange("(k p) n -> p k n", p=128)).then_inc(weights_in, 16)
            sp.dma_start(wb[:, :, :], M.wb_dram.rearrange("(k p) n -> p k n", p=128)).then_inc(weights_in, 16)

            def load_x(j, u):
                sp.wait_ge(small_done[u], j)
                sp.dma_start(xT[:, u, :, :],
                             M.xT_dram[:, bass.ds((2 * j + u) * BLK, BLK)].rearrange("(k p) n -> p k n", p=128)
                             ).then_inc(xT_in[u], 16)
                sp.wait_ge(gate_step, 2 * j + u)
                sp.dma_start(gpart[:, u, :, :], M.gw1s_dram[:, bass.ds((2 * j + u) * GPART, GPART), :]
                             ).then_inc(gate_in[u], 16)

            def store_qk(j, u):
                sp.wait_ge(silu_done, NT * (2 * j + u) + 2 * KD)
                for i, dst in enumerate((M.qT_dram, M.kT_dram)):
                    sp.dma_start(dst[:, bass.ds((2 * j + u) * BLK, BLK)].rearrange("(k p) n -> p k n", p=128),
                                 qkv[:, u, KD * i:KD * i + KD, :]).then_inc(qk_stored[u], 16)

            def store_decays(j, u):
                n = 2 * j + u
                for q in range(BB):
                    sp.wait_ge(nd_done[u][q % 2], 2 * j + q // 2 + 1)
                    for c in range(NC):
                        rows = slice(c * CB, c * CB + CB)
                        sp.dma_start(M.nd_dram[bass.ds(BB * n + q, 1), :, rows, :].rearrange("b h t c -> t (b h) c"),
                                       ndG[rows, q % 2, :, rows]).then_inc(nd_stored[q % 2], 16)

            def stores(j, u):
                store_qk(j, u)
                store_decays(j, u)

            skewed_pair_loop(sp, NBLK, load_x, stores)
            for u in range(2):
                sp.wait_ge(qk_stored[u], 32 * (NBLK // 2))
                sp.wait_ge(nd_stored[u], 64 * B // 2)

        @block.tensor
        def _(pe):
            def projections(j, u):
                pe.wait_ge(xT_in[u], 16 * (j + 1))
                for m in range(NT):
                    b, r = bank_use(u, m)
                    pe.wait_ge(conv_done[b], USES * j + r)
                    for k in range(KD):
                        mm = pe.matmul(psum[:, b, :], wqkv[:, m // KD, k, (m % KD) * 128:(m % KD) * 128 + 128],
                                       xT[:, u, k, :], start=(k == 0), stop=(k == KD - 1))
                    mm.then_inc(proj_done, 1)

            def derived(j, u):
                n = 2 * j + u
                pe.wait_ge(squares_done, 2 * KD * (n + 1))
                pe.wait_ge(tanh_done, n)
                pe.wait_ge(ssq_done, n)
                for q in range(BB):
                    tok = slice(q * L, q * L + L)
                    for t in range(2 * KD):
                        pe.matmul(psum[:, S_BANK, 12 * q + 2 * t:12 * q + 2 * t + 2], squares[:, u, t, tok],
                                  headsel[:, :], start=True, stop=True)
                    for k in range(KD):
                        mm = pe.matmul(psum[:, S_BANK, 12 * q + 8:12 * q + 12], xT[:, u, k, tok], wb[:, k, :],
                                       start=(k == 0), stop=(k == KD - 1))
                mm.then_inc(small_done[u], 1)
                pe.wait_ge(silu_done, NT * (n + 1))
                for g in range(BB // 2):
                    pe.wait_ge(v_kept, 2 * n + g)
                    for q in (2 * g, 2 * g + 1):
                        for t in range(KD):
                            at = (q % 2) * D + t * 128
                            mm = pe.transpose(psum[:, V_BANK, at:at + 128],
                                              qkv[:, u, 2 * KD + t, q * L:q * L + L], M.ident[:, :])
                    mm.then_inc(vT_done, 1)
                    for p in range(2):
                        if g == 1:
                            pe.wait_ge(nd_done[u][p], 2 * j + 1)
                        else:
                            pe.wait_ge(nd_done[1 - u][p], 2 * j + 2 * u)
                    for q in (2 * g, 2 * g + 1):
                        for h in range(H):
                            rows = slice((h % 2) * DV, (h % 2) * DV + DV)
                            at = (2 * (q % 2) + h // 2) * L
                            kT = qkv[rows, u, KD + h // 2, q * L:q * L + L]
                            mm = pe.matmul(psum[:, G_BANK + h % 2, at:at + L], kT, kT, start=True, stop=True)
                    mm.then_inc(gram_done[u], 1)

            pe.wait_ge(weights_in, 7 * 16)
            pe.wait_ge(sel_set, 1)
            skewed_pair_loop(pe, NBLK, projections, derived)

        @block.scalar
        def _(act):
            act.wait_ge(weights_in, 7 * 16)

            def scaled_tap(j, u, m):
                n = 2 * j + u
                b, r = bank_use(u, m)
                act.wait_ge(proj_done, NT * n + m + 1)
                act.wait_ge(silu_done, NT * n)
                act.activation(conv[:, m, :], psum[:, b, :], ACT.Copy,
                               scale=taps[:, m // KD, m % KD, TAPS - 1:TAPS]).then_inc(tap3_done, 1)

            def silu(j, u, m):
                b, r = bank_use(u, m)
                act.wait_ge(conv_done[b], USES * j + r + 1)
                if m == 0:
                    act.wait_ge(qk_stored[u], 32 * j)
                    act.wait_ge(gram_done[u], 2 * j)
                    act.wait_ge(squares_done, 2 * KD * 2 * j)
                act.activation(qkv[:, u, m, :], conv[:, m, :], ACT.Silu).then_inc(silu_done, 1)

            def convolved(j, u):
                for m in range(NT + 2):
                    if m < NT:
                        scaled_tap(j, u, m)
                    if m >= 2:
                        silu(j, u, m - 2)

            def small(j, u):
                n = 2 * j + u
                act.wait_ge(small_done[u], j + 1)
                act.wait_ge(decay_done, n)
                act.activation(tanh_b[:, u, :, :],
                               psum[:, S_BANK, 0:12 * BB].rearrange("p (q c) -> p q c", c=12)[:, :, 8:12],
                               ACT.Tanh, scale=0.5).then_inc(tanh_done, 1)
                for g in range(2):
                    act.wait_ge(vT_done, 2 * n + g + 1)
                    act.activation(M.value[:, bass.ds(BB * n + 2 * g, 2), :],
                                   psum[:, V_BANK, :].rearrange("p (q c) -> p q c", c=D),
                                   ACT.Copy).then_inc(v_kept, 1)

            skewed_pair_loop(act, NBLK, convolved, small)

        @block.vector
        def _(dve):
            dve.memset(headsel[:, :], 0.0).then_inc(taps_step, 1)
            dve.wait_ge(taps_step, 1)
            dve.memset(headsel[0:DV, 0:1], 1.0)
            dve.memset(headsel[DV:128, 1:2], 1.0).then_inc(sel_set, 1)
            dve.wait_ge(weights_in, 7 * 16)

            def convolutions(j, u):
                n = 2 * j + u
                for m0 in range(0, NT, 2):
                    for s in range(1, TAPS):
                        for m in (m0, m0 + 1):
                            b, _ = bank_use(u, m)
                            if s == 1:
                                dve.wait_ge(tap3_done, NT * n + m + 1)
                            else:
                                dve.wait_ge(taps_step, 1 + NT * (TAPS - 2) * n
                                            + m0 * (TAPS - 2) + 2 * (s - 2) + (m - m0) + 1)
                            acc = conv[:, m, :].rearrange("p (q t) -> p q t", t=L)
                            raw = psum[:, b, :].rearrange("p (q t) -> p q t", t=L)
                            ins = dve.scalar_tensor_tensor(
                                out=acc[:, :, s:L], in0=raw[:, :, 0:L - s],
                                scalar=taps[:, m // KD, m % KD, TAPS - 1 - s:TAPS - s],
                                in1=acc[:, :, s:L], op0=ALU.mult, op1=ALU.add)
                            ins.then_inc(taps_step if s < TAPS - 1 else conv_done[b], 1)

            def decays(j, u):
                n = 2 * j + u
                dve.wait_ge(small_done[u], j + 1)
                dve.wait_ge(tanh_done, n + 1)
                dve.wait_ge(decay_done, n)
                dve.tensor_scalar(ssq[:, u, :, :],
                                  psum[:, S_BANK, 0:12 * BB].rearrange("p (q c) -> p q c", c=12)[:, :, 0:8],
                                  1e-6, None, ALU.add).then_inc(ssq_done, 1)
                here = bass.ds(BB * n, BB)
                dve.tensor_scalar(tanh_b[:, u, :, :], tanh_b[:, u, :, :], 0.5, 0.5, ALU.mult,
                                  ALU.add).then_inc(decay_step, 1)
                dve.wait_ge(norm_done, n + 1)
                dve.tensor_copy(M.rq[:, here, :], ssq[:, u, :, 0:H])
                dve.wait_ge(decay_step, 3 * n + 1)
                dve.tensor_tensor(M.beta_r[:, here, :], tanh_b[:, u, :, :], ssq[:, u, :, H:2 * H],
                                  ALU.mult).then_inc(decay_step, 1)
                dve.wait_ge(decay_step, 3 * n + 2)
                dve.tensor_tensor(M.decay[:, here, :], M.beta_r[:, here, :], ssq[:, u, :, H:2 * H],
                                  ALU.mult).then_inc(decay_step, 1)
                dve.wait_ge(decay_step, 3 * n + 3)
                dve.tensor_scalar(neg_decay[:, u, :, :], M.decay[:, here, :], -1.0, None,
                                  ALU.mult).then_inc(decay_done, 1)
                dve.wait_ge(decay_done, n + 1)
                for q in range(BB):
                    dve.wait_ge(gram_done[u], 2 * j + q // 2 + 1)
                    dve.wait_ge(nd_stored[q % 2], 64 * (2 * n + q // 2))
                    dve.tensor_tensor(ndG[:, q % 2, :, :].rearrange("p (a b) t -> p b a t", b=2),
                                      psum[:, G_BANK:G_BANK + 2, (q % 2) * 2 * L:(q % 2) * 2 * L + 2 * L]
                                      .rearrange("p b (a t) -> p b a t", t=L),
                                      wide(neg_decay[:, u, q, :].rearrange("p (a b) -> p b a", b=2),
                                           [128, 2, 2, L], 3),
                                      ALU.mult).then_inc(nd_done[u][q % 2], 1)

            skewed_pair_loop(dve, NBLK, convolutions, decays)

        @block.gpsimd
        def _(pool):
            def square_qk(j, u):
                n = 2 * j + u
                pool.wait_ge(small_done[u], j)
                for t in range(2 * KD):
                    pool.wait_ge(silu_done, NT * n + t + 1)
                    pool.tensor_tensor(squares[:, u, t, :], qkv[:, u, t, :], qkv[:, u, t, :],
                                       ALU.mult).then_inc(squares_done, 1)

            def gate_rows(j, u):
                pool.wait_ge(gate_in[u], 16 * (j + 1))
                pool.wait_ge(gate_step, 2 * j + u + 1)
                pool.tensor_tensor(gsum[:, :, :], gsum[:, :, :], gpart[:, u, :, :], ALU.add).then_inc(gate_step, 1)

            def square_and_sum(j, u):
                square_qk(j, u)
                gate_rows(j, u)

            def inverse_norms(j, u):
                n = 2 * j + u
                pool.wait_ge(ssq_done, n + 1)
                pool.tensor_tensor(ssq[:, u, :, :], ssq[:, u, :, :],
                                   wide(wide(M.minus_half[:, 0], [128, 2 * H], 1), [128, BB, 2 * H], 1),
                                   ALU.pow).then_inc(norm_done, 1)

            pool.memset(gsum[:, :, :], 0.0).then_inc(gate_step, 1)
            skewed_pair_loop(pool, NBLK, square_and_sum, inverse_norms)

            done = NBLK + 1
            for half in (4, 2, 1):
                pool.wait_ge(gate_step, done)
                pool.tensor_tensor(gsum[:, 0:half, :], gsum[:, 0:half, :], gsum[:, half:2 * half, :],
                                   ALU.add).then_inc(gate_step, 1)
                done += 1
            pool.wait_ge(gate_step, done)
            pool.tensor_scalar(M.gw1s[:, :], gsum[:, 0, :], M.stat_scale[:, 0:1], None, ALU.mult)


def invert_and_filter(nc, M):
    NFIR = len(FIRS)
    with signals(nc) as signal, ExitStack() as ctx:
        def sb(name, shape):
            return ctx.enter_context(nc.sbuf_tensor(name, shape, fp32))

        def sem(name):
            return signal(name)

        nd = sb("neg_decay_blocks", [128, NC, CB, CB])
        inv = sb("inverses", [128, NC, CB, CB])
        prod = sb("products", [128, 2, 2, (CB - 1) * (CB - 1)])
        toep = sb("toep", [128, 2, NFIR, HALF, FC])
        window = sb("window", [128, 2, FC, 2, B])
        psum = ctx.enter_context(nc.psum_tensor("fir_psum", [128, 2, 3, FC * 2 * B], fp32))
        LONG, SHORT, WINDOW = range(3)

        nd_in = sem("nd_in")
        inv_row = [sem(f"inv_row{g}") for g in range(2)]
        inv_mul = [sem(f"inv_mul{g}") for g in range(2)]
        inv_set = sem("inv_set")
        inv_stored = sem("inv_stored")
        toep_in = [sem(f"toep_in{u}") for u in range(2)]
        window_done = [sem(f"window_done{u}") for u in range(2)]
        window_kept = [sem(f"window_kept{u}") for u in range(2)]
        fir_done = [sem(f"fir_done{u}") for u in range(2)]
        fir_kept = [sem(f"fir_kept{u}") for u in range(2)]
        block = ctx.enter_context(nc.Block())

        @block.sync
        def _(sp):
            sp.dma_start(nd[:, :, :, :], M.nd_dram.rearrange("b h (c i) j -> (b h) c i j", i=CB)).then_inc(nd_in, 16)

            def load_toeplitz(j, u):
                sp.wait_ge(fir_done[u], j)
                src = bass.AP(tensor=M.fir_dram.tensor, offset=(2 * j + u) * FIR_PAD * NFIR * FC,
                              ap=[[FC, 128], [FIR_PAD * FC, NFIR], [1, HALF * FC]])
                sp.dma_start(toep[:, u, :, :, :].rearrange("p f t c -> p f (t c)"), src).then_inc(toep_in[u], 16)

            pair_loop(sp, NFC, load_toeplitz)
            for g in range(2):
                sp.wait_ge(inv_row[g], CB - 1)
            sp.dma_start(M.inv_dram.rearrange("b h (c i) j -> (b h) c i j", i=CB), inv[:, :, :, :]).then_inc(inv_stored, 16)
            sp.wait_ge(inv_stored, 16)

        @block.tensor
        def _(pe):
            def windows(j, u):
                pe.wait_ge(window_kept[u], j)
                src = M.value[:, :, bass.ds((2 * j + u) * FC, FC)]
                pe.matmul(psum[:, u, WINDOW, 0:B * FC], M.reverse_first[:, :], src, start=True, stop=True)
                pe.matmul(psum[:, u, WINDOW, B * FC:2 * B * FC], M.reverse[:, :], src, start=True, stop=True
                          ).then_inc(window_done[u], 1)

            def filters(j, u):
                pe.wait_ge(toep_in[u], 16 * (j + 1))
                pe.wait_ge(window_kept[u], j + 1)
                pe.wait_ge(fir_kept[u], 6 * j)
                for c in range(FC):
                    tokens = window[:, u, c, :, :].rearrange("p h b -> p (h b)")
                    out = slice(c * 2 * B, (c + 1) * 2 * B)
                    pe.matmul(psum[:, u, LONG, out], toep[:, u, 1:3, :, c].rearrange("p f t -> p (f t)"), tokens,
                              start=True, stop=True)
                    mm = pe.matmul(psum[0:HALF, u, SHORT, out], toep[:, u, 0, :, c], tokens, start=True, stop=True)
                mm.then_inc(fir_done[u], 1)

            staged_pair_loop(pe, NFC, (windows, 0), (filters, 1))

        @block.scalar
        def _(act):
            def keep_windows(j, u):
                act.wait_ge(window_done[u], j + 1)
                act.wait_ge(fir_done[u], j)
                act.activation(window[:, u, :, :, :].rearrange("p c h b -> p h b c"),
                               psum[:, u, WINDOW, :].rearrange("p (h b c) -> p h b c", h=2, b=B),
                               ACT.Copy).then_inc(window_kept[u], 1)

            def keep(j, u):
                act.wait_ge(fir_done[u], j + 1)
                for f, bank, r in ((0, SHORT, 0), (1, LONG, 0), (2, LONG, HALF)):
                    for h in range(2):
                        out = M.filtered[h * HALF:(h + 1) * HALF, :, f, bass.ds((2 * j + u) * FC, FC)]
                        src = psum[r:r + HALF, u, bank, :].rearrange("p (c h b) -> p h b c", h=2, b=B)
                        act.activation(out, src[:, h, :, :], ACT.Copy).then_inc(fir_kept[u], 1)

            staged_pair_loop(act, NFC, (keep_windows, 0), (keep, 2))

        @block.vector
        def _(dve):
            dve.memset(inv[:, :, :, :], 0.0).then_inc(inv_set, 1)
            dve.wait_ge(inv_set, 1)
            for c in range(NC):
                ins = dve.memset(inv[:, c, :, :].rearrange("p k i -> p (k i)")[:, 0:CB * CB:CB + 1], 1.0)
            ins.then_inc(inv_set, 1)
            dve.wait_ge(inv_set, 2)
            dve.wait_ge(nd_in, 16)
            for i in range(1, CB):
                for g in range(2):
                    blocks = slice(2 * g, 2 * g + 2)
                    if i > 1:
                        dve.wait_ge(inv_row[g], i - 1)
                    p = prod[:, g, :, 0:i * i].rearrange("p c (k j) -> p c k j", j=i)
                    dve.tensor_tensor(p, inv[:, blocks, 0:i, 0:i], wide(nd[:, blocks, i, 0:i], [128, 2, i, i], 2),
                                      ALU.mult).then_inc(inv_mul[g], 1)
                for g in range(2):
                    blocks = slice(2 * g, 2 * g + 2)
                    dve.wait_ge(inv_mul[g], i)
                    p = prod[:, g, :, 0:i * i].rearrange("p c (k j) -> p c k j", j=i)
                    dve.tensor_reduce(inv[:, blocks, 0:i, i], p, AX.X, ALU.add).then_inc(inv_row[g], 1)


def mix_paths(nc, M):
    P, S, W = 4, 3, DV * H
    with signals(nc) as signal, ExitStack() as ctx:
        def sb(name, shape):
            return ctx.enter_context(nc.sbuf_tensor(name, shape, fp32))

        def pair(name):
            return [signal(f"{name}{u}") for u in range(2)]

        qT = sb("qT_tile", [128, 2, KD, L])
        kT = sb("kT_tile", [128, 2, KD, L])
        xT = sb("xT_tile", [128, 2, KD, L])
        x = sb("x_tile", [128, 2, D])
        invp = sb("inv_packed", [128, 2, H, CB])
        inv = sb("inv_tile", [128, 2, H, L])
        n32 = sb("gram_off32", [128, 2, H, L])
        n64 = sb("gram_off64", [128, 2, H, L])
        att = sb("causal_scores", [128, 2, H, L])
        rhs = sb("beta_r_v", [128, 2, W])
        x1s = sb("solve_x1", [128, 2, W])
        ys = sb("solve_y", [128, 2, W])
        x2s = sb("solve_x2", [128, 2, W])
        w1s = sb("solve_w1", [128, 2, W])
        delta = sb("delta_path", [128, 2, W])
        sq = sb("path_squares", [128, 2, NP, D])
        stat = sb("path_stats", [128, 2, NP * H, 4])
        statT = sb("path_statsT", [80, 2, L])
        hid = sb("gate_hiddenT", [128, 2, GH // 128, L])
        lg = sb("gate_logits", [128, 2, H, NP])
        ex = sb("gate_exps", [128, 2, H, NP])
        hsum = sb("gate_sums", [128, 2, 4, H])
        mixed = sb("mixed", [128, 2, D])
        mixT = sb("mixedT", [128, 2, KD, L])
        y = sb("residual", [128, 2, D])
        bn = sb("ln_stats", [128, 2, 6])
        mv = sb("ln_mean_var", [128, 2, 2])
        carrier = sb("carrier", [128, 1])
        psum = ctx.enter_context(nc.psum_tensor("mix_psum", [128, 2, 4, 512], fp32))
        EVEN, ODD, SOLVE, GATE = range(4)

        loaded = pair("tile_loaded")
        scores_done = pair("scores_done")
        masked = pair("masked")
        expanded = pair("expanded")
        solve_mm = pair("solve_mm")
        solve_ev = pair("solve_ev")
        delta_done = pair("delta_done")
        squared = pair("squared")
        stats_done = pair("stats_done")
        norms_done = pair("norms_done")
        gate_mm = pair("gate_mm")
        gate_ev = pair("gate_ev")
        small = pair("small_step")
        shifted = pair("logits_shifted")
        exps_done = pair("exps_done")
        probs_done = pair("probs_done")
        weighted = pair("weighted")
        mix_summed = pair("mix_summed")
        mix_squared = pair("mix_squared")
        power_asked = pair("power_asked")
        power_done = pair("power_done")
        ln_step = pair("ln_step")
        x1_done = pair("x1_done")
        block = ctx.enter_context(nc.Block())

        def tiles(eng, *groups):
            with eng.Fori(0, B // 2) as j:
                for group in groups:
                    for step in group:
                        for u in range(2):
                            step(j, u)

        @block.sync
        def _(sp):
            def load(j, u):
                n = 2 * j + u
                cols = bass.ds(n * L, L)
                sp.wait_ge(gate_mm[u], 5 * j)
                sp.wait_ge(scores_done[u], j)
                sp.wait_ge(x1_done[u], j)
                sp.dma_start(kT[:, u, :, :], M.kT_dram[:, cols].rearrange("(k p) n -> p k n", p=128)).then_inc(loaded[u], 16)
                sp.dma_start(qT[:, u, :, :], M.qT_dram[:, cols].rearrange("(k p) n -> p k n", p=128)).then_inc(loaded[u], 16)
                sp.dma_start(invp[:, u, :, :], M.inv_dram[bass.ds(n, 1)].rearrange("b h t c -> t (b h) c")).then_inc(loaded[u], 16)
                sp.dma_start(xT[:, u, :, :], M.xT_dram[:, cols].rearrange("(k p) n -> p k n", p=128)).then_inc(loaded[u], 16)
                sp.dma_start(x[:, u, :], M.x_dram[cols, :]).then_inc(loaded[u], 16)

            tiles(sp, [load])

        @block.tensor
        def _(pe):
            def scores(j, u):
                pe.wait_ge(loaded[u], 80 * (j + 1))
                pe.wait_ge(masked[u], j)
                for h in range(H):
                    rows = slice((h % 2) * DV, (h % 2) * DV + DV)
                    at = (h // 2) * L
                    k, q = kT[rows, u, h // 2, :], qT[rows, u, h // 2, :]
                    pe.matmul(psum[:, u, EVEN + h % 2, at:at + L], k, k, start=True, stop=True)
                    mm = pe.matmul(psum[:, u, EVEN + h % 2, 2 * L + at:2 * L + at + L], k, q, start=True, stop=True)
                mm.then_inc(scores_done[u], 1)

            def product(i, left, right):
                def step(j, u):
                    if i == 0:
                        pe.wait_ge(expanded[u], j + 1)
                        pe.wait_ge(delta_done[u], j)
                    else:
                        pe.wait_ge(solve_ev[u], 7 * j + i)
                    if i == 1:
                        pe.wait_ge(masked[u], j + 1)
                    for h in range(H):
                        mm = pe.matmul(psum[:, u, SOLVE, h * DV:h * DV + DV], left[:, u, h, :],
                                       right[:, u, h * DV:h * DV + DV], start=True, stop=True)
                    mm.then_inc(solve_mm[u], 1)
                return step

            def statsT(j, u):
                pe.wait_ge(norms_done[u], j + 1)
                pe.wait_ge(gate_ev[u], 5 * j)
                pe.transpose(psum[0:80, u, GATE, 0:L], stat[:, u, :, :].rearrange("p a s -> p (a s)"),
                             M.ident[:, :]).then_inc(gate_mm[u], 1)

            def hidden(j, u):
                pe.wait_ge(gate_ev[u], 5 * j + 1)
                for m in range(GH // 128):
                    cols = slice(m * 128, m * 128 + 128)
                    pe.matmul(psum[:, u, GATE, cols], M.gw1x[:, 0, cols], xT[:, u, 0, :], start=True, stop=False)
                    pe.matmul(psum[:, u, GATE, cols], M.gw1x[:, 1, cols], xT[:, u, 1, :], start=False, stop=False)
                    mm = pe.matmul(psum[:, u, GATE, cols], M.gw1s[:, cols], statT[:, u, :], start=False, stop=True)
                mm.then_inc(gate_mm[u], 1)

            def logits(j, u):
                pe.wait_ge(gate_ev[u], 5 * j + 2)
                for m in range(GH // 128):
                    mm = pe.matmul(psum[:, u, GATE, 0:H * NP], hid[:, u, m, :], M.gw2[:, m, :],
                                   start=(m == 0), stop=(m == GH // 128 - 1))
                mm.then_inc(gate_mm[u], 1)

            def mixedT(j, u):
                pe.wait_ge(gate_ev[u], 5 * j + 3)
                pe.wait_ge(ln_step[u], 3 * j + 1)
                for k in range(KD):
                    mm = pe.transpose(psum[:, u, GATE, k * 128:k * 128 + 128], mixed[:, u, k * 128:k * 128 + 128],
                                      M.ident[:, :])
                mm.then_inc(gate_mm[u], 1)

            def output(j, u):
                pe.wait_ge(gate_ev[u], 5 * j + 4)
                for k in range(KD):
                    mm = pe.matmul(psum[:, u, GATE, 0:D], mixT[:, u, k, :], M.wo[:, k, :], start=(k == 0), stop=(k == KD - 1))
                mm.then_inc(gate_mm[u], 1)

            solve = [product(0, inv, rhs), product(1, n32, x1s), product(2, inv, ys), product(3, n64, x2s),
                     product(4, inv, ys), product(5, n32, w1s), product(6, inv, ys), product(7, att, x2s)]
            tiles(pe, [scores], solve, [statsT, hidden, logits, mixedT, output])

        @block.scalar
        def _(act):
            def square_paths(j, u):
                act.wait_ge(stats_done[u], j)
                n = 2 * j + u
                act.activation(sq[:, u, 0:3, :], M.filtered[:, bass.ds(n, 1), :, :].rearrange("p b f c -> p (b f) c"), ACT.Square)
                act.activation(sq[:, u, 4, :], M.value[:, bass.ds(n, 1), :].rearrange("p b c -> p (b c)"), ACT.Square)

            def copy_product(i, out):
                def step(j, u):
                    act.wait_ge(solve_mm[u], 8 * j + i + 1)
                    act.activation(out[:, u, :], psum[:, u, SOLVE, 0:W], ACT.Copy).then_inc(solve_ev[u], 1)
                return step

            def square_delta(j, u):
                act.wait_ge(delta_done[u], j + 1)
                act.activation(sq[:, u, 3, :], delta[:, u, :], ACT.Square).then_inc(squared[u], 1)

            def copy_stats(j, u):
                act.wait_ge(gate_mm[u], 5 * j + 1)
                act.activation(statT[:, u, :], psum[0:80, u, GATE, 0:L], ACT.Copy).then_inc(gate_ev[u], 1)

            def gelu(j, u):
                act.wait_ge(gate_mm[u], 5 * j + 2)
                for m in range(GH // 128):
                    a = act.activation(hid[:, u, m, :], psum[:, u, GATE, m * L:m * L + L], ACT.Gelu, bias=M.gb1[:, m:m + 1])
                a.then_inc(gate_ev[u], 1)

            def copy_mixed(j, u):
                act.wait_ge(gate_mm[u], 5 * j + 4)
                act.activation(mixT[:, u, :, :], psum[:, u, GATE, 0:D].rearrange("p (k t) -> p k t", t=L),
                               ACT.Copy).then_inc(gate_ev[u], 1)

            tiles(act, [copy_product(0, x1s), square_paths, copy_product(4, w1s), square_delta],
                  [copy_stats, gelu, copy_mixed])

        @block.vector
        def _(dve):
            def banks(u, at):
                return psum[:, u, EVEN:ODD + 1, at:at + 2 * L].rearrange("p b (a t) -> p b a t", t=L)

            def by_bank(t, u):
                return t[:, u, :, :].rearrange("p (a b) t -> p b a t", b=2)

            def mask(m):
                return wide(wide(m[:, :], [128, 2, L], 1), [128, 2, 2, L], 1)

            def mask_scores(j, u):
                dve.wait_ge(scores_done[u], j + 1)
                dve.wait_ge(solve_mm[u], 8 * j)
                dve.tensor_tensor(by_bank(n32, u), banks(u, 0), mask(M.off32), ALU.mult)
                dve.tensor_tensor(by_bank(n64, u), banks(u, 0), mask(M.off64), ALU.mult)
                dve.tensor_tensor(by_bank(att, u), banks(u, 2 * L), mask(M.causal), ALU.mult).then_inc(masked[u], 1)

            def heads(ap):
                return ap.rearrange("p (h d) -> p h d", d=DV)

            def scale_product(i):
                def step(j, u):
                    n = 2 * j + u
                    dve.wait_ge(solve_mm[u], 8 * j + i + 1)
                    dve.tensor_tensor(heads(ys[:, u, :]), heads(psum[:, u, SOLVE, 0:W]),
                                      wide(M.decay[:, bass.ds(n, 1), :].rearrange("p b h -> p (b h)"), [128, H, DV], 2),
                                      ALU.mult).then_inc(solve_ev[u], 1)
                return step

            def join_pairs(j, u):
                dve.wait_ge(solve_mm[u], 8 * j + 3)
                dve.tensor_tensor(x2s[:, u, :], x1s[:, u, :], psum[:, u, SOLVE, 0:W], ALU.subtract).then_inc(solve_ev[u], 1)

            def less_w1(j, u):
                dve.wait_ge(solve_ev[u], 7 * j + 5)
                dve.tensor_tensor(x2s[:, u, :], x2s[:, u, :], w1s[:, u, :], ALU.subtract).then_inc(small[u], 1)

            def join_halves(j, u):
                dve.wait_ge(solve_mm[u], 8 * j + 7)
                dve.wait_ge(small[u], SM * j + 1)
                dve.tensor_tensor(x2s[:, u, :], x2s[:, u, :], psum[:, u, SOLVE, 0:W], ALU.add).then_inc(solve_ev[u], 1)

            def scale_delta(j, u):
                n = 2 * j + u
                dve.wait_ge(solve_mm[u], 8 * j + 8)
                dve.wait_ge(weighted[u], j)
                dve.tensor_tensor(heads(delta[:, u, :]), heads(psum[:, u, SOLVE, 0:W]),
                                  wide(M.rq[:, bass.ds(n, 1), :].rearrange("p b h -> p (b h)"), [128, H, DV], 2),
                                  ALU.mult).then_inc(delta_done[u], 1)

            def path_sums(j, u):
                n = 2 * j + u
                fir = M.filtered[:, bass.ds(n, 1), :, :].rearrange("p b f (h d) -> p (b f h) d", d=DV)
                val = M.value[:, bass.ds(n, 1), :].rearrange("p b (h d) -> p (b h) d", d=DV)
                dve.wait_ge(gate_mm[u], 5 * j)
                for s, mag in ((0, False), (2, True)):
                    dve.tensor_reduce(stat[:, u, 0:12, s], fir, AX.X, ALU.add, apply_absolute_value=mag)
                    dve.tensor_reduce(stat[:, u, 16:20, s], val, AX.X, ALU.add, apply_absolute_value=mag)

            def delta_sums(j, u):
                dve.wait_ge(delta_done[u], j + 1)
                for s, mag in ((0, False), (2, True)):
                    dve.tensor_reduce(stat[:, u, 12:16, s], heads(delta[:, u, :]), AX.X, ALU.add, apply_absolute_value=mag)
                dve.wait_ge(squared[u], j + 1)
                dve.tensor_reduce(stat[:, u, :, 1], sq[:, u, :, :].rearrange("p f (h d) -> p (f h) d", d=DV),
                                  AX.X, ALU.add).then_inc(stats_done[u], 1)

            SM = 8

            def shift_logits(j, u):
                dve.wait_ge(gate_mm[u], 5 * j + 3)
                flat = lg[:, u, :, :].rearrange("p h f -> p (h f)")
                dve.tensor_tensor(flat, psum[:, u, GATE, 0:H * NP], M.gb2[:, :], ALU.add).then_inc(gate_ev[u], 1)
                dve.wait_ge(gate_ev[u], 5 * j + 3)
                dve.tensor_tensor(lg[:, u, :, :], lg[:, u, :, :], wide(M.inv_tau[:, :], [128, H, NP], 2),
                                  ALU.mult).then_inc(small[u], 1)
                dve.wait_ge(small[u], SM * j + 2)
                dve.tensor_reduce(hsum[:, u, 0, :], lg[:, u, :, :], AX.X, ALU.max).then_inc(small[u], 1)
                dve.wait_ge(small[u], SM * j + 3)
                dve.tensor_tensor(lg[:, u, :, :], lg[:, u, :, :], wide(hsum[:, u, 0, :], [128, H, NP], 2),
                                  ALU.subtract).then_inc(shifted[u], 1)

            def probabilities(j, u):
                dve.wait_ge(exps_done[u], j + 1)
                dve.tensor_reduce(hsum[:, u, 1, :], ex[:, u, :, :], AX.X, ALU.add).then_inc(small[u], 1)
                dve.wait_ge(small[u], SM * j + 4)
                dve.reciprocal(hsum[:, u, 2, :], hsum[:, u, 1, :]).then_inc(small[u], 1)
                dve.wait_ge(small[u], SM * j + 5)
                dve.tensor_tensor(hsum[:, u, 3, :], hsum[:, u, 2, :], M.keep[:, :], ALU.mult).then_inc(small[u], 1)
                dve.wait_ge(small[u], SM * j + 6)
                dve.tensor_tensor(ex[:, u, :, :], ex[:, u, :, :], wide(hsum[:, u, 3, :], [128, H, NP], 2),
                                  ALU.mult).then_inc(small[u], 1)
                dve.wait_ge(small[u], SM * j + 7)
                dve.tensor_tensor(ex[:, u, :, :], ex[:, u, :, :], M.floor[:, :, :], ALU.add).then_inc(probs_done[u], 1)

            def sum_paths(j, u):
                dve.wait_ge(weighted[u], j + 1)
                dve.tensor_reduce(mixed[:, u, :], sq[:, u, :, :].rearrange("p f c -> p c f"), AX.X,
                                  ALU.add).then_inc(mix_summed[u], 1)

            def mix_norm(j, u):
                dve.wait_ge(mix_squared[u], j + 1)
                dve.tensor_reduce(hsum[:, u, 0, :], heads(y[:, u, :]), AX.X, ALU.add).then_inc(small[u], 1)
                dve.wait_ge(small[u], SM * j + 8)
                dve.tensor_scalar(hsum[:, u, 1, :], hsum[:, u, 0, :], 1.0 / DV, 1e-5, ALU.mult,
                                  ALU.add).then_inc(power_asked[u], 1)

            def scale_mix(j, u):
                dve.wait_ge(power_done[u], 2 * j + 1)
                dve.tensor_tensor(heads(mixed[:, u, :]), heads(mixed[:, u, :]), wide(hsum[:, u, 2, :], [128, H, DV], 2),
                                  ALU.mult).then_inc(ln_step[u], 1)

            def residual(j, u):
                dve.wait_ge(gate_mm[u], 5 * j + 5)
                dve.tensor_tensor(y[:, u, :], psum[:, u, GATE, 0:D], x[:, u, :], ALU.add).then_inc(gate_ev[u], 1)
                dve.wait_ge(gate_ev[u], 5 * j + 5)
                dve.bn_stats(bn[:, u, :], y[:, u, :]).then_inc(ln_step[u], 1)
                dve.wait_ge(ln_step[u], 3 * j + 2)
                dve.memset(carrier[:, :], 0.0)
                dve.bn_aggr(mv[:, u, :], bn[:, u, :]).then_inc(ln_step[u], 1)
                dve.wait_ge(ln_step[u], 3 * j + 3)
                dve.tensor_scalar(mv[:, u, 1:2], mv[:, u, 1:2], 1e-5, None, ALU.add).then_inc(power_asked[u], 1)

            def normalize(j, u):
                n = 2 * j + u
                dve.wait_ge(power_done[u], 2 * j + 2)
                dve.tensor_scalar(M.value[:, bass.ds(n, 1), :].rearrange("p b c -> p (b c)"), y[:, u, :],
                                  mv[:, u, 0:1], bn[:, u, 0:1], ALU.subtract, ALU.mult).then_inc(x1_done[u], 1)

            tiles(dve, [mask_scores, scale_product(1), join_pairs, scale_product(3), scale_product(5), less_w1,
                        join_halves, path_sums, scale_delta, delta_sums],
                  [shift_logits, probabilities, sum_paths, mix_norm, scale_mix, residual, normalize])

        @block.gpsimd
        def _(pool):
            def expand(j, u):
                n = 2 * j + u
                pool.wait_ge(loaded[u], 80 * (j + 1))
                pool.wait_ge(solve_mm[u], 8 * j)
                pool.tensor_tensor(inv[:, u, :, :].rearrange("p h (c i) -> p h c i", i=CB),
                                   wide(invp[:, u, :, :], [128, H, NC, CB], 2),
                                   wide(M.blockdiag[:, :].rearrange("p (c i) -> p c i", i=CB), [128, H, NC, CB], 1),
                                   ALU.mult)
                pool.tensor_tensor(rhs[:, u, :].rearrange("p (h d) -> p h d", d=DV),
                                   M.value[:, bass.ds(n, 1), :].rearrange("p b (h d) -> p (b h) d", d=DV),
                                   wide(M.beta_r[:, bass.ds(n, 1), :].rearrange("p b h -> p (b h)"), [128, H, DV], 2),
                                   ALU.mult).then_inc(expanded[u], 1)

            def norms(j, u):
                pool.wait_ge(stats_done[u], j + 1)
                pool.tensor_tensor(stat[:, u, :, 3], stat[:, u, :, 1],
                                   M.plus_half[:, 0:1].broadcast_to([128, NP * H]), ALU.pow).then_inc(norms_done[u], 1)

            def exps(j, u):
                pool.wait_ge(shifted[u], j + 1)
                pool.tensor_tensor(ex[:, u, :, :].rearrange("p h f -> p (h f)"),
                                   M.euler[:, 0:1].broadcast_to([128, H * NP]),
                                   lg[:, u, :, :].rearrange("p h f -> p (h f)"), ALU.pow).then_inc(exps_done[u], 1)

            def weight(j, u):
                n = 2 * j + u
                pool.wait_ge(probs_done[u], j + 1)

                def prob(f0, nf):
                    return wide(ex[:, u, :, f0:f0 + nf].rearrange("p h f -> p f h"), [128, nf, H, DV], 3)

                def split(ap):
                    return ap.rearrange("p f (h d) -> p f h d", d=DV)

                pool.tensor_tensor(split(sq[:, u, 3:4, :]), split(delta[:, u:u + 1, :]), prob(3, 1), ALU.mult)
                pool.tensor_tensor(split(sq[:, u, 0:3, :]),
                                   M.filtered[:, bass.ds(n, 1), :, :].rearrange("p b f (h d) -> p (b f) h d", d=DV),
                                   prob(0, 3), ALU.mult)
                pool.tensor_tensor(split(sq[:, u, 4:5, :]), split(M.value[:, bass.ds(n, 1), :]), prob(4, 1),
                                   ALU.mult).then_inc(weighted[u], 1)

            def square_mix(j, u):
                pool.wait_ge(mix_summed[u], j + 1)
                pool.tensor_tensor(y[:, u, :], mixed[:, u, :], mixed[:, u, :], ALU.mult).then_inc(mix_squared[u], 1)

            def mix_power(j, u):
                pool.wait_ge(power_asked[u], 2 * j + 1)
                pool.tensor_tensor(hsum[:, u, 2, :], hsum[:, u, 1, :], M.minus_half[:, 0:1].broadcast_to([128, H]),
                                   ALU.pow).then_inc(power_done[u], 1)

            def ln_power(j, u):
                pool.wait_ge(power_asked[u], 2 * j + 2)
                pool.tensor_tensor(bn[:, u, 0:1], mv[:, u, 1:2], M.minus_half[:, 0:1], ALU.pow).then_inc(power_done[u], 1)

            tiles(pool, [expand, norms, exps, weight, square_mix, mix_power, ln_power])


def load_experts(nc, M):
    with signals(nc) as signal, ExitStack() as ctx:
        weights_in = signal("expert_weights_in")
        block = ctx.enter_context(nc.Block())

        @block.sync
        def _(sp):
            full = EH // 128 * 128
            for w, routed, shared in ((M.wg, M.wg_dram, M.wg_s_dram), (M.wu, M.wu_dram, M.wu_s_dram)):
                for e in range(NE + 1):
                    src = routed[e] if e < NE else shared
                    sp.dma_start(w[:, e, :, :], src.rearrange("(k p) n -> p k n", p=128)).then_inc(weights_in, 16)
            for e in range(NE + 1):
                src = M.wd_dram[e] if e < NE else M.wd_s_dram
                sp.dma_start(M.wd[:, e, 0:full // 128, :], src[0:full, :].rearrange("(k p) n -> p k n", p=128)
                             ).then_inc(weights_in, 16)
                sp.dma_start(M.wd[0:EH - full, e, full // 128, :], src[full:EH, :]).then_inc(weights_in, 16)
            sp.wait_ge(weights_in, 16 * 4 * (NE + 1))


def attend(nc, M):
    SCALE = 1.0 / math.sqrt(XD)
    NK = CTX // 128
    with signals(nc) as signal, ExitStack() as ctx:
        def sb(name, shape):
            return ctx.enter_context(nc.sbuf_tensor(name, shape, fp32))

        def pair(name):
            return [signal(f"{name}{u}") for u in range(2)]

        w_src = sb("w_src", [128, NK, 2 * D])
        w_tgt = sb("w_tgt", [128, KD, D])
        w_out = sb("w_out", [128, 2 * KD, D])
        w_router = sb("w_router", [128, KD, NE])
        b_key = sb("b_key", [128, KD])
        b_tgt = sb("b_tgt", [128, KD])
        b_val = sb("b_val", [128, D])
        b_out = sb("b_out", [128, D])
        cT = sb("ctxT_tile", [128, 2, NK, L])
        mrow = sb("mask_row", [128, 2, L])
        mcol = sb("mask_col", [128, 2, 1])
        shut = sb("mask_shut", [128, 2, L])
        x1 = sb("x1_tile", [128, 2, D])
        x1b = sb("x1_plus_bias", [128, 2, D])
        x1T = sb("x1T_tile", [128, 2, KD, L])
        keyT = sb("keyT", [128, 2, KD, L])
        qryT = sb("queryT", [128, 2, KD, L])
        vraw = sb("value_raw", [128, 2, D])
        val = sb("value_ones", [128, 2, XH, XD + 1])
        sc = sb("scores", [128, 2, XH, L])
        scT = sb("scoresT", [128, 2, XH, L])
        mx = sb("score_max", [128, 2, XH])
        den = sb("softmax_den", [128, 2, XH])
        upd = sb("update", [128, 2, D])
        updT = sb("updateT", [128, 2, KD, L])
        y = sb("residual2", [128, 2, D])
        x2 = sb("x2_tile", [128, 2, D])
        x2T = sb("x2T_tile", [128, 2, KD, L])
        bn = sb("ln_stats2", [128, 2, 6])
        mv = sb("ln_mean_var2", [128, 2, 2])
        carrier = sb("carrier2", [128, 1])
        spsum = ctx.enter_context(nc.psum_tensor("score_psum", [128, 4, 512], fp32))
        psum = ctx.enter_context(nc.psum_tensor("attend_psum", [128, 2, 2, 512], fp32))
        K, V = 0, 1

        weights_in = signal("attend_weights_in")
        ones_set = signal("ones_set")
        loaded = pair("ctx_loaded")
        x1_copied = pair("x1_copied")
        x1_biased = pair("x1_biased")
        k_mm = pair("k_bank_mm")
        k_ev = pair("k_bank_ev")
        v_mm = pair("v_bank_mm")
        v_ev = pair("v_bank_ev")
        mask_made = pair("mask_made")
        val_done = pair("val_done")
        scores_mm = pair("scores_mm")
        scores_ev = pair("scores_ev")
        max_done = pair("max_done")
        shifted = pair("scores_shifted")
        exp_done = pair("exp_done")
        den_done = pair("den_done")
        ln_step = pair("ln2_step")
        power_asked = pair("ln2_power_asked")
        power_done = pair("ln2_power_done")
        x2_done = pair("x2_done")
        x2_kept = pair("x2_kept")
        x2_stored = pair("x2_stored")
        logits_kept = pair("logits_kept")
        block = ctx.enter_context(nc.Block())
        NKM, NVM, KM = 6, 4, 6

        def tiles(eng, *steps):
            with eng.Fori(0, B // 2) as j:
                for step in steps:
                    for u in range(2):
                        step(j, u)

        @block.sync
        def _(sp):
            def part(w, k):
                return w.rearrange("(k p) n -> p k n", k=k)
            for dst, src in ((w_src, part(M.w_srcT_dram, NK)), (w_tgt, part(M.w_tgtT_dram, KD)),
                             (w_out, part(M.w_outT_dram, 2 * KD)), (w_router, part(M.w_routerT_dram, KD))):
                sp.dma_start(dst[:, :, :], src).then_inc(weights_in, 16)
            sp.dma_start(b_key[:, :], M.b_key_dram).then_inc(weights_in, 16)
            sp.dma_start(b_tgt[:, :], M.b_tgt_dram).then_inc(weights_in, 16)
            sp.dma_start(b_val[:, :], M.b_src_dram[D:2 * D].partition_broadcast(128)).then_inc(weights_in, 16)
            sp.dma_start(b_out[:, :], M.b_out_dram.partition_broadcast(128)).then_inc(weights_in, 16)

            def load(j, u):
                n = 2 * j + u
                sp.wait_ge(v_mm[u], NVM * j)
                sp.wait_ge(scores_ev[u], j)
                sp.wait_ge(val_done[u], j)
                sp.dma_start(mcol[:, u, :], M.mask_col_dram[bass.ds(n * L, L), :]).then_inc(loaded[u], 16)
                sp.dma_start(mrow[:, u, :], M.mask_dram[bass.ds(n, 1), :].rearrange("b t -> (b t)").partition_broadcast(128)
                             ).then_inc(loaded[u], 16)
                sp.dma_start(cT[:, u, :, :], M.ctxT_dram[:, bass.ds(n * L, L)].rearrange("(k p) n -> p k n", p=128)
                             ).then_inc(loaded[u], 16)

            def store(j, u):
                n = 2 * j + u
                sp.wait_ge(x2_done[u], j + 1)
                sp.dma_start(M.rows_dram[bass.ds(n * L, L), :], x2[:, u, :]).then_inc(x2_stored[u], 16)

            tiles(sp, load, store)
            for u in range(2):
                sp.wait_ge(x2_stored[u], 16 * (B // 2))

        @block.tensor
        def _(pe):
            pe.wait_ge(weights_in, 8 * 16)

            def keys(j, u):
                pe.wait_ge(loaded[u], 48 * (j + 1))
                pe.wait_ge(x1_copied[u], j + 1)
                pe.wait_ge(k_ev[u], NKM * j)
                for m in range(KD):
                    for k in range(NK):
                        pe.matmul(psum[:, u, K, m * L:m * L + L], w_src[:, k, m * 128:m * 128 + 128], cT[:, u, k, :],
                                  start=(k == 0), stop=(k == NK - 1))
                for k in range(KD):
                    mm = pe.transpose(psum[:, u, K, (KD + k) * L:(KD + k) * L + L], x1[:, u, k * 128:k * 128 + 128],
                                      M.ident[:, :])
                mm.then_inc(k_mm[u], 1)

            def values(j, u):
                pe.wait_ge(v_ev[u], NVM * j)
                for k in range(NK):
                    mm = pe.matmul(psum[:, u, V, 0:D], cT[:, u, k, :], w_src[:, k, D:2 * D], start=(k == 0), stop=(k == NK - 1))
                mm.then_inc(v_mm[u], 1)

            def queries(j, u):
                pe.wait_ge(k_ev[u], NKM * j + 1)
                for m in range(KD):
                    for k in range(KD):
                        mm = pe.matmul(psum[:, u, K, m * L:m * L + L], w_tgt[:, k, m * 128:m * 128 + 128], x1T[:, u, k, :],
                                       start=(k == 0), stop=(k == KD - 1))
                mm.then_inc(k_mm[u], 1)

            def scores(j, u):
                pe.wait_ge(k_ev[u], NKM * j + 2)
                pe.wait_ge(scores_ev[1 - u], j + u)
                for h in range(XH):
                    rows = slice((h % 4) * XD, (h % 4) * XD + XD)
                    mm = pe.matmul(spsum[:, h % 4, (h // 4) * 2 * L:(h // 4) * 2 * L + L], qryT[rows, u, h // 4, :],
                                   keyT[rows, u, h // 4, :], start=True, stop=True)
                mm.then_inc(scores_mm[u], 1)

            def turn_probs(j, u):
                pe.wait_ge(exp_done[u], j + 1)
                pe.wait_ge(v_ev[u], NVM * j + 1)
                for i in range(XH):
                    bank = K if i < 4 else V
                    mm = pe.transpose(psum[:, u, bank, (i % 4) * L:(i % 4) * L + L], sc[:, u, i, :], M.ident[:, :])
                    if i == 3:
                        mm.then_inc(k_mm[u], 1)
                mm.then_inc(v_mm[u], 1)

            def average(j, u):
                pe.wait_ge(k_ev[u], NKM * j + 3)
                pe.wait_ge(v_ev[u], NVM * j + 2)
                pe.wait_ge(val_done[u], j + 1)
                for h in range(XH):
                    i = 2 * (h % 4) + h // 4
                    mm = pe.matmul(psum[:, u, K, h * (XD + 1):(h + 1) * (XD + 1)], scT[:, u, i, :], val[:, u, h, :],
                                   start=True, stop=True)
                mm.then_inc(k_mm[u], 1)

            def turn_update(j, u):
                pe.wait_ge(k_ev[u], NKM * j + 4)
                for k in range(KD):
                    mm = pe.transpose(psum[:, u, V, k * L:k * L + L], upd[:, u, k * 128:k * 128 + 128], M.ident[:, :])
                mm.then_inc(v_mm[u], 1)

            def output(j, u):
                for k in range(KD):
                    pe.matmul(psum[:, u, K, 0:D], x1T[:, u, k, :], w_out[:, k, :], start=(k == 0), stop=False)
                pe.wait_ge(v_ev[u], NVM * j + 3)
                for k in range(KD):
                    mm = pe.matmul(psum[:, u, K, 0:D], updT[:, u, k, :], w_out[:, KD + k, :], start=False, stop=(k == KD - 1))
                mm.then_inc(k_mm[u], 1)

            def turn_x2(j, u):
                pe.wait_ge(x2_done[u], j + 1)
                for k in range(KD):
                    mm = pe.transpose(psum[:, u, V, k * L:k * L + L], x2[:, u, k * 128:k * 128 + 128], M.ident[:, :])
                mm.then_inc(v_mm[u], 1)

            def router(j, u):
                pe.wait_ge(v_ev[u], NVM * j + 4)
                for k in range(KD):
                    mm = pe.matmul(psum[:, u, K, 0:NE], x2T[:, u, k, :], w_router[:, k, :], start=(k == 0), stop=(k == KD - 1))
                mm.then_inc(k_mm[u], 1)

            tiles(pe, keys, values, queries, scores, turn_probs, average, turn_update, output, turn_x2, router)

        @block.scalar
        def _(act):
            def copy_x1(j, u):
                n = 2 * j + u
                act.wait_ge(x1_biased[u], j)
                act.wait_ge(k_mm[u], KM * j)
                act.activation(x1[:, u, :], M.value[:, bass.ds(n, 1), :].rearrange("p b c -> p (b c)"), ACT.Copy
                               ).then_inc(x1_copied[u], 1)

            def mask_values(j, u):
                act.wait_ge(v_ev[u], NVM * j + 1)
                act.wait_ge(k_mm[u], KM * j)
                act.activation(val[:, u, :, 0:XD], vraw[:, u, :].rearrange("p (h d) -> p h d", d=XD), ACT.Copy,
                               scale=mcol[:, u, :]).then_inc(val_done[u], 1)

            def exps(j, u):
                act.wait_ge(shifted[u], j + 1)
                act.activation(sc[:, u, :, :], sc[:, u, :, :], ACT.Exp).then_inc(exp_done[u], 1)

            def copy_probs(j, u):
                act.wait_ge(k_mm[u], KM * j + 3)
                act.activation(scT[:, u, 0:4, :], psum[:, u, K, :].rearrange("p (i t) -> p i t", t=L), ACT.Copy
                               ).then_inc(k_ev[u], 1)

            def copy_update(j, u):
                act.wait_ge(v_mm[u], NVM * j + 3)
                act.activation(updT[:, u, :, :], psum[:, u, V, 0:D].rearrange("p (k t) -> p k t", t=L), ACT.Copy
                               ).then_inc(v_ev[u], 1)

            def copy_x2(j, u):
                n = 2 * j + u
                act.wait_ge(v_mm[u], NVM * j + 4)
                act.activation(x2T[:, u, :, :], psum[:, u, V, 0:D].rearrange("p (k t) -> p k t", t=L), ACT.Copy
                               ).then_inc(v_ev[u], 1)
                act.activation(M.value[:, bass.ds(n, 1), :].rearrange("p b c -> p (b c)"), x2[:, u, :], ACT.Copy
                               ).then_inc(x2_kept[u], 1)

            act.wait_ge(ones_set, 1)
            tiles(act, copy_x1, mask_values, exps, copy_probs, copy_update, copy_x2)

        @block.vector
        def _(dve):
            dve.memset(val[:, :, :, XD:XD + 1], 1.0).then_inc(ones_set, 1)
            dve.wait_ge(weights_in, 8 * 16)
            def masks(j, u):
                dve.wait_ge(loaded[u], 48 * (j + 1))
                dve.tensor_scalar(shut[:, u, :], mrow[:, u, :], 0.0, -1e30, ALU.is_equal, ALU.mult).then_inc(mask_made[u], 1)

            def keep_keys(j, u):
                dve.wait_ge(k_mm[u], KM * j + 1)
                dve.wait_ge(scores_mm[u], j)
                for m in range(KD):
                    dve.scalar_tensor_tensor(out=keyT[:, u, m, :], in0=psum[:, u, K, m * L:m * L + L],
                                             scalar=b_key[:, m:m + 1], in1=mrow[:, u, :], op0=ALU.add, op1=ALU.mult)
                dve.tensor_copy(x1T[:, u, :, :], psum[:, u, K, KD * L:2 * KD * L].rearrange("p (k t) -> p k t", t=L)
                                ).then_inc(k_ev[u], 1)

            def keep_values(j, u):
                dve.wait_ge(v_mm[u], NVM * j + 1)
                dve.wait_ge(val_done[u], j)
                dve.tensor_tensor(vraw[:, u, :], psum[:, u, V, 0:D], b_val[:, :], ALU.add).then_inc(v_ev[u], 1)

            def keep_queries(j, u):
                dve.wait_ge(k_mm[u], KM * j + 2)
                for m in range(KD):
                    ins = dve.scalar_tensor_tensor(out=qryT[:, u, m, :], in0=psum[:, u, K, m * L:m * L + L],
                                                   scalar=b_tgt[:, m:m + 1], in1=mrow[:, u, :], op0=ALU.add, op1=ALU.mult)
                ins.then_inc(k_ev[u], 1)

            def scale_scores(j, u):
                dve.wait_ge(scores_mm[u], j + 1)
                dve.wait_ge(mask_made[u], j + 1)
                dve.wait_ge(v_mm[u], NVM * j)
                dve.scalar_tensor_tensor(out=sc[:, u, :, :],
                                         in0=spsum[:, :, :].rearrange("p b (a t) -> p (b a) t", t=2 * L)[:, :, 0:L],
                                         scalar=SCALE, in1=wide(shut[:, u, :], [128, XH, L], 1),
                                         op0=ALU.mult, op1=ALU.add).then_inc(scores_ev[u], 1)
                dve.wait_ge(scores_ev[u], j + 1)
                dve.tensor_reduce(mx[:, u, :], sc[:, u, :, :], AX.X, ALU.max).then_inc(max_done[u], 1)

            def copy_probs(j, u):
                dve.wait_ge(v_mm[u], NVM * j + 2)
                dve.tensor_copy(scT[:, u, 4:8, :], psum[:, u, V, :].rearrange("p (i t) -> p i t", t=L)).then_inc(v_ev[u], 1)

            def divide(j, u):
                dve.wait_ge(k_mm[u], KM * j + 4)
                av = psum[:, u, K, 0:XH * (XD + 1)].rearrange("p (h d) -> p h d", d=XD + 1)
                dve.reciprocal(den[:, u, :], av[:, :, XD]).then_inc(den_done[u], 1)
                dve.wait_ge(den_done[u], j + 1)
                dve.tensor_tensor(upd[:, u, :].rearrange("p (h d) -> p h d", d=XD), av[:, :, 0:XD],
                                  wide(den[:, u, :], [128, XH, XD], 2), ALU.mult).then_inc(k_ev[u], 1)

            def residual(j, u):
                dve.wait_ge(k_mm[u], KM * j + 5)
                dve.wait_ge(x1_biased[u], j + 1)
                dve.tensor_tensor(y[:, u, :], psum[:, u, K, 0:D], x1b[:, u, :], ALU.add).then_inc(k_ev[u], 1)
                dve.wait_ge(k_ev[u], NKM * j + 5)
                dve.bn_stats(bn[:, u, :], y[:, u, :]).then_inc(ln_step[u], 1)
                dve.wait_ge(ln_step[u], 2 * j + 1)
                dve.memset(carrier[:, :], 0.0)
                dve.bn_aggr(mv[:, u, :], bn[:, u, :]).then_inc(ln_step[u], 1)
                dve.wait_ge(ln_step[u], 2 * j + 2)
                dve.tensor_scalar(mv[:, u, 1:2], mv[:, u, 1:2], 1e-5, None, ALU.add).then_inc(power_asked[u], 1)

            def normalize(j, u):
                dve.wait_ge(power_done[u], j + 1)
                dve.wait_ge(x2_stored[u], 16 * j)
                dve.wait_ge(x2_kept[u], j)
                dve.tensor_scalar(x2[:, u, :], y[:, u, :], mv[:, u, 0:1], bn[:, u, 0:1], ALU.subtract,
                                  ALU.mult).then_inc(x2_done[u], 1)

            def keep_logits(j, u):
                n = 2 * j + u
                dve.wait_ge(k_mm[u], KM * j + 6)
                dve.tensor_copy(M.logits[:, bass.ds(n, 1), :].rearrange("p b e -> p (b e)"), psum[:, u, K, 0:NE]
                                ).then_inc(k_ev[u], 1)

            tiles(dve, masks, keep_keys, keep_values, keep_queries, scale_scores, copy_probs, divide, residual,
                  normalize, keep_logits)

        @block.gpsimd
        def _(pool):
            pool.wait_ge(weights_in, 8 * 16)

            def bias_x1(j, u):
                pool.wait_ge(x1_copied[u], j + 1)
                pool.wait_ge(power_asked[u], j)
                pool.tensor_tensor(x1b[:, u, :], x1[:, u, :], b_out[:, :], ALU.add).then_inc(x1_biased[u], 1)

            def shift(j, u):
                pool.wait_ge(max_done[u], j + 1)
                pool.tensor_tensor(sc[:, u, :, :], sc[:, u, :, :], wide(mx[:, u, :], [128, XH, L], 2),
                                   ALU.subtract).then_inc(shifted[u], 1)

            def power(j, u):
                pool.wait_ge(power_asked[u], j + 1)
                pool.tensor_tensor(bn[:, u, 0:1], mv[:, u, 1:2], M.minus_half[:, 0:1], ALU.pow).then_inc(power_done[u], 1)

            tiles(pool, bias_x1, shift, power)


def route(nc, M):
    with signals(nc) as signal, ExitStack() as ctx:
        def sb(name, shape, dt=fp32):
            return ctx.enter_context(nc.sbuf_tensor(name, shape, dt))

        ones = sb("ones", [128, 128])
        before = sb("before", [128, 128])
        rank8 = sb("rank8", [128, NE])
        slots = sb("slots", [128, SLOT_TILES])
        zero_row = sb("zero_row", [128, 8 * D])
        l2 = sb("logits_less_top", [128, B, NE])
        exps = sb("router_exps", [128, B, NE])
        diff = sb("router_diff", [128, B, NE])
        tie = sb("tie", [128, B, NE])
        hot = [sb(f"hot{i}", [128, B, NE]) for i in range(2)]
        both = sb("hot_both", [128, B, NE])
        top = sb("top", [128, 2, B])
        tmax = sb("tie_max", [128, B])
        d2 = sb("top_diff", [128, B])
        pr = sb("top_probs", [128, 2, B])
        rsum = sb("router_rsum", [128, B])
        scan = [sb(f"scan{i}", [128, B, NE]) for i in range(2)]
        base = sb("base", [128, B, NE])
        cnt = sb("counts", [128, NE])
        cnti = sb("counts_int", [128, NE], mybir.dt.int32)
        ends = [sb(f"ends{i}", [128, NE]) for i in range(2)]
        nt = sb("tiles_of", [128, NE])
        posf = sb("posf", [128, B])
        past = sb("past", [128, SLOT_TILES, NE])
        ef = sb("expert_f", [128, SLOT_TILES])
        prefix = ctx.enter_context(nc.psum_tensor("prefix_psum", [128, 512], fp32))
        totals = ctx.enter_context(nc.psum_tensor("totals_psum", [128, 512], fp32))
        made = signal("route_constants")
        zero_set = signal("zero_set")
        dve_step = signal("route_step")
        asked = signal("router_exps_asked")
        answered = signal("router_exps_done")
        both_done = signal("both_done")
        counted = signal("counted")
        placed = signal("placed")
        scattered = signal("scattered")
        cleared = signal("cleared")
        block = ctx.enter_context(nc.Block())

        @block.sync
        def _(sp):
            sp.wait_ge(zero_set, 1)
            for i in range(SLOT_TILES // 8):
                r0 = B * L + i * 8 * L
                sp.dma_start(M.rows_dram[r0:r0 + 8 * L, :].rearrange("(p a) c -> p (a c)", a=8), zero_row[:, :]
                             ).then_inc(cleared, 16)

        @block.tensor
        def _(pe):
            pe.wait_ge(made, 4)
            pe.wait_ge(both_done, 1)
            flat = both[:, :, :].rearrange("p b e -> p (b e)")
            pe.matmul(prefix[:, 0:B * NE], before[:, :], flat, start=True, stop=True)
            pe.matmul(totals[:, 0:B * NE], ones[:, :], flat, start=True, stop=True).then_inc(counted, 1)

        @block.vector
        def _(dve):
            steps = [0]

            def link(ins):
                steps[0] += 1
                ins.then_inc(dve_step, 1)
                dve.wait_ge(dve_step, steps[0])

            def eights(ap):
                return wide(ap, [128, B, NE], 2)

            dve.memset(zero_row[:, :], 0.0).then_inc(zero_set, 1)
            dve.wait_ge(made, 4)
            lg = M.logits[:, :, :]
            for i in range(2):
                src = lg if i == 0 else l2[:, :, :]
                link(dve.tensor_reduce(top[:, i, :], src, AX.X, ALU.max))
                link(dve.tensor_tensor(tie[:, :, :], src, eights(top[:, i, :]), ALU.is_equal))
                link(dve.tensor_tensor(tie[:, :, :], tie[:, :, :], wide(rank8[:, :], [128, B, NE], 1), ALU.mult))
                link(dve.tensor_reduce(tmax[:, :], tie[:, :, :], AX.X, ALU.max))
                link(dve.tensor_tensor(hot[i][:, :, :], tie[:, :, :], eights(tmax[:, :]), ALU.is_equal))
                if i == 0:
                    link(dve.scalar_tensor_tensor(out=l2[:, :, :], in0=hot[0][:, :, :], scalar=-1e30, in1=lg,
                                                  op0=ALU.mult, op1=ALU.add))
            link(dve.tensor_tensor(diff[:, :, :], lg, eights(top[:, 0, :]), ALU.subtract))
            dve.tensor_tensor(d2[:, :], top[:, 1, :], top[:, 0, :], ALU.subtract).then_inc(asked, 1)
            dve.tensor_tensor(both[:, :, :], hot[0][:, :, :], hot[1][:, :, :], ALU.add).then_inc(both_done, 1)
            dve.wait_ge(answered, 2)
            link(dve.tensor_reduce(rsum[:, :], exps[:, :, :], AX.X, ALU.add))
            link(dve.reciprocal(pr[:, 0, :], rsum[:, :]))
            link(dve.tensor_tensor(pr[:, 1, :], pr[:, 1, :], pr[:, 0, :], ALU.mult))
            link(dve.tensor_tensor(rsum[:, :], pr[:, 0, :], pr[:, 1, :], ALU.add))
            link(dve.tensor_scalar(rsum[:, :], rsum[:, :], 1e-20, None, ALU.add))
            link(dve.reciprocal(rsum[:, :], rsum[:, :]))
            for i in range(2):
                link(dve.tensor_tensor(M.weight[:, :, i], pr[:, i, :], rsum[:, :], ALU.mult))
            dve.wait_ge(counted, 1)
            tot = totals[:, 0:B * NE].rearrange("p (b e) -> p b e", e=NE)
            link(dve.tensor_copy(scan[0][:, :, :], tot))
            now, s = 0, 1
            while s < B:
                a, c = scan[now], scan[1 - now]
                link(dve.tensor_copy(c[:, 0:s, :], a[:, 0:s, :]))
                link(dve.tensor_tensor(c[:, s:B, :], a[:, s:B, :], a[:, 0:B - s, :], ALU.add))
                now, s = 1 - now, 2 * s
            incl = scan[now]
            link(dve.tensor_tensor(base[:, :, :], incl[:, :, :], tot, ALU.subtract))
            link(dve.tensor_tensor(base[:, :, :], base[:, :, :], prefix[:, 0:B * NE].rearrange("p (b e) -> p b e", e=NE), ALU.add))
            link(dve.tensor_scalar(cnt[:, :], incl[:, B - 1, :], float(L - 1), None, ALU.add))
            link(dve.tensor_copy(cnti[:, :], cnt[:, :]))
            link(dve.tensor_scalar(cnti[:, :], cnti[:, :], 7, None, ALU.arith_shift_right))
            link(dve.tensor_copy(nt[:, :], cnti[:, :]))
            link(dve.tensor_copy(ends[0][:, :], nt[:, :]))
            now, s = 0, 1
            while s < NE:
                a, c = ends[now], ends[1 - now]
                link(dve.tensor_copy(c[:, 0:s], a[:, 0:s]))
                link(dve.tensor_tensor(c[:, s:NE], a[:, s:NE], a[:, 0:NE - s], ALU.add))
                now, s = 1 - now, 2 * s
            end = ends[now]
            link(dve.tensor_tensor(cnt[:, :], end[:, :], nt[:, :], ALU.subtract))
            link(dve.tensor_scalar(cnt[:, :], cnt[:, :], float(L), float(B * L), ALU.mult, ALU.add))
            link(dve.tensor_tensor(base[:, :, :], base[:, :, :], wide(cnt[:, :], [128, B, NE], 1), ALU.add))
            for i in range(2):
                link(dve.tensor_tensor(tie[:, :, :], hot[i][:, :, :], base[:, :, :], ALU.mult))
                link(dve.tensor_reduce(posf[:, :], tie[:, :, :], AX.X, ALU.add))
                link(dve.tensor_copy(M.place[:, i, :], posf[:, :]))
            link(dve.tensor_tensor(past[:, :, :], wide(slots[:, :], [128, SLOT_TILES, NE], 2),
                                   wide(end[:, :], [128, SLOT_TILES, NE], 1), ALU.is_ge))
            link(dve.tensor_reduce(ef[:, :], past[:, :, :], AX.X, ALU.add))
            link(dve.tensor_scalar(ef[:, :], ef[:, :], float(NE - 1), None, ALU.min))
            link(dve.memset(M.expert_of[:, 0:B], NE))
            dve.tensor_copy(M.expert_of[:, B:UNITS], ef[:, :]).then_inc(placed, 1)

        @block.gpsimd
        def _(pool):
            pool.memset(ones[:, :], 1.0).then_inc(made, 1)
            pool.memset(before[:, :], 1.0).then_inc(made, 1)
            pool.iota(rank8[:, :], pattern=[[-1, NE]], base=NE, channel_multiplier=0,
                      allow_small_or_imprecise_dtypes=True)
            pool.iota(slots[:, :], pattern=[[1, SLOT_TILES]], base=0, channel_multiplier=0,
                      allow_small_or_imprecise_dtypes=True).then_inc(made, 1)
            pool.wait_ge(made, 3)
            pool.affine_select(out=before[:, :], in_=before[:, :], compare_op=ALU.is_gt, fill=0.0,
                               base=0, pattern=[[1, 128]], channel_multiplier=-1).then_inc(made, 1)
            pool.wait_ge(asked, 1)
            pool.tensor_tensor(exps[:, :, :].rearrange("p b e -> p (b e)"), M.euler[:, 0:1].broadcast_to([128, B * NE]),
                               diff[:, :, :].rearrange("p b e -> p (b e)"), ALU.pow).then_inc(answered, 1)
            pool.tensor_tensor(pr[:, 1, :], M.euler[:, 0:1].broadcast_to([128, B]), d2[:, :], ALU.pow).then_inc(answered, 1)
            pool.wait_ge(placed, 1)
            pool.wait_ge(cleared, 16 * (SLOT_TILES // 8))
            for b in range(B):
                for i in range(2):
                    pool.indirect_dma_start(out=M.rows_dram[:, :],
                                            out_offset=bass.IndirectOffsetOnAxis(ap=M.place[:, i, b:b + 1], axis=0),
                                            in_=M.value[:, b, :], in_offset=None).then_inc(scattered, 16)
            pool.wait_ge(scattered, 16 * 2 * B)


def experts(nc, M):
    HT = -(-EH // 128)
    HR = [min(128, EH - 128 * t) for t in range(HT)]
    with signals(nc) as signal, ExitStack() as ctx:
        def sb(name, shape):
            return ctx.enter_context(nc.sbuf_tensor(name, shape, fp32))

        def pair(name):
            return [signal(f"{name}{u}") for u in range(2)]

        rows = sb("unit_rows", [128, 2, D])
        rowsT = sb("rowsT", [128, 2, KD, L])
        gate = sb("gate", [128, 2, EH])
        hid = sb("hidden", [128, 2, EH])
        hidT = sb("hiddenT", [128, 2, HT, L])
        done = sb("unit_out", [128, 2, D])
        psum = ctx.enter_context(nc.psum_tensor("unit_psum", [128, 2, 4, 512], fp32))
        TURN, GATE, UP, DOWN = range(4)
        rows_in = pair("rows_in")
        turned = pair("rows_turned")
        rowsT_done = pair("rowsT_done")
        gate_mm = pair("unit_gate_mm")
        gate_done = pair("unit_gate_done")
        hid_done = pair("unit_hid_done")
        hidT_mm = pair("unit_hidT_mm")
        hidT_done = pair("unit_hidT_done")
        down_mm = pair("unit_down_mm")
        down_done = pair("unit_down_done")
        stored = pair("unit_stored")
        block = ctx.enter_context(nc.Block())

        @block.sync
        def _(sp):
            def load(j, u):
                sp.wait_ge(turned[u], j)
                sp.dma_start(rows[:, u, :], M.rows_dram[bass.ds((2 * j + u) * L, L), :]).then_inc(rows_in[u], 16)

            def store(j, u):
                sp.wait_ge(down_done[u], j + 1)
                sp.dma_start(M.outs_dram[bass.ds((2 * j + u) * L, L), :], done[:, u, :]).then_inc(stored[u], 16)

            staged_pair_loop(sp, UNITS, (load, 0), (store, 2))
            for u in range(2):
                sp.wait_ge(stored[u], 16 * (UNITS // 2))

        @block.tensor
        def _(pe):
            def turn_rows(j, u):
                pe.wait_ge(rows_in[u], 16 * (j + 1))
                pe.wait_ge(hidT_done[u], j)
                for k in range(KD):
                    mm = pe.transpose(psum[:, u, TURN, k * L:k * L + L], rows[:, u, k * 128:k * 128 + 128], M.ident[:, :])
                mm.then_inc(turned[u], 1)

            def gate_up(j, u):
                e = pe.value_load(M.expert_of[0:1, bass.ds(2 * j + u, 1)], min_val=0, max_val=NE)
                pe.wait_ge(rowsT_done[u], j + 1)
                pe.wait_ge(hid_done[u], j)
                for bank, w in ((GATE, M.wg), (UP, M.wu)):
                    for k in range(KD):
                        mm = pe.matmul(psum[:, u, bank, 0:EH], rowsT[:, u, k, :],
                                       w[:, bass.ds(e, 1), k, :].rearrange("p e n -> p (e n)"),
                                       start=(k == 0), stop=(k == KD - 1))
                mm.then_inc(gate_mm[u], 1)

            def turn_hidden(j, u):
                pe.wait_ge(hid_done[u], j + 1)
                for t in range(HT):
                    mm = pe.transpose(psum[0:HR[t], u, TURN, t * L:t * L + L], hid[:, u, t * 128:t * 128 + HR[t]],
                                      M.ident[:, :])
                mm.then_inc(hidT_mm[u], 1)

            def down(j, u):
                e = pe.value_load(M.expert_of[0:1, bass.ds(2 * j + u, 1)], min_val=0, max_val=NE)
                pe.wait_ge(hidT_done[u], j + 1)
                pe.wait_ge(down_done[u], j)
                for t in range(HT):
                    mm = pe.matmul(psum[:, u, DOWN, 0:D], hidT[0:HR[t], u, t, :],
                                   M.wd[0:HR[t], bass.ds(e, 1), t, :].rearrange("p e n -> p (e n)"),
                                   start=(t == 0), stop=(t == HT - 1))
                mm.then_inc(down_mm[u], 1)

            staged_pair_loop(pe, UNITS, (turn_hidden, 2), (turn_rows, 0), (gate_up, 1), (down, 2))

        @block.scalar
        def _(act):
            def copy_rows(j, u):
                act.wait_ge(turned[u], j + 1)
                act.wait_ge(gate_mm[u], j)
                act.activation(rowsT[:, u, :, :], psum[:, u, TURN, 0:D].rearrange("p (k t) -> p k t", t=L), ACT.Copy
                               ).then_inc(rowsT_done[u], 1)

            def silu(j, u):
                act.wait_ge(gate_mm[u], j + 1)
                act.wait_ge(hid_done[u], j)
                act.activation(gate[:, u, :], psum[:, u, GATE, 0:EH], ACT.Silu).then_inc(gate_done[u], 1)

            def copy_hidden(j, u):
                act.wait_ge(hidT_mm[u], j + 1)
                act.wait_ge(down_mm[u], j)
                act.activation(hidT[:, u, 0:HT - 1, :], psum[:, u, TURN, 0:(HT - 1) * L].rearrange("p (k t) -> p k t", t=L),
                               ACT.Copy)
                act.activation(hidT[0:HR[-1], u, HT - 1, :], psum[0:HR[-1], u, TURN, (HT - 1) * L:HT * L],
                               ACT.Copy).then_inc(hidT_done[u], 1)

            staged_pair_loop(act, UNITS, (copy_hidden, 2), (copy_rows, 0), (silu, 1))

        @block.vector
        def _(dve):
            def multiply(j, u):
                dve.wait_ge(gate_done[u], j + 1)
                dve.wait_ge(hidT_mm[u], j)
                dve.tensor_tensor(hid[:, u, :], psum[:, u, UP, 0:EH], gate[:, u, :], ALU.mult).then_inc(hid_done[u], 1)

            def copy_out(j, u):
                dve.wait_ge(down_mm[u], j + 1)
                dve.wait_ge(stored[u], 16 * j)
                dve.tensor_copy(done[:, u, :], psum[:, u, DOWN, 0:D]).then_inc(down_done[u], 1)

            staged_pair_loop(dve, UNITS, (multiply, 1), (copy_out, 2))


def combine(nc, M, out):
    NBUF = 4
    with signals(nc) as signal, ExitStack() as ctx:
        def sb(name, shape):
            return ctx.enter_context(nc.sbuf_tensor(name, shape, fp32))

        got = sb("gathered", [128, NBUF, 2, D])
        shared = sb("shared_out", [128, NBUF, D])
        acc = sb("sum_out", [128, NBUF, D])
        bn = sb("ln_stats3", [128, B, 6])
        mv = sb("ln_mean_var3", [128, B, 2])
        rstd = sb("ln_rstd3", [128, B])
        gathered = [signal(f"gathered{i}") for i in range(NBUF)]
        shared_in = [signal(f"shared_in{i}") for i in range(NBUF)]
        summed = signal("summed")
        steps = signal("combine_step")
        var_done = signal("var_done")
        rstd_done = signal("rstd_done")
        normed = signal("normed")
        out_stored = signal("out_stored")
        block = ctx.enter_context(nc.Block())

        @block.gpsimd
        def _(pool):
            for b in range(B):
                if b >= NBUF:
                    pool.wait_ge(summed, b - NBUF + 1)
                for i in range(2):
                    pool.indirect_dma_start(out=got[:, b % NBUF, i, :], out_offset=None, in_=M.outs_dram[:, :],
                                            in_offset=bass.IndirectOffsetOnAxis(ap=M.place[:, i, b:b + 1], axis=0)
                                            ).then_inc(gathered[b % NBUF], 16)
                if b >= 2:
                    pool.wait_ge(var_done, b - 1)
                    pool.tensor_tensor(rstd[:, b - 2:b - 1], mv[:, b - 2, 1:2], M.minus_half[:, 0:1], ALU.pow).then_inc(rstd_done, 1)
            for b in (B - 2, B - 1):
                pool.wait_ge(var_done, b + 1)
                pool.tensor_tensor(rstd[:, b:b + 1], mv[:, b, 1:2], M.minus_half[:, 0:1], ALU.pow).then_inc(rstd_done, 1)

        @block.sync
        def _(sp):
            for b in range(B):
                if b >= NBUF:
                    sp.wait_ge(summed, b - NBUF + 1)
                sp.dma_start(shared[:, b % NBUF, :], M.outs_dram[b * L:b * L + L, :]).then_inc(shared_in[b % NBUF], 16)
                if b >= 3:
                    sp.wait_ge(normed, b - 2)
                    sp.dma_start(out[(b - 3) * L:(b - 2) * L, :], M.value[:, b - 3, :]).then_inc(out_stored, 16)
            for b in (B - 3, B - 2, B - 1):
                sp.wait_ge(normed, b + 1)
                sp.dma_start(out[b * L:b * L + L, :], M.value[:, b, :]).then_inc(out_stored, 16)
            sp.wait_ge(out_stored, 16 * B)

        @block.vector
        def _(dve):
            count = [0]

            def link(ins):
                count[0] += 1
                ins.then_inc(steps, 1)
                dve.wait_ge(steps, count[0])

            def normalize(b):
                dve.wait_ge(rstd_done, b + 1)
                dve.tensor_scalar(M.value[:, b, :], M.value[:, b, :], mv[:, b, 0:1], rstd[:, b:b + 1], ALU.subtract,
                                  ALU.mult).then_inc(normed, 1)

            for b in range(B):
                v = M.value[:, b, :]
                r = b % NBUF
                dve.wait_ge(shared_in[r], 16 * (b // NBUF + 1))
                link(dve.tensor_tensor(acc[:, r, :], v, shared[:, r, :], ALU.add))
                dve.wait_ge(gathered[r], 32 * (b // NBUF + 1))
                link(dve.scalar_tensor_tensor(out=acc[:, r, :], in0=got[:, r, 0, :], scalar=M.weight[:, b, 0:1],
                                              in1=acc[:, r, :], op0=ALU.mult, op1=ALU.add))
                dve.scalar_tensor_tensor(out=v, in0=got[:, r, 1, :], scalar=M.weight[:, b, 1:2],
                                         in1=acc[:, r, :], op0=ALU.mult, op1=ALU.add).then_inc(summed, 1)
                dve.wait_ge(summed, b + 1)
                link(dve.bn_stats(bn[:, b, :], v))
                link(dve.bn_aggr(mv[:, b, :], bn[:, b, :]))
                dve.tensor_scalar(mv[:, b, 1:2], mv[:, b, 1:2], 1e-5, None, ALU.add).then_inc(var_done, 1)
                if b >= 3:
                    normalize(b - 3)
            for b in (B - 3, B - 2, B - 1):
                normalize(b)


def program(nc, M, out):
    with ExitStack() as ctx:
        def sb(name, shape, dt=fp32):
            return ctx.enter_context(nc.sbuf_tensor(name, shape, dt))

        M.value = sb("value", [128, B, D])
        M.ident = sb("ident", [128, 128])
        M.causal = sb("causal", [128, 128])
        M.reverse = sb("reverse", [128, 128])
        M.reverse_first = sb("reverse_first", [128, 128])
        M.off32 = sb("off32", [128, 128])
        M.off64 = sb("off64", [128, 128])
        M.blockdiag = sb("blockdiag", [128, 128])
        M.minus_half = sb("minus_half", [128, 1])
        M.plus_half = sb("plus_half", [128, 1])
        M.euler = sb("euler", [128, 1])
        M.rq = sb("rq", [128, B, H])
        M.beta_r = sb("beta_r", [128, B, H])
        M.decay = sb("decay", [128, B, H])
        M.inv_tau = sb("inv_tau", [128, H])
        M.floor = sb("floor", [128, H, NP])
        M.keep = sb("keep", [128, H])
        M.gb2 = sb("gb2", [128, H * NP])
        M.gb1 = sb("gb1", [128, GH // 128])
        M.stat_scale = sb("stat_scale", [80, 1])
        M.wo = sb("wo", [128, KD, D])
        M.gw1x = sb("gw1x", [128, KD, GH])
        M.gw1s = sb("gw1s", [80, GH])
        M.gw2 = sb("gw2", [128, GH // 128, H * NP])
        M.logits = sb("router_logits", [128, B, NE])
        M.weight = sb("expert_weight", [128, B, 2])
        M.place = sb("row_of_token", [128, 2, B], mybir.dt.uint32)
        M.expert_of = sb("expert_of_unit", [128, UNITS], mybir.dt.uint32)
        build_constants(nc, M)
        project(nc, M)
        with ExitStack() as mixing:
            M.filtered = mixing.enter_context(nc.sbuf_tensor("filtered", [128, B, len(FIRS), D], fp32))
            invert_and_filter(nc, M)
            mix_paths(nc, M)
        M.wg = sb("wg", [128, NE + 1, KD, EH])
        M.wu = sb("wu", [128, NE + 1, KD, EH])
        M.wd = sb("wd", [128, NE + 1, -(-EH // 128), D])
        load_experts(nc, M)
        attend(nc, M)
        route(nc, M)
        experts(nc, M)
        combine(nc, M, out)


def kernel(**inputs):
    import numpy as np
    import concourse.bacc as bacc
    from concourse.bass_utils import run_bass_kernel_spmd

    a = {k: np.asarray(v) for k, v in inputs.items()}
    f = {k[len("L0_"):]: v for k, v in a.items() if k.startswith("L0_")}
    tokens = B * L
    x = a["x"].reshape(tokens, D)
    fir = np.zeros((FIR_PAD, len(FIRS), D), np.float32)
    for i, (name, taps) in enumerate(zip(("attn_fir_s", "attn_fir_m", "attn_fir_l"), FIRS)):
        fir[HALF - 1:HALF - 1 + taps, i, :] = f[name][:, ::-1].T
    fir = fir.reshape(FIR_PAD, len(FIRS), NFC, FC).transpose(2, 1, 0, 3)
    stat_scale = np.array([[1 / DV], [1 / DV], [1 / DV], [1.0]] * (H * NP), np.float32)
    arrays = dict(
        x=x, xT=x.T, ctxT=a["ctx_2048"].reshape(tokens, CTX).T, mask=a["mask_BxS2_fk1"],
        wq=f["attn_Wq"], wk=f["attn_Wk"], wv=f["attn_Wv"], wb=f["attn_Wb"],
        conv_q=f["attn_conv_q"], conv_k=f["attn_conv_k"], conv_v=f["attn_conv_v"],
        fir=fir, gw1=f["attn_gW1"], gw1s=f["attn_gW1"][D:].reshape(H * NP * 4, DV, GH),
        gb1=f["attn_gb1"].reshape(GH // 128, 128).T, gw2=f["attn_gW2"], gb2=f["attn_gb2"],
        log_tau=f["attn_log_tau"], eps_logit=f["attn_eps_logit"],
        norm_w=f["attn_norm_w"].reshape(DV, 1), wo=f["attn_Wo"], stat_scale=stat_scale,
        w_srcT=f["xattn_W_src"].T, b_src=f["xattn_b_src"], w_tgtT=f["xattn_W_tgt"].T, b_tgt=f["xattn_b_tgt"].reshape(KD, 128).T,
        b_key=f["xattn_b_src"][0:D].reshape(KD, 128).T, mask_col=a["mask_BxS2_fk1"].reshape(tokens, 1),
        w_outT=f["xattn_W_out"].T, b_out=f["xattn_b_out"], w_routerT=f["ffn_w_router"].T,
        wg=f["ffn_wg"], wu=f["ffn_wu"], wd=f["ffn_wd"], wg_s=f["ffn_wg_s"], wu_s=f["ffn_wu_s"], wd_s=f["ffn_wd_s"],
    )
    nc = bacc.Bacc("TRN2", target_bir_lowering=False, num_devices=1)
    M = Memory()
    given = {}
    ap = {}
    for name, v in arrays.items():
        v = np.ascontiguousarray(v)
        given[f"in_{name}"] = v
        ap[name] = nc.dram_tensor(f"in_{name}", v.shape, mybir.dt.from_np(v.dtype), kind="ExternalInput").ap()
    M.x_dram, M.xT_dram, M.ctxT_dram, M.mask_dram = ap["x"], ap["xT"], ap["ctxT"], ap["mask"]
    M.mask_col_dram, M.b_key_dram = ap["mask_col"], ap["b_key"]
    M.wq_dram, M.wk_dram, M.wv_dram, M.wb_dram = ap["wq"], ap["wk"], ap["wv"], ap["wb"]
    M.conv_q_dram, M.conv_k_dram, M.conv_v_dram = ap["conv_q"], ap["conv_k"], ap["conv_v"]
    M.fir_dram, M.gw1_dram, M.gw1s_dram, M.gb1_dram = ap["fir"], ap["gw1"], ap["gw1s"], ap["gb1"]
    M.gw2_dram, M.gb2_dram, M.log_tau, M.eps_logit = ap["gw2"], ap["gb2"], ap["log_tau"], ap["eps_logit"]
    M.norm_w_dram, M.wo_dram, M.stat_scale_dram = ap["norm_w"], ap["wo"], ap["stat_scale"]
    M.w_srcT_dram, M.b_src_dram, M.w_tgtT_dram, M.b_tgt_dram = ap["w_srcT"], ap["b_src"], ap["w_tgtT"], ap["b_tgt"]
    M.w_outT_dram, M.b_out_dram, M.w_routerT_dram = ap["w_outT"], ap["b_out"], ap["w_routerT"]
    M.wg_dram, M.wu_dram, M.wd_dram = ap["wg"], ap["wu"], ap["wd"]
    M.wg_s_dram, M.wu_s_dram, M.wd_s_dram = ap["wg_s"], ap["wu_s"], ap["wd_s"]
    M.qT_dram = nc.dram_tensor("qT", [D, tokens], fp32).ap()
    M.kT_dram = nc.dram_tensor("kT", [D, tokens], fp32).ap()
    M.nd_dram = nc.dram_tensor("nd", [B, H, L, CB], fp32).ap()
    M.inv_dram = nc.dram_tensor("inv", [B, H, L, CB], fp32).ap()
    M.rows_dram = nc.dram_tensor("rows", [UNITS * L, D], fp32).ap()
    M.outs_dram = nc.dram_tensor("outs", [UNITS * L, D], fp32).ap()
    out = nc.dram_tensor("out", [tokens, D], fp32, kind="ExternalOutput").ap()
    program(nc, M, out)
    r = run_bass_kernel_spmd(nc, [given], core_ids=[0])
    return r.results[0]["out"].reshape(B, L, D)
```

```python
import math

import concourse.bass as bass
from concourse import mybir
from contextlib import ExitStack, contextmanager

B, L, D = 32, 128, 256
H, DV = 4, 64
NP = 5
TAPS = 4
FIRS = (3, 15, 64)
CTX = 512
XH, XD = 8, 32
GH = 512
NE, EH = 8, 352
KD = D // 128
BLK = 512
BB = BLK // L
NBLK = B * L // BLK
CB = 32
NC = L // CB
FC = 8
HALF = L // 2
NFC = D // FC
SLOT_TILES = 2 * B + NE
UNITS = B + SLOT_TILES
FIR_PAD = L + HALF - 1

fp32 = mybir.dt.float32
ALU = mybir.AluOpType
ACT = mybir.ActivationFunctionType
AX = mybir.AxisListType


def pair_loop(eng, count, step):
    step(0, 0)
    step(0, 1)
    with eng.Fori(1, count // 2) as j:
        step(j, 0)
        step(j, 1)


def skewed_pair_loop(eng, count, early, late):
    early(0, 0)
    early(0, 1)
    late(0, 0)
    early(1, 0)
    late(0, 1)
    with eng.Fori(1, count // 2 - 1) as j:
        early(j, 1)
        late(j, 0)
        early(j + 1, 0)
        late(j, 1)
    last = count // 2 - 1
    early(last, 1)
    late(last, 0)
    late(last, 1)


def wide(ap, shape, axis):
    return ap.unsqueeze(axis).broadcast_to(shape)


def staged_pair_loop(eng, count, *stages):
    most = max(lag for _, lag in stages)
    fill = most + most % 2 + 2

    def turn(n):
        for step, lag in stages:
            if 0 <= n - lag < count:
                step((n - lag) // 2, (n - lag) % 2)

    for n in range(fill):
        turn(n)
    with eng.Fori(fill // 2, count // 2) as j:
        for u in range(2):
            for step, lag in stages:
                step(j + (u - lag) // 2, (u - lag) % 2)
    for n in range(count, count + most):
        turn(n)


def overlapped_pairs(eng, count, *steps):
    pairs = count // 2
    first = min(lag for _, _, lag in steps)
    last = max(lag for _, _, lag in steps)

    def turn(j):
        for step, u, lag in steps:
            if 0 <= j - lag < pairs:
                step(j - lag, u)

    for j in range(first, last + 1):
        turn(j)
    with eng.Fori(last + 1, pairs + first) as j:
        for step, u, lag in steps:
            step(j - lag, u)
    for j in range(pairs + first, pairs + last):
        turn(j)


def is_first(j):
    return isinstance(j, int) and j == 0


@contextmanager
def signals(nc):
    taken = []

    def signal(name):
        taken.append(nc.alloc_semaphore(name))
        return taken[-1]

    yield signal
    nc.clear_and_free_semaphores(taken)
    nc.all_engine_barrier()


class Memory:
    pass


def build_constants(nc, M):
    with signals(nc) as signal, ExitStack() as ctx:
        logtau = ctx.enter_context(nc.sbuf_tensor("logtau", [128, H], fp32))
        softp = ctx.enter_context(nc.sbuf_tensor("softp", [128, 3, H], fp32))
        epsl = ctx.enter_context(nc.sbuf_tensor("epsl", [128, H, NP], fp32))
        norm_w = ctx.enter_context(nc.sbuf_tensor("norm_w", [128, 1], fp32))
        loaded = signal("const_loaded")
        zeroed = signal("const_zeroed")
        act_step = signal("const_act_step")
        dve_step = signal("const_dve_step")
        block = ctx.enter_context(nc.Block())

        @block.sync
        def _(sp):
            sp.dma_start(logtau[:, :], M.log_tau.partition_broadcast(128)).then_inc(loaded, 16)
            sp.dma_start(epsl[:, :, :], M.eps_logit.partition_broadcast(128)).then_inc(loaded, 16)
            sp.dma_start(M.gb2[:, :], M.gb2_dram.partition_broadcast(128)).then_inc(loaded, 16)
            sp.dma_start(norm_w[0:DV, :], M.norm_w_dram).then_inc(loaded, 16)
            sp.dma_start(norm_w[DV:128, :], M.norm_w_dram).then_inc(loaded, 16)
            sp.dma_start(M.wo[:, :, :], M.wo_dram.rearrange("(k p) n -> p k n", p=128)).then_inc(loaded, 16)
            sp.dma_start(M.gw1x[:, :, :], M.gw1_dram[0:D, :].rearrange("(k p) n -> p k n", p=128)).then_inc(loaded, 16)
            sp.dma_start(M.gw2[:, :, :], M.gw2_dram.rearrange("(k p) n -> p k n", p=128)).then_inc(loaded, 16)
            sp.dma_start(M.gb1[:, :], M.gb1_dram).then_inc(loaded, 16)
            sp.dma_start(M.stat_scale[:, :], M.stat_scale_dram).then_inc(loaded, 16)
            sp.wait_ge(loaded, 160)

        @block.gpsimd
        def _(pool):
            pool.memset(M.ident[:, :], 0.0).then_inc(zeroed, 1)
            pool.memset(M.causal[:, :], 1.0).then_inc(zeroed, 1)
            for m in (M.reverse, M.reverse_first):
                pool.memset(m[:, :], 0.0).then_inc(zeroed, 1)
            pool.memset(M.minus_half[:, :], -0.5)
            pool.memset(M.plus_half[:, :], 0.5)
            pool.memset(M.euler[:, :], 2.718281828459045)
            pool.wait_ge(zeroed, 4)
            pool.affine_select(out=M.ident[:, :], in_=M.ident[:, :], compare_op=ALU.not_equal, fill=1.0,
                               base=0, pattern=[[-1, 128]], channel_multiplier=1)
            for m, last in ((M.reverse, L - 1), (M.reverse_first, HALF - 1)):
                pool.affine_select(out=m[:, :], in_=m[:, :], compare_op=ALU.not_equal, fill=1.0,
                                   base=-last, pattern=[[1, 128]], channel_multiplier=1)
            pool.affine_select(out=M.causal[:, :], in_=M.causal[:, :], compare_op=ALU.is_ge, fill=0.0,
                               base=0, pattern=[[1, 128]], channel_multiplier=-1)

        @block.scalar
        def _(act):
            act.wait_ge(loaded, 160)
            act.activation(softp[:, 0, :], logtau[:, :], ACT.Abs).then_inc(act_step, 1)
            act.wait_ge(act_step, 1)
            act.activation(softp[:, 1, :], softp[:, 0, :], ACT.Exp, scale=-1.0).then_inc(act_step, 1)
            act.wait_ge(act_step, 2)
            act.activation(softp[:, 2, :], softp[:, 1, :], ACT.Ln, bias=1.0).then_inc(act_step, 1)
            act.activation(epsl[:, :, :], epsl[:, :, :], ACT.Exp, scale=-1.0).then_inc(act_step, 1)

        @block.vector
        def _(dve):
            steps = [0]

            def link(ins):
                steps[0] += 1
                ins.then_inc(dve_step, 1)
                dve.wait_ge(dve_step, steps[0])

            for m in (M.off32, M.off64, M.blockdiag):
                link(dve.memset(m[:, :], 0.0))
            dve.memset(M.off32[0:32, 32:64], 1.0)
            dve.memset(M.off32[64:96, 96:128], 1.0)
            dve.memset(M.off64[0:64, 64:128], 1.0)
            for c in range(NC):
                dve.memset(M.blockdiag[c * CB:(c + 1) * CB, c * CB:(c + 1) * CB], 1.0)
            dve.wait_ge(loaded, 160)
            for k in range(KD):
                link(dve.tensor_scalar(M.wo[:, k, :], M.wo[:, k, :], norm_w[:, 0:1], None, ALU.mult))
            dve.wait_ge(act_step, 4)
            link(dve.tensor_scalar(logtau[:, :], logtau[:, :], 0.0, 0.5, ALU.max, ALU.add))
            link(dve.tensor_tensor(logtau[:, :], logtau[:, :], softp[:, 2, :], ALU.add))
            link(dve.reciprocal(M.inv_tau[:, :], logtau[:, :]))
            link(dve.tensor_scalar(epsl[:, :, :], epsl[:, :, :], 1.0, None, ALU.add))
            link(dve.reciprocal(epsl[:, :, :], epsl[:, :, :]))
            link(dve.tensor_scalar(M.floor[:, :, :], epsl[:, :, :], 0.2, None, ALU.mult))
            link(dve.tensor_reduce(M.keep[:, :], M.floor[:, :, :], AX.X, ALU.add))
            link(dve.tensor_scalar(M.keep[:, :], M.keep[:, :], -1.0, 1.0, ALU.mult, ALU.add))


def project(nc, M):
    NT = 3 * KD
    PB = 4
    USES = 2 * NT // PB
    with signals(nc) as signal, ExitStack() as ctx:
        def sb(name, shape):
            return ctx.enter_context(nc.sbuf_tensor(name, shape, fp32))

        def sem(name):
            return signal(name)

        wqkv = sb("wqkv", [128, 3, KD, D])
        taps = sb("conv_taps", [128, 3, KD, TAPS])
        wb = sb("wb", [128, KD, H])
        headsel = sb("headsel", [128, 2])
        xT = sb("xT_block", [128, 2, KD, BLK])
        conv = sb("conv_acc", [128, NT, BLK])
        qkv = sb("qkv_block", [128, 2, NT, BLK])
        squares = sb("qk_squares", [128, 2, 2 * KD, BLK])
        tanh_b = sb("tanh_beta", [128, 2, BB, H])
        ssq = sb("qk_ssq", [128, 2, BB, 2 * H])
        neg_decay = sb("neg_decay", [128, 2, BB, H])
        ndG = sb("decay_gram", [128, 2, BB, H, L])
        GPART = DV // NBLK
        gsum = sb("gate_rows", [80, GPART, GH])
        gpart = sb("gate_part", [80, 2, GPART, GH])
        psum = ctx.enter_context(nc.psum_tensor("proj_psum", [128, 8, BLK], fp32))
        V_BANK, S_BANK, G_BANK = PB, PB + 1, PB + 2

        weights_in = sem("weights_in")
        xT_in = [sem(f"xT_in{u}") for u in range(2)]
        proj_done = sem("proj_done")
        tap3_done = sem("tap3_done")
        conv_done = [sem(f"conv_done{b}") for b in range(PB)]
        silu_done = sem("silu_done")
        qk_stored = [sem(f"qk_stored{u}") for u in range(2)]
        squares_done = sem("squares_done")
        small_done = [sem(f"small_done{u}") for u in range(2)]
        tanh_done = sem("tanh_done")
        ssq_done = sem("ssq_done")
        decay_done = sem("decay_done")
        vT_done = sem("vT_done")
        v_kept = sem("v_kept")
        gram_done = [sem(f"gram_done{u}") for u in range(2)]
        nd_done = sem("nd_done")
        nd_stored = [sem(f"nd_stored{u}") for u in range(2)]
        norm_done = sem("norm_done")
        decay_step = sem("decay_step")
        taps_step = sem("taps_step")
        gate_in = [sem(f"gate_in{u}") for u in range(2)]
        gate_step = sem("gate_step")
        sel_set = sem("sel_set")
        block = ctx.enter_context(nc.Block())

        def bank_use(u, m):
            return (NT * u + m) % PB, (NT * u + m) // PB

        @block.sync
        def _(sp):
            for i, w in enumerate((M.wq_dram, M.wk_dram, M.wv_dram)):
                sp.dma_start(wqkv[:, i, :, :], w.rearrange("(k p) n -> p k n", p=128)).then_inc(weights_in, 16)
            for i, w in enumerate((M.conv_q_dram, M.conv_k_dram, M.conv_v_dram)):
                sp.dma_start(taps[:, i, :, :], w.rearrange("(k p) n -> p k n", p=128)).then_inc(weights_in, 16)
            sp.dma_start(wb[:, :, :], M.wb_dram.rearrange("(k p) n -> p k n", p=128)).then_inc(weights_in, 16)

            def load_x(j, u):
                sp.wait_ge(small_done[u], j)
                sp.dma_start(xT[:, u, :, :],
                             M.xT_dram[:, bass.ds((2 * j + u) * BLK, BLK)].rearrange("(k p) n -> p k n", p=128)
                             ).then_inc(xT_in[u], 16)
                sp.wait_ge(gate_step, 2 * j + u)
                sp.dma_start(gpart[:, u, :, :], M.gw1s_dram[:, bass.ds((2 * j + u) * GPART, GPART), :]
                             ).then_inc(gate_in[u], 16)

            pair_loop(sp, NBLK, load_x)

        @block.tensor
        def _(pe):
            def projections(j, u):
                pe.wait_ge(xT_in[u], 16 * (j + 1))
                for m in range(NT):
                    b, r = bank_use(u, m)
                    pe.wait_ge(conv_done[b], USES * j + r)
                    for k in range(KD):
                        mm = pe.matmul(psum[:, b, :], wqkv[:, m // KD, k, (m % KD) * 128:(m % KD) * 128 + 128],
                                       xT[:, u, k, :], start=(k == 0), stop=(k == KD - 1))
                    mm.then_inc(proj_done, 1)

            def derived(j, u):
                n = 2 * j + u
                pe.wait_ge(squares_done, 2 * KD * (n + 1))
                pe.wait_ge(tanh_done, n)
                pe.wait_ge(ssq_done, n)
                for q in range(BB):
                    tok = slice(q * L, q * L + L)
                    for t in range(2 * KD):
                        pe.matmul(psum[:, S_BANK, 12 * q + 2 * t:12 * q + 2 * t + 2], squares[:, u, t, tok],
                                  headsel[:, :], start=True, stop=True)
                    for k in range(KD):
                        mm = pe.matmul(psum[:, S_BANK, 12 * q + 8:12 * q + 12], xT[:, u, k, tok], wb[:, k, :],
                                       start=(k == 0), stop=(k == KD - 1))
                mm.then_inc(small_done[u], 1)
                pe.wait_ge(silu_done, NT * (n + 1))
                for g in range(BB // 2):
                    pe.wait_ge(v_kept, 2 * n + g)
                    for q in (2 * g, 2 * g + 1):
                        for t in range(KD):
                            at = (q % 2) * D + t * 128
                            mm = pe.transpose(psum[:, V_BANK, at:at + 128],
                                              qkv[:, u, 2 * KD + t, q * L:q * L + L], M.ident[:, :])
                    mm.then_inc(vT_done, 1)
                    pe.wait_ge(nd_done, BB * n + 2 * g)
                    for q in (2 * g, 2 * g + 1):
                        for h in range(H):
                            rows = slice((h % 2) * DV, (h % 2) * DV + DV)
                            at = (2 * (q % 2) + h // 2) * L
                            kT = qkv[rows, u, KD + h // 2, q * L:q * L + L]
                            mm = pe.matmul(psum[:, G_BANK + h % 2, at:at + L], kT, kT, start=True, stop=True)
                    mm.then_inc(gram_done[u], 1)

            pe.wait_ge(weights_in, 7 * 16)
            pe.wait_ge(sel_set, 1)
            skewed_pair_loop(pe, NBLK, projections, derived)

        @block.scalar
        def _(act):
            act.wait_ge(weights_in, 7 * 16)

            def scaled_tap(j, u, m):
                n = 2 * j + u
                b, r = bank_use(u, m)
                act.wait_ge(proj_done, NT * n + m + 1)
                act.wait_ge(silu_done, NT * n)
                act.activation(conv[:, m, :], psum[:, b, :], ACT.Copy,
                               scale=taps[:, m // KD, m % KD, TAPS - 1:TAPS]).then_inc(tap3_done, 1)

            def silu(j, u, m):
                b, r = bank_use(u, m)
                act.wait_ge(conv_done[b], USES * j + r + 1)
                if m == 0:
                    act.wait_ge(qk_stored[u], 32 * j)
                    act.wait_ge(gram_done[u], 2 * j)
                    act.wait_ge(squares_done, 2 * KD * 2 * j)
                act.activation(qkv[:, u, m, :], conv[:, m, :], ACT.Silu).then_inc(silu_done, 1)

            def convolved(j, u):
                for m in range(NT + 2):
                    if m < NT:
                        scaled_tap(j, u, m)
                    if m >= 2:
                        silu(j, u, m - 2)

            def small(j, u):
                n = 2 * j + u
                act.wait_ge(small_done[u], j + 1)
                act.wait_ge(decay_done, n)
                act.activation(tanh_b[:, u, :, :],
                               psum[:, S_BANK, 0:12 * BB].rearrange("p (q c) -> p q c", c=12)[:, :, 8:12],
                               ACT.Tanh, scale=0.5).then_inc(tanh_done, 1)
                for g in range(2):
                    act.wait_ge(vT_done, 2 * n + g + 1)
                    act.activation(M.value[:, bass.ds(BB * n + 2 * g, 2), :],
                                   psum[:, V_BANK, :].rearrange("p (q c) -> p q c", c=D),
                                   ACT.Copy).then_inc(v_kept, 1)

            def store_qk(j, u):
                act.wait_ge(silu_done, NT * (2 * j + u) + 2 * KD)
                for i, dst in enumerate((M.qT_dram, M.kT_dram)):
                    act.dma_start(dst[:, bass.ds((2 * j + u) * BLK, BLK)].rearrange("(k p) n -> p k n", p=128),
                                  qkv[:, u, KD * i:KD * i + KD, :]).then_inc(qk_stored[u], 16)

            def store_decays(j, u):
                n = 2 * j + u
                act.wait_ge(nd_done, BB * (n + 1))
                for c in range(NC):
                    rows = slice(c * CB, c * CB + CB)
                    act.dma_start(M.nd_dram[bass.ds(BB * n, BB), :, rows, :].rearrange("b h t c -> t (b h) c"),
                                  ndG[rows, u, :, :, rows].rearrange("t b h c -> t (b h) c")).then_inc(nd_stored[u], 16)

            staged_pair_loop(act, NBLK, (convolved, 0), (store_qk, 0), (small, 1), (store_decays, 2))
            for u in range(2):
                act.wait_ge(qk_stored[u], 32 * (NBLK // 2))
                act.wait_ge(nd_stored[u], 16 * NC * (NBLK // 2))

        @block.vector
        def _(dve):
            dve.memset(headsel[:, :], 0.0).then_inc(taps_step, 1)
            dve.wait_ge(taps_step, 1)
            dve.memset(headsel[0:DV, 0:1], 1.0)
            dve.memset(headsel[DV:128, 1:2], 1.0).then_inc(sel_set, 1)
            dve.wait_ge(weights_in, 7 * 16)

            def convolutions(j, u):
                n = 2 * j + u
                for m0 in range(0, NT, 2):
                    for s in range(1, TAPS):
                        for m in (m0, m0 + 1):
                            b, _ = bank_use(u, m)
                            if s == 1:
                                dve.wait_ge(tap3_done, NT * n + m + 1)
                            else:
                                dve.wait_ge(taps_step, 1 + NT * (TAPS - 2) * n
                                            + m0 * (TAPS - 2) + 2 * (s - 2) + (m - m0) + 1)
                            acc = conv[:, m, :].rearrange("p (q t) -> p q t", t=L)
                            raw = psum[:, b, :].rearrange("p (q t) -> p q t", t=L)
                            ins = dve.scalar_tensor_tensor(
                                out=acc[:, :, s:L], in0=raw[:, :, 0:L - s],
                                scalar=taps[:, m // KD, m % KD, TAPS - 1 - s:TAPS - s],
                                in1=acc[:, :, s:L], op0=ALU.mult, op1=ALU.add)
                            ins.then_inc(taps_step if s < TAPS - 1 else conv_done[b], 1)

            def decays(j, u):
                n = 2 * j + u
                dve.wait_ge(small_done[u], j + 1)
                dve.wait_ge(tanh_done, n + 1)
                dve.wait_ge(decay_done, n)
                dve.tensor_scalar(ssq[:, u, :, :],
                                  psum[:, S_BANK, 0:12 * BB].rearrange("p (q c) -> p q c", c=12)[:, :, 0:8],
                                  1e-6, None, ALU.add).then_inc(ssq_done, 1)
                here = bass.ds(BB * n, BB)
                dve.tensor_scalar(tanh_b[:, u, :, :], tanh_b[:, u, :, :], 0.5, 0.5, ALU.mult,
                                  ALU.add).then_inc(decay_step, 1)
                dve.wait_ge(norm_done, n + 1)
                dve.tensor_copy(M.rq[:, here, :], ssq[:, u, :, 0:H])
                dve.wait_ge(decay_step, 3 * n + 1)
                dve.tensor_tensor(M.beta_r[:, here, :], tanh_b[:, u, :, :], ssq[:, u, :, H:2 * H],
                                  ALU.mult).then_inc(decay_step, 1)
                dve.wait_ge(decay_step, 3 * n + 2)
                dve.tensor_tensor(M.decay[:, here, :], M.beta_r[:, here, :], ssq[:, u, :, H:2 * H],
                                  ALU.mult).then_inc(decay_step, 1)
                dve.wait_ge(decay_step, 3 * n + 3)
                dve.tensor_scalar(neg_decay[:, u, :, :], M.decay[:, here, :], -1.0, None,
                                  ALU.mult).then_inc(decay_done, 1)
                dve.wait_ge(decay_done, n + 1)
                dve.wait_ge(nd_stored[u], 16 * NC * j)
                for q in range(BB):
                    dve.wait_ge(gram_done[u], 2 * j + q // 2 + 1)
                    dve.tensor_tensor(ndG[:, u, q, :, :].rearrange("p (a b) t -> p b a t", b=2),
                                      psum[:, G_BANK:G_BANK + 2, (q % 2) * 2 * L:(q % 2) * 2 * L + 2 * L]
                                      .rearrange("p b (a t) -> p b a t", t=L),
                                      wide(neg_decay[:, u, q, :].rearrange("p (a b) -> p b a", b=2),
                                           [128, 2, 2, L], 3),
                                      ALU.mult).then_inc(nd_done, 1)

            skewed_pair_loop(dve, NBLK, convolutions, decays)

        @block.gpsimd
        def _(pool):
            def square_qk(j, u):
                n = 2 * j + u
                pool.wait_ge(small_done[u], j)
                for t in range(2 * KD):
                    pool.wait_ge(silu_done, NT * n + t + 1)
                    pool.tensor_tensor(squares[:, u, t, :], qkv[:, u, t, :], qkv[:, u, t, :],
                                       ALU.mult).then_inc(squares_done, 1)

            def gate_rows(j, u):
                pool.wait_ge(gate_in[u], 16 * (j + 1))
                pool.wait_ge(gate_step, 2 * j + u + 1)
                pool.tensor_tensor(gsum[:, :, :], gsum[:, :, :], gpart[:, u, :, :], ALU.add).then_inc(gate_step, 1)

            def square_and_sum(j, u):
                square_qk(j, u)
                gate_rows(j, u)

            def inverse_norms(j, u):
                n = 2 * j + u
                pool.wait_ge(ssq_done, n + 1)
                pool.tensor_tensor(ssq[:, u, :, :], ssq[:, u, :, :],
                                   wide(wide(M.minus_half[:, 0], [128, 2 * H], 1), [128, BB, 2 * H], 1),
                                   ALU.pow).then_inc(norm_done, 1)

            pool.memset(gsum[:, :, :], 0.0).then_inc(gate_step, 1)
            skewed_pair_loop(pool, NBLK, square_and_sum, inverse_norms)

            done = NBLK + 1
            for half in (4, 2, 1):
                pool.wait_ge(gate_step, done)
                pool.tensor_tensor(gsum[:, 0:half, :], gsum[:, 0:half, :], gsum[:, half:2 * half, :],
                                   ALU.add).then_inc(gate_step, 1)
                done += 1
            pool.wait_ge(gate_step, done)
            pool.tensor_scalar(M.gw1s[:, :], gsum[:, 0, :], M.stat_scale[:, 0:1], None, ALU.mult)


def invert_and_filter(nc, M):
    NFIR = len(FIRS)
    with signals(nc) as signal, ExitStack() as ctx:
        def sb(name, shape):
            return ctx.enter_context(nc.sbuf_tensor(name, shape, fp32))

        def sem(name):
            return signal(name)

        nd = sb("neg_decay_blocks", [128, NC, CB, CB])
        inv = sb("inverses", [128, NC, CB, CB])
        prod = sb("products", [128, 2, 2, (CB - 1) * (CB - 1)])
        toep = sb("toep", [128, 2, NFIR, HALF, FC])
        window = sb("window", [128, 2, FC, 2, B])
        psum = ctx.enter_context(nc.psum_tensor("fir_psum", [128, 2, 3, FC * 2 * B], fp32))
        LONG, SHORT, WINDOW = range(3)

        nd_in = sem("nd_in")
        inv_row = [sem(f"inv_row{g}") for g in range(2)]
        inv_mul = [sem(f"inv_mul{g}") for g in range(2)]
        inv_set = sem("inv_set")
        inv_stored = sem("inv_stored")
        toep_in = [sem(f"toep_in{u}") for u in range(2)]
        window_done = [sem(f"window_done{u}") for u in range(2)]
        window_kept = [sem(f"window_kept{u}") for u in range(2)]
        fir_done = [sem(f"fir_done{u}") for u in range(2)]
        fir_kept = [sem(f"fir_kept{u}") for u in range(2)]
        block = ctx.enter_context(nc.Block())

        @block.sync
        def _(sp):
            sp.dma_start(nd[:, :, :, :], M.nd_dram.rearrange("b h (c i) j -> (b h) c i j", i=CB)).then_inc(nd_in, 16)

            def load_toeplitz(j, u):
                sp.wait_ge(fir_done[u], j)
                src = bass.AP(tensor=M.fir_dram.tensor, offset=(2 * j + u) * FIR_PAD * NFIR * FC,
                              ap=[[FC, 128], [FIR_PAD * FC, NFIR], [1, HALF * FC]])
                sp.dma_start(toep[:, u, :, :, :].rearrange("p f t c -> p f (t c)"), src).then_inc(toep_in[u], 16)

            pair_loop(sp, NFC, load_toeplitz)
            for g in range(2):
                sp.wait_ge(inv_row[g], CB - 1)
            sp.dma_start(M.inv_dram.rearrange("b h (c i) j -> (b h) c i j", i=CB), inv[:, :, :, :]).then_inc(inv_stored, 16)
            sp.wait_ge(inv_stored, 16)

        @block.tensor
        def _(pe):
            def windows(j, u):
                pe.wait_ge(window_kept[u], j)
                src = M.value[:, :, bass.ds((2 * j + u) * FC, FC)]
                pe.matmul(psum[:, u, WINDOW, 0:B * FC], M.reverse_first[:, :], src, start=True, stop=True)
                pe.matmul(psum[:, u, WINDOW, B * FC:2 * B * FC], M.reverse[:, :], src, start=True, stop=True
                          ).then_inc(window_done[u], 1)

            def filters(j, u):
                pe.wait_ge(toep_in[u], 16 * (j + 1))
                pe.wait_ge(window_kept[u], j + 1)
                pe.wait_ge(fir_kept[u], 6 * j)
                for c in range(FC):
                    tokens = window[:, u, c, :, :].rearrange("p h b -> p (h b)")
                    out = slice(c * 2 * B, (c + 1) * 2 * B)
                    pe.matmul(psum[:, u, LONG, out], toep[:, u, 1:3, :, c].rearrange("p f t -> p (f t)"), tokens,
                              start=True, stop=True)
                    mm = pe.matmul(psum[0:HALF, u, SHORT, out], toep[:, u, 0, :, c], tokens, start=True, stop=True)
                mm.then_inc(fir_done[u], 1)

            staged_pair_loop(pe, NFC, (windows, 0), (filters, 1))

        @block.scalar
        def _(act):
            def keep_windows(j, u):
                act.wait_ge(window_done[u], j + 1)
                act.wait_ge(fir_done[u], j)
                act.activation(window[:, u, :, :, :].rearrange("p c h b -> p h b c"),
                               psum[:, u, WINDOW, :].rearrange("p (h b c) -> p h b c", h=2, b=B),
                               ACT.Copy).then_inc(window_kept[u], 1)

            def keep(j, u):
                act.wait_ge(fir_done[u], j + 1)
                for f, bank, r in ((0, SHORT, 0), (1, LONG, 0), (2, LONG, HALF)):
                    for h in range(2):
                        out = M.filtered[h * HALF:(h + 1) * HALF, :, f, bass.ds((2 * j + u) * FC, FC)]
                        src = psum[r:r + HALF, u, bank, :].rearrange("p (c h b) -> p h b c", h=2, b=B)
                        act.activation(out, src[:, h, :, :], ACT.Copy).then_inc(fir_kept[u], 1)

            staged_pair_loop(act, NFC, (keep_windows, 0), (keep, 2))

        @block.vector
        def _(dve):
            dve.memset(inv[:, :, :, :], 0.0).then_inc(inv_set, 1)
            dve.wait_ge(inv_set, 1)
            for c in range(NC):
                ins = dve.memset(inv[:, c, :, :].rearrange("p k i -> p (k i)")[:, 0:CB * CB:CB + 1], 1.0)
            ins.then_inc(inv_set, 1)
            dve.wait_ge(inv_set, 2)
            dve.wait_ge(nd_in, 16)
            for i in range(1, CB):
                for g in range(2):
                    blocks = slice(2 * g, 2 * g + 2)
                    if i > 1:
                        dve.wait_ge(inv_row[g], i - 1)
                    p = prod[:, g, :, 0:i * i].rearrange("p c (k j) -> p c k j", j=i)
                    dve.tensor_tensor(p, inv[:, blocks, 0:i, 0:i], wide(nd[:, blocks, i, 0:i], [128, 2, i, i], 2),
                                      ALU.mult).then_inc(inv_mul[g], 1)
                for g in range(2):
                    blocks = slice(2 * g, 2 * g + 2)
                    dve.wait_ge(inv_mul[g], i)
                    p = prod[:, g, :, 0:i * i].rearrange("p c (k j) -> p c k j", j=i)
                    dve.tensor_reduce(inv[:, blocks, 0:i, i], p, AX.X, ALU.add).then_inc(inv_row[g], 1)


def mix_paths(nc, M):
    P, S, W = 4, 3, DV * H
    with signals(nc) as signal, ExitStack() as ctx:
        def sb(name, shape):
            return ctx.enter_context(nc.sbuf_tensor(name, shape, fp32))

        def pair(name):
            return [signal(f"{name}{u}") for u in range(2)]

        qT = sb("qT_tile", [128, 2, KD, L])
        kT = sb("kT_tile", [128, 2, KD, L])
        xT = sb("xT_tile", [128, 2, KD, L])
        x = sb("x_tile", [128, 2, D])
        invp = sb("inv_packed", [128, 2, H, CB])
        inv = sb("inv_tile", [128, 2, H, L])
        n32 = sb("gram_off32", [128, 2, H, L])
        n64 = sb("gram_off64", [128, 2, H, L])
        att = sb("causal_scores", [128, 2, H, L])
        rhs = sb("beta_r_v", [128, 2, W])
        x1s = sb("solve_x1", [128, 2, W])
        ys = sb("solve_y", [128, 2, W])
        x2s = sb("solve_x2", [128, 2, W])
        w1s = sb("solve_w1", [128, 2, W])
        delta = sb("delta_path", [128, 2, W])
        sq = sb("path_squares", [128, 2, NP, D])
        stat = sb("path_stats", [128, 2, NP * H, 4])
        statT = sb("path_statsT", [80, 2, L])
        hid = sb("gate_hiddenT", [128, 2, GH // 128, L])
        lg = sb("gate_logits", [128, 2, H, NP])
        ex = sb("gate_exps", [128, 2, H, NP])
        hsum = sb("gate_sums", [128, 2, 4, H])
        mixed = sb("mixed", [128, 2, D])
        mixT = sb("mixedT", [128, 2, KD, L])
        y = sb("residual", [128, 2, D])
        bn = sb("ln_stats", [128, 2, 6])
        mv = sb("ln_mean_var", [128, 2, 2])
        carrier = sb("carrier", [128, 1])
        psum = ctx.enter_context(nc.psum_tensor("mix_psum", [128, 2, 4, 512], fp32))
        EVEN, ODD, SOLVE, GATE = range(4)

        loaded = pair("tile_loaded")
        gate_loaded = pair("gate_loaded")
        scores_done = pair("scores_done")
        masked = pair("masked")
        expanded = pair("expanded")
        solve_mm = pair("solve_mm")
        solve_ev = pair("solve_ev")
        delta_done = pair("delta_done")
        squared = pair("squared")
        less_done = pair("less_w1_done")
        stats_done = pair("stats_done")
        norms_done = pair("norms_done")
        gate_mm = pair("gate_mm")
        gate_ev = pair("gate_ev")
        small = pair("small_step")
        shifted = pair("logits_shifted")
        exps_done = pair("exps_done")
        probs_done = pair("probs_done")
        weighted = pair("weighted")
        path_added = pair("path_added")
        mix_summed = pair("mix_summed")
        mix_squared = pair("mix_squared")
        power_asked = pair("power_asked")
        power_done = pair("power_done")
        ln_step = pair("ln_step")
        x1_done = pair("x1_done")
        block = ctx.enter_context(nc.Block())

        @block.sync
        def _(sp):
            def load_delta(j, u):
                n = 2 * j + u
                cols = bass.ds(n * L, L)
                sp.wait_ge(scores_done[u], j)
                sp.wait_ge(expanded[u], j)
                sp.dma_start(kT[:, u, :, :], M.kT_dram[:, cols].rearrange("(k p) n -> p k n", p=128)).then_inc(loaded[u], 16)
                sp.dma_start(qT[:, u, :, :], M.qT_dram[:, cols].rearrange("(k p) n -> p k n", p=128)).then_inc(loaded[u], 16)
                sp.dma_start(invp[:, u, :, :], M.inv_dram[bass.ds(n, 1)].rearrange("b h t c -> t (b h) c")).then_inc(loaded[u], 16)

            def load_gate(j, u):
                cols = bass.ds((2 * j + u) * L, L)
                sp.wait_ge(gate_mm[u], 5 * j)
                sp.dma_start(xT[:, u, :, :], M.xT_dram[:, cols].rearrange("(k p) n -> p k n", p=128)).then_inc(gate_loaded[u], 16)
                sp.wait_ge(x1_done[u], j)
                sp.dma_start(x[:, u, :], M.x_dram[cols, :]).then_inc(gate_loaded[u], 16)

            overlapped_pairs(sp, B, (load_delta, 0, 0), (load_delta, 1, 0), (load_gate, 0, 1), (load_gate, 1, 1))

        @block.tensor
        def _(pe):
            def scores(j, u):
                pe.wait_ge(loaded[u], 48 * (j + 1))
                pe.wait_ge(masked[u], j)
                for h in range(H):
                    rows = slice((h % 2) * DV, (h % 2) * DV + DV)
                    at = (h // 2) * L
                    k, q = kT[rows, u, h // 2, :], qT[rows, u, h // 2, :]
                    pe.matmul(psum[:, u, EVEN + h % 2, at:at + L], k, k, start=True, stop=True)
                    mm = pe.matmul(psum[:, u, EVEN + h % 2, 2 * L + at:2 * L + at + L], k, q, start=True, stop=True)
                mm.then_inc(scores_done[u], 1)

            def product(i, left, right):
                def step(j, u):
                    if i == 0:
                        pe.wait_ge(expanded[u], j + 1)
                        pe.wait_ge(delta_done[u], j)
                    else:
                        pe.wait_ge(solve_ev[u], 7 * j + i)
                    if i == 1:
                        pe.wait_ge(masked[u], j + 1)
                    for h in range(H):
                        mm = pe.matmul(psum[:, u, SOLVE, h * DV:h * DV + DV], left[:, u, h, :],
                                       right[:, u, h * DV:h * DV + DV], start=True, stop=True)
                    mm.then_inc(solve_mm[u], 1)
                return step

            def statsT(j, u):
                pe.wait_ge(norms_done[u], j + 1)
                pe.wait_ge(gate_ev[u], 5 * j)
                pe.transpose(psum[0:80, u, GATE, 0:L], stat[:, u, :, :].rearrange("p a s -> p (a s)"),
                             M.ident[:, :]).then_inc(gate_mm[u], 1)

            def hidden(j, u):
                pe.wait_ge(gate_loaded[u], 32 * (j + 1))
                pe.wait_ge(gate_ev[u], 5 * j + 1)
                for m in range(GH // 128):
                    cols = slice(m * 128, m * 128 + 128)
                    pe.matmul(psum[:, u, GATE, cols], M.gw1x[:, 0, cols], xT[:, u, 0, :], start=True, stop=False)
                    pe.matmul(psum[:, u, GATE, cols], M.gw1x[:, 1, cols], xT[:, u, 1, :], start=False, stop=False)
                    mm = pe.matmul(psum[:, u, GATE, cols], M.gw1s[:, cols], statT[:, u, :], start=False, stop=True)
                mm.then_inc(gate_mm[u], 1)

            def logits(j, u):
                pe.wait_ge(gate_ev[u], 5 * j + 2)
                for m in range(GH // 128):
                    mm = pe.matmul(psum[:, u, GATE, 0:H * NP], hid[:, u, m, :], M.gw2[:, m, :],
                                   start=(m == 0), stop=(m == GH // 128 - 1))
                mm.then_inc(gate_mm[u], 1)

            def mixedT(j, u):
                pe.wait_ge(gate_ev[u], 5 * j + 3)
                pe.wait_ge(ln_step[u], 3 * j + 1)
                for k in range(KD):
                    mm = pe.transpose(psum[:, u, GATE, k * 128:k * 128 + 128], mixed[:, u, k * 128:k * 128 + 128],
                                      M.ident[:, :])
                mm.then_inc(gate_mm[u], 1)

            def output(j, u):
                pe.wait_ge(gate_ev[u], 5 * j + 4)
                for k in range(KD):
                    mm = pe.matmul(psum[:, u, GATE, 0:D], mixT[:, u, k, :], M.wo[:, k, :], start=(k == 0), stop=(k == KD - 1))
                mm.then_inc(gate_mm[u], 1)

            solve = [product(0, inv, rhs), product(1, n32, x1s), product(2, inv, ys), product(3, n64, x2s),
                     product(4, inv, ys), product(5, n32, w1s), product(6, inv, ys), product(7, att, x2s)]
            p = solve
            overlapped_pairs(pe, B, (hidden, 0, 1), (p[1], 0, 0), (p[1], 1, 0), (hidden, 1, 1),
                             (logits, 0, 1), (p[2], 0, 0), (p[2], 1, 0), (logits, 1, 1),
                             *((q, u, 0) for q in p[3:] for u in range(2)), (scores, 0, -1), (scores, 1, -1),
                             (mixedT, 0, 1), (mixedT, 1, 1), (output, 0, 1), (output, 1, 1),
                             (p[0], 0, -1), (p[0], 1, -1), (statsT, 0, 0), (statsT, 1, 0))

        @block.scalar
        def _(act):
            def square_paths(j, u):
                act.wait_ge(stats_done[u], j)
                n = 2 * j + u
                act.activation(sq[:, u, 0:3, :], M.filtered[:, bass.ds(n, 1), :, :].rearrange("p b f c -> p (b f) c"), ACT.Square)
                act.activation(sq[:, u, 4, :], M.value[:, bass.ds(n, 1), :].rearrange("p b c -> p (b c)"), ACT.Square)

            def copy_product(i, out):
                def step(j, u):
                    act.wait_ge(solve_mm[u], 8 * j + i + 1)
                    act.activation(out[:, u, :], psum[:, u, SOLVE, 0:W], ACT.Copy).then_inc(solve_ev[u], 1)
                return step

            def square_delta(j, u):
                act.wait_ge(delta_done[u], j + 1)
                act.activation(sq[:, u, 3, :], delta[:, u, :], ACT.Square).then_inc(squared[u], 1)

            def copy_stats(j, u):
                act.wait_ge(gate_mm[u], 5 * j + 1)
                act.activation(statT[:, u, :], psum[0:80, u, GATE, 0:L], ACT.Copy).then_inc(gate_ev[u], 1)

            def gelu(j, u):
                act.wait_ge(gate_mm[u], 5 * j + 2)
                for m in range(GH // 128):
                    a = act.activation(hid[:, u, m, :], psum[:, u, GATE, m * L:m * L + L], ACT.Gelu, bias=M.gb1[:, m:m + 1])
                a.then_inc(gate_ev[u], 1)

            def exps(j, u):
                act.wait_ge(shifted[u], j + 1)
                act.activation(ex[:, u, :, :], lg[:, u, :, :], ACT.Exp).then_inc(exps_done[u], 1)

            def copy_mixed(j, u):
                act.wait_ge(gate_mm[u], 5 * j + 4)
                act.activation(mixT[:, u, :, :], psum[:, u, GATE, 0:D].rearrange("p (k t) -> p k t", t=L),
                               ACT.Copy).then_inc(gate_ev[u], 1)

            def square_mix(j, u):
                act.wait_ge(mix_summed[u], j + 1)
                act.activation(y[:, u, :], mixed[:, u, :], ACT.Square).then_inc(mix_squared[u], 1)

            first, fifth = copy_product(0, x1s), copy_product(4, w1s)
            overlapped_pairs(act, B, (square_paths, 0, 0), (gelu, 0, 1), (square_paths, 1, 0), (gelu, 1, 1),
                             (exps, 0, 1), (exps, 1, 1), (fifth, 0, 0), (fifth, 1, 0), (square_mix, 0, 1),
                             (square_delta, 0, 0), (square_mix, 1, 1), (square_delta, 1, 0), (copy_mixed, 0, 1),
                             (copy_mixed, 1, 1), (first, 0, -1), (first, 1, -1), (copy_stats, 0, 0), (copy_stats, 1, 0))

        @block.vector
        def _(dve):
            def banks(u, at):
                return psum[:, u, EVEN:ODD + 1, at:at + 2 * L].rearrange("p b (a t) -> p b a t", t=L)

            def by_bank(t, u):
                return t[:, u, :, :].rearrange("p (a b) t -> p b a t", b=2)

            def mask(m):
                return wide(wide(m[:, :], [128, 2, L], 1), [128, 2, 2, L], 1)

            def mask_scores(j, u):
                dve.wait_ge(scores_done[u], j + 1)
                dve.wait_ge(solve_mm[u], 8 * j)
                dve.tensor_tensor(by_bank(n32, u), banks(u, 0), mask(M.off32), ALU.mult)
                dve.tensor_tensor(by_bank(n64, u), banks(u, 0), mask(M.off64), ALU.mult)
                dve.tensor_tensor(by_bank(att, u), banks(u, 2 * L), mask(M.causal), ALU.mult).then_inc(masked[u], 1)

            def heads(ap):
                return ap.rearrange("p (h d) -> p h d", d=DV)

            def scale_product(i):
                def step(j, u):
                    n = 2 * j + u
                    dve.wait_ge(solve_mm[u], 8 * j + i + 1)
                    dve.tensor_tensor(heads(ys[:, u, :]), heads(psum[:, u, SOLVE, 0:W]),
                                      wide(M.decay[:, bass.ds(n, 1), :].rearrange("p b h -> p (b h)"), [128, H, DV], 2),
                                      ALU.mult).then_inc(solve_ev[u], 1)
                return step

            def join_pairs(j, u):
                dve.wait_ge(solve_mm[u], 8 * j + 3)
                dve.tensor_tensor(x2s[:, u, :], x1s[:, u, :], psum[:, u, SOLVE, 0:W], ALU.subtract).then_inc(solve_ev[u], 1)

            def less_w1(j, u):
                dve.wait_ge(solve_ev[u], 7 * j + 5)
                dve.tensor_tensor(x2s[:, u, :], x2s[:, u, :], w1s[:, u, :], ALU.subtract).then_inc(less_done[u], 1)

            def join_halves(j, u):
                dve.wait_ge(solve_mm[u], 8 * j + 7)
                dve.wait_ge(less_done[u], j + 1)
                dve.tensor_tensor(x2s[:, u, :], x2s[:, u, :], psum[:, u, SOLVE, 0:W], ALU.add).then_inc(solve_ev[u], 1)

            def scale_delta(j, u):
                n = 2 * j + u
                dve.wait_ge(solve_mm[u], 8 * j + 8)
                dve.wait_ge(mix_summed[u], j)
                dve.tensor_tensor(heads(delta[:, u, :]), heads(psum[:, u, SOLVE, 0:W]),
                                  wide(M.rq[:, bass.ds(n, 1), :].rearrange("p b h -> p (b h)"), [128, H, DV], 2),
                                  ALU.mult).then_inc(delta_done[u], 1)

            def path_sums(j, u):
                n = 2 * j + u
                fir = M.filtered[:, bass.ds(n, 1), :, :].rearrange("p b f (h d) -> p (b f h) d", d=DV)
                val = M.value[:, bass.ds(n, 1), :].rearrange("p b (h d) -> p (b h) d", d=DV)
                if not is_first(j):
                    dve.wait_ge(gate_mm[u], 5 * j - 4)
                for s, mag in ((0, False), (2, True)):
                    dve.tensor_reduce(stat[:, u, 0:12, s], fir, AX.X, ALU.add, apply_absolute_value=mag)
                    dve.tensor_reduce(stat[:, u, 16:20, s], val, AX.X, ALU.add, apply_absolute_value=mag)

            def delta_sums(j, u):
                dve.wait_ge(delta_done[u], j + 1)
                for s, mag in ((0, False), (2, True)):
                    dve.tensor_reduce(stat[:, u, 12:16, s], heads(delta[:, u, :]), AX.X, ALU.add, apply_absolute_value=mag)
                dve.wait_ge(squared[u], j + 1)
                dve.tensor_reduce(stat[:, u, :, 1], sq[:, u, :, :].rearrange("p f (h d) -> p (f h) d", d=DV),
                                  AX.X, ALU.add).then_inc(stats_done[u], 1)

            SM = 7

            def shift_logits(j, u):
                dve.wait_ge(gate_mm[u], 5 * j + 3)
                flat = lg[:, u, :, :].rearrange("p h f -> p (h f)")
                dve.tensor_tensor(flat, psum[:, u, GATE, 0:H * NP], M.gb2[:, :], ALU.add).then_inc(gate_ev[u], 1)
                dve.wait_ge(gate_ev[u], 5 * j + 3)
                dve.tensor_tensor(lg[:, u, :, :], lg[:, u, :, :], wide(M.inv_tau[:, :], [128, H, NP], 2),
                                  ALU.mult).then_inc(small[u], 1)
                dve.wait_ge(small[u], SM * j + 1)
                dve.tensor_reduce(hsum[:, u, 0, :], lg[:, u, :, :], AX.X, ALU.max).then_inc(small[u], 1)
                dve.wait_ge(small[u], SM * j + 2)
                dve.tensor_tensor(lg[:, u, :, :], lg[:, u, :, :], wide(hsum[:, u, 0, :], [128, H, NP], 2),
                                  ALU.subtract).then_inc(shifted[u], 1)

            def probabilities(j, u):
                dve.wait_ge(exps_done[u], j + 1)
                dve.tensor_reduce(hsum[:, u, 1, :], ex[:, u, :, :], AX.X, ALU.add).then_inc(small[u], 1)
                dve.wait_ge(small[u], SM * j + 3)
                dve.reciprocal(hsum[:, u, 2, :], hsum[:, u, 1, :]).then_inc(small[u], 1)
                dve.wait_ge(small[u], SM * j + 4)
                dve.tensor_tensor(hsum[:, u, 3, :], hsum[:, u, 2, :], M.keep[:, :], ALU.mult).then_inc(small[u], 1)
                dve.wait_ge(small[u], SM * j + 5)
                dve.tensor_tensor(ex[:, u, :, :], ex[:, u, :, :], wide(hsum[:, u, 3, :], [128, H, NP], 2),
                                  ALU.mult).then_inc(small[u], 1)
                dve.wait_ge(small[u], SM * j + 6)
                dve.tensor_tensor(ex[:, u, :, :], ex[:, u, :, :], M.floor[:, :, :], ALU.add).then_inc(probs_done[u], 1)

            def sum_paths(j, u):
                n = 2 * j + u
                dve.wait_ge(weighted[u], j + 1)
                dve.tensor_reduce(mixed[:, u, :], M.filtered[:, bass.ds(n, 1), :, :].rearrange("p b f c -> p (b c) f"),
                                  AX.X, ALU.add).then_inc(path_added[u], 1)
                dve.wait_ge(path_added[u], 2 * j + 1)
                dve.tensor_tensor(mixed[:, u, :], mixed[:, u, :], delta[:, u, :], ALU.add).then_inc(path_added[u], 1)
                dve.wait_ge(path_added[u], 2 * j + 2)
                dve.tensor_tensor(mixed[:, u, :], mixed[:, u, :], M.value[:, bass.ds(n, 1), :].rearrange("p b c -> p (b c)"),
                                  ALU.add).then_inc(mix_summed[u], 1)

            def mix_norm(j, u):
                dve.wait_ge(mix_squared[u], j + 1)
                dve.tensor_reduce(hsum[:, u, 0, :], heads(y[:, u, :]), AX.X, ALU.add).then_inc(small[u], 1)
                dve.wait_ge(small[u], SM * j + 7)
                dve.tensor_scalar(hsum[:, u, 1, :], hsum[:, u, 0, :], 1.0 / DV, 1e-5, ALU.mult,
                                  ALU.add).then_inc(power_asked[u], 1)

            def scale_mix(j, u):
                dve.wait_ge(power_done[u], 2 * j + 1)
                dve.tensor_tensor(heads(mixed[:, u, :]), heads(mixed[:, u, :]), wide(hsum[:, u, 2, :], [128, H, DV], 2),
                                  ALU.mult).then_inc(ln_step[u], 1)

            def residual(j, u):
                dve.wait_ge(gate_mm[u], 5 * j + 5)
                dve.tensor_tensor(y[:, u, :], psum[:, u, GATE, 0:D], x[:, u, :], ALU.add).then_inc(gate_ev[u], 1)
                dve.wait_ge(gate_ev[u], 5 * j + 5)
                dve.bn_stats(bn[:, u, :], y[:, u, :]).then_inc(ln_step[u], 1)
                dve.wait_ge(ln_step[u], 3 * j + 2)
                dve.memset(carrier[:, :], 0.0)
                dve.bn_aggr(mv[:, u, :], bn[:, u, :]).then_inc(ln_step[u], 1)
                dve.wait_ge(ln_step[u], 3 * j + 3)
                dve.tensor_scalar(mv[:, u, 1:2], mv[:, u, 1:2], 1e-5, None, ALU.add).then_inc(power_asked[u], 1)

            def normalize(j, u):
                n = 2 * j + u
                dve.wait_ge(power_done[u], 2 * j + 2)
                dve.tensor_scalar(M.value[:, bass.ds(n, 1), :].rearrange("p b c -> p (b c)"), y[:, u, :],
                                  mv[:, u, 0:1], bn[:, u, 0:1], ALU.subtract, ALU.mult).then_inc(x1_done[u], 1)

            y1, y3, y5 = scale_product(1), scale_product(3), scale_product(5)
            overlapped_pairs(dve, B, (path_sums, 0, 0), (y1, 0, 0), (y1, 1, 0), (path_sums, 1, 0),
                             (join_pairs, 0, 0), (shift_logits, 0, 1), (join_pairs, 1, 0),
                             (shift_logits, 1, 1), (y3, 0, 0), (y3, 1, 0), (probabilities, 0, 1),
                             (less_w1, 0, 0), (less_w1, 1, 0), (y5, 0, 0), (y5, 1, 0), (probabilities, 1, 1),
                             (join_halves, 0, 0), (join_halves, 1, 0), (sum_paths, 0, 1),
                             (scale_delta, 0, 0), (mix_norm, 0, 1), (sum_paths, 1, 1), (scale_delta, 1, 0),
                             (delta_sums, 0, 0), (scale_mix, 0, 1), (mix_norm, 1, 1), (delta_sums, 1, 0),
                             (mask_scores, 0, -1), (scale_mix, 1, 1), (mask_scores, 1, -1),
                             (residual, 0, 1), (residual, 1, 1), (normalize, 0, 1), (normalize, 1, 1))

        @block.gpsimd
        def _(pool):
            def expand(j, u):
                n = 2 * j + u
                pool.wait_ge(loaded[u], 48 * (j + 1))
                pool.wait_ge(solve_mm[u], 8 * j)
                pool.tensor_tensor(inv[:, u, :, :].rearrange("p h (c i) -> p h c i", i=CB),
                                   wide(invp[:, u, :, :], [128, H, NC, CB], 2),
                                   wide(M.blockdiag[:, :].rearrange("p (c i) -> p c i", i=CB), [128, H, NC, CB], 1),
                                   ALU.mult)
                pool.tensor_tensor(rhs[:, u, :].rearrange("p (h d) -> p h d", d=DV),
                                   M.value[:, bass.ds(n, 1), :].rearrange("p b (h d) -> p (b h) d", d=DV),
                                   wide(M.beta_r[:, bass.ds(n, 1), :].rearrange("p b h -> p (b h)"), [128, H, DV], 2),
                                   ALU.mult).then_inc(expanded[u], 1)

            def norms(j, u):
                pool.wait_ge(stats_done[u], j + 1)
                pool.tensor_tensor(stat[:, u, :, 3], stat[:, u, :, 1],
                                   M.plus_half[:, 0:1].broadcast_to([128, NP * H]), ALU.pow).then_inc(norms_done[u], 1)

            def weight(j, u):
                n = 2 * j + u
                pool.wait_ge(probs_done[u], j + 1)

                def prob(f0, nf):
                    return wide(ex[:, u, :, f0:f0 + nf].rearrange("p h f -> p f h"), [128, nf, H, DV], 3)

                def split(ap):
                    return ap.rearrange("p f (h d) -> p f h d", d=DV)

                for paths, f0, nf in ((split(delta[:, u:u + 1, :]), 3, 1),
                                      (M.filtered[:, bass.ds(n, 1), :, :].rearrange("p b f (h d) -> p (b f) h d", d=DV), 0, 3),
                                      (split(M.value[:, bass.ds(n, 1), :]), 4, 1)):
                    ins = pool.tensor_tensor(paths, paths, prob(f0, nf), ALU.mult)
                ins.then_inc(weighted[u], 1)

            def mix_power(j, u):
                pool.wait_ge(power_asked[u], 2 * j + 1)
                pool.tensor_tensor(hsum[:, u, 2, :], hsum[:, u, 1, :], M.minus_half[:, 0:1].broadcast_to([128, H]),
                                   ALU.pow).then_inc(power_done[u], 1)

            def ln_power(j, u):
                pool.wait_ge(power_asked[u], 2 * j + 2)
                pool.tensor_tensor(bn[:, u, 0:1], mv[:, u, 1:2], M.minus_half[:, 0:1], ALU.pow).then_inc(power_done[u], 1)

            overlapped_pairs(pool, B, (weight, 0, 1), (weight, 1, 1), (mix_power, 0, 1), (expand, 0, -1),
                             (mix_power, 1, 1), (norms, 0, 0), (expand, 1, -1), (ln_power, 0, 1), (norms, 1, 0),
                             (ln_power, 1, 1))


def load_experts(nc, M):
    with signals(nc) as signal, ExitStack() as ctx:
        weights_in = signal("expert_weights_in")
        block = ctx.enter_context(nc.Block())

        @block.sync
        def _(sp):
            full = EH // 128 * 128
            for w, routed, shared in ((M.wg, M.wg_dram, M.wg_s_dram), (M.wu, M.wu_dram, M.wu_s_dram)):
                for e in range(NE + 1):
                    src = routed[e] if e < NE else shared
                    sp.dma_start(w[:, e, :, :], src.rearrange("(k p) n -> p k n", p=128)).then_inc(weights_in, 16)
            for e in range(NE + 1):
                src = M.wd_dram[e] if e < NE else M.wd_s_dram
                sp.dma_start(M.wd[:, e, 0:full // 128, :], src[0:full, :].rearrange("(k p) n -> p k n", p=128)
                             ).then_inc(weights_in, 16)
                sp.dma_start(M.wd[0:EH - full, e, full // 128, :], src[full:EH, :]).then_inc(weights_in, 16)
            sp.wait_ge(weights_in, 16 * 4 * (NE + 1))


def attend(nc, M):
    SCALE = 1.0 / math.sqrt(XD)
    NK = CTX // 128
    with signals(nc) as signal, ExitStack() as ctx:
        def sb(name, shape):
            return ctx.enter_context(nc.sbuf_tensor(name, shape, fp32))

        def pair(name):
            return [signal(f"{name}{u}") for u in range(2)]

        w_src = sb("w_src", [128, NK, 2 * D])
        w_tgt = sb("w_tgt", [128, KD, D])
        w_out = sb("w_out", [128, 2 * KD, D])
        w_router = sb("w_router", [128, KD, NE])
        b_key = sb("b_key", [128, KD])
        b_tgt = sb("b_tgt", [128, KD])
        b_val = sb("b_val", [128, D])
        b_out = sb("b_out", [128, D])
        cT = sb("ctxT_tile", [128, 2, NK, L])
        mrow = sb("mask_row", [128, 2, L])
        mcol = sb("mask_col", [128, 2, 1])
        shut = sb("mask_shut", [128, 2, L])
        x1 = sb("x1_tile", [128, 2, D])
        x1b = sb("x1_plus_bias", [128, 2, D])
        x1T = sb("x1T_tile", [128, 2, KD, L])
        keyT = sb("keyT", [128, 2, KD, L])
        qryT = sb("queryT", [128, 2, KD, L])
        vraw = sb("value_raw", [128, 2, D])
        val = sb("value_ones", [128, 2, XH, XD + 1])
        sc = sb("scores", [128, 2, XH, L])
        scT = sb("scoresT", [128, 2, XH, L])
        mx = sb("score_max", [128, 2, XH])
        den = sb("softmax_den", [128, 2, XH])
        upd = sb("update", [128, 2, D])
        updT = sb("updateT", [128, 2, KD, L])
        y = sb("residual2", [128, 2, D])
        x2 = sb("x2_tile", [128, 2, D])
        x2T = sb("x2T_tile", [128, 2, KD, L])
        bn = sb("ln_stats2", [128, 2, 6])
        mv = sb("ln_mean_var2", [128, 2, 2])
        carrier = sb("carrier2", [128, 1])
        spsum = ctx.enter_context(nc.psum_tensor("score_psum", [128, 4, 512], fp32))
        psum = ctx.enter_context(nc.psum_tensor("attend_psum", [128, 2, 2, 512], fp32))
        FRONT, BACK = 0, 1

        weights_in = signal("attend_weights_in")
        ones_set = signal("ones_set")
        loaded = pair("ctx_loaded")
        x1_copied = pair("x1_copied")
        x1_biased = pair("x1_biased")
        front_mm = pair("front_mm")
        front_ev = pair("front_ev")
        queries_kept = pair("queries_kept")
        back_mm = pair("back_mm")
        back_ev = pair("back_ev")
        mask_made = pair("mask_made")
        val_done = pair("val_done")
        scores_mm = pair("scores_mm")
        scores_ev = pair("scores_ev")
        max_done = pair("max_done")
        shifted = pair("scores_shifted")
        exp_done = pair("exp_done")
        den_done = pair("den_done")
        ln_step = pair("ln2_step")
        power_asked = pair("ln2_power_asked")
        power_done = pair("ln2_power_done")
        x2_done = pair("x2_done")
        x2_kept = pair("x2_kept")
        x2_stored = pair("x2_stored")
        logits_kept = pair("logits_kept")
        block = ctx.enter_context(nc.Block())
        NF, NB = 3, 7

        @block.sync
        def _(sp):
            def part(w, k):
                return w.rearrange("(k p) n -> p k n", k=k)
            for dst, src in ((w_src, part(M.w_srcT_dram, NK)), (w_tgt, part(M.w_tgtT_dram, KD)),
                             (w_out, part(M.w_outT_dram, 2 * KD)), (w_router, part(M.w_routerT_dram, KD))):
                sp.dma_start(dst[:, :, :], src).then_inc(weights_in, 16)
            sp.dma_start(b_key[:, :], M.b_key_dram).then_inc(weights_in, 16)
            sp.dma_start(b_tgt[:, :], M.b_tgt_dram).then_inc(weights_in, 16)
            sp.dma_start(b_val[:, :], M.b_src_dram[D:2 * D].partition_broadcast(128)).then_inc(weights_in, 16)
            sp.dma_start(b_out[:, :], M.b_out_dram.partition_broadcast(128)).then_inc(weights_in, 16)

            def load(j, u):
                n = 2 * j + u
                if not is_first(j):
                    sp.wait_ge(front_mm[u], NF * j - 1)
                sp.wait_ge(queries_kept[u], j)
                sp.wait_ge(mask_made[u], j)
                sp.wait_ge(val_done[u], j)
                sp.dma_start(mcol[:, u, :], M.mask_col_dram[bass.ds(n * L, L), :]).then_inc(loaded[u], 16)
                sp.dma_start(mrow[:, u, :], M.mask_dram[bass.ds(n, 1), :].rearrange("b t -> (b t)").partition_broadcast(128)
                             ).then_inc(loaded[u], 16)
                sp.dma_start(cT[:, u, :, :], M.ctxT_dram[:, bass.ds(n * L, L)].rearrange("(k p) n -> p k n", p=128)
                             ).then_inc(loaded[u], 16)

            def store(j, u):
                n = 2 * j + u
                sp.wait_ge(x2_done[u], j + 1)
                sp.dma_start(M.rows_dram[bass.ds(n * L, L), :], x2[:, u, :]).then_inc(x2_stored[u], 16)

            overlapped_pairs(sp, B, (load, 0, -1), (load, 1, -1), (store, 0, 1), (store, 1, 1))
            for u in range(2):
                sp.wait_ge(x2_stored[u], 16 * (B // 2))

        @block.tensor
        def _(pe):
            pe.wait_ge(weights_in, 8 * 16)

            def keys(j, u):
                pe.wait_ge(loaded[u], 48 * (j + 1))
                pe.wait_ge(x1_copied[u], j + 1)
                pe.wait_ge(front_ev[u], NF * j)
                for m in range(KD):
                    for k in range(NK):
                        pe.matmul(psum[:, u, FRONT, m * L:m * L + L], w_src[:, k, m * 128:m * 128 + 128], cT[:, u, k, :],
                                  start=(k == 0), stop=(k == NK - 1))
                for k in range(KD):
                    mm = pe.transpose(psum[:, u, FRONT, (KD + k) * L:(KD + k) * L + L], x1[:, u, k * 128:k * 128 + 128],
                                      M.ident[:, :])
                mm.then_inc(front_mm[u], 1)

            def queries(j, u):
                pe.wait_ge(front_ev[u], NF * j + 1)
                for k in range(NK):
                    pe.matmul(psum[:, u, FRONT, D:2 * D], cT[:, u, k, :], w_src[:, k, D:2 * D], start=(k == 0),
                              stop=(k == NK - 1))
                for m in range(KD):
                    for k in range(KD):
                        mm = pe.matmul(psum[:, u, FRONT, m * L:m * L + L], w_tgt[:, k, m * 128:m * 128 + 128],
                                       x1T[:, u, k, :], start=(k == 0), stop=(k == KD - 1))
                mm.then_inc(front_mm[u], 1)

            def output_x1(j, u):
                pe.wait_ge(front_ev[u], NF * j + 2)
                for k in range(KD):
                    mm = pe.matmul(psum[:, u, FRONT, 0:D], x1T[:, u, k, :], w_out[:, k, :], start=(k == 0), stop=(k == KD - 1))
                mm.then_inc(front_mm[u], 1)

            def scores(j, u):
                pe.wait_ge(queries_kept[u], j + 1)
                pe.wait_ge(scores_ev[1 - u], j + u)
                for h in range(XH):
                    rows = slice((h % 4) * XD, (h % 4) * XD + XD)
                    at = (h // 4) * 2 * L
                    mm = pe.matmul(spsum[:, h % 4, at:at + L], qryT[rows, u, h // 4, :],
                                   keyT[rows, u, h // 4, :], start=True, stop=True)
                mm.then_inc(scores_mm[u], 1)

            def turn_probs(half):
                def step(j, u):
                    pe.wait_ge(exp_done[u], j + 1)
                    pe.wait_ge(back_ev[u], NB * j + half)
                    for i in range(4):
                        mm = pe.transpose(psum[:, u, BACK, i * L:i * L + L], sc[:, u, 4 * half + i, :], M.ident[:, :])
                    mm.then_inc(back_mm[u], 1)
                return step

            def average(j, u):
                pe.wait_ge(back_ev[u], NB * j + 2)
                for h in range(XH):
                    i = 2 * (h % 4) + h // 4
                    mm = pe.matmul(psum[:, u, BACK, h * (XD + 1):(h + 1) * (XD + 1)], scT[:, u, i, :], val[:, u, h, :],
                                   start=True, stop=True)
                mm.then_inc(back_mm[u], 1)

            def turn_update(j, u):
                pe.wait_ge(back_ev[u], NB * j + 3)
                for k in range(KD):
                    mm = pe.transpose(psum[:, u, BACK, k * L:k * L + L], upd[:, u, k * 128:k * 128 + 128], M.ident[:, :])
                mm.then_inc(back_mm[u], 1)

            def output(j, u):
                pe.wait_ge(back_ev[u], NB * j + 4)
                for k in range(KD):
                    mm = pe.matmul(psum[:, u, BACK, 0:D], updT[:, u, k, :], w_out[:, KD + k, :], start=(k == 0),
                                   stop=(k == KD - 1))
                mm.then_inc(back_mm[u], 1)

            def turn_x2(j, u):
                pe.wait_ge(back_ev[u], NB * j + 5)
                pe.wait_ge(x2_done[u], j + 1)
                for k in range(KD):
                    mm = pe.transpose(psum[:, u, BACK, k * L:k * L + L], x2[:, u, k * 128:k * 128 + 128], M.ident[:, :])
                mm.then_inc(back_mm[u], 1)

            def router(j, u):
                pe.wait_ge(back_ev[u], NB * j + 6)
                for k in range(KD):
                    mm = pe.matmul(psum[:, u, BACK, 0:NE], x2T[:, u, k, :], w_router[:, k, :], start=(k == 0), stop=(k == KD - 1))
                mm.then_inc(back_mm[u], 1)

            low, high = turn_probs(0), turn_probs(1)
            overlapped_pairs(pe, B, (turn_x2, 0, 2), (turn_x2, 1, 2), (keys, 0, 0), (router, 0, 2), (router, 1, 2),
                             (low, 0, 1), (keys, 1, 0), (low, 1, 1), (high, 0, 1), (high, 1, 1),
                             (queries, 0, 0), (average, 0, 1), (average, 1, 1), (turn_update, 0, 1), (queries, 1, 0),
                             (turn_update, 1, 1), (output, 0, 1), (scores, 0, 0), (output, 1, 1), (output_x1, 0, 0),
                             (scores, 1, 0), (output_x1, 1, 0))

        @block.scalar
        def _(act):
            def copy_x1(j, u):
                n = 2 * j + u
                if not is_first(j):
                    act.wait_ge(front_mm[u], NF * j - 2)
                act.wait_ge(x1_biased[u], j)
                act.activation(x1[:, u, :], M.value[:, bass.ds(n, 1), :].rearrange("p b c -> p (b c)"), ACT.Copy
                               ).then_inc(x1_copied[u], 1)

            def mask_values(j, u):
                act.wait_ge(front_ev[u], NF * j + 2)
                if not is_first(j):
                    act.wait_ge(back_mm[u], NB * j - 4)
                act.activation(val[:, u, :, 0:XD], vraw[:, u, :].rearrange("p (h d) -> p h d", d=XD), ACT.Copy,
                               scale=mcol[:, u, :]).then_inc(val_done[u], 1)

            def exps(j, u):
                act.wait_ge(shifted[u], j + 1)
                act.activation(sc[:, u, :, :], sc[:, u, :, :], ACT.Exp).then_inc(exp_done[u], 1)

            def copy_probs(j, u):
                act.wait_ge(back_mm[u], NB * j + 1)
                act.activation(scT[:, u, 0:4, :], psum[:, u, BACK, :].rearrange("p (i t) -> p i t", t=L), ACT.Copy
                               ).then_inc(back_ev[u], 1)

            def copy_update(j, u):
                act.wait_ge(back_mm[u], NB * j + 4)
                act.activation(updT[:, u, :, :], psum[:, u, BACK, 0:D].rearrange("p (k t) -> p k t", t=L), ACT.Copy
                               ).then_inc(back_ev[u], 1)

            def copy_x2(j, u):
                n = 2 * j + u
                act.wait_ge(back_mm[u], NB * j + 6)
                act.activation(x2T[:, u, :, :], psum[:, u, BACK, 0:D].rearrange("p (k t) -> p k t", t=L), ACT.Copy
                               ).then_inc(back_ev[u], 1)
                act.activation(M.value[:, bass.ds(n, 1), :].rearrange("p b c -> p (b c)"), x2[:, u, :], ACT.Copy
                               ).then_inc(x2_kept[u], 1)

            act.wait_ge(ones_set, 1)
            overlapped_pairs(act, B, (copy_x2, 0, 2), (copy_x2, 1, 2), (exps, 1, 1), (copy_probs, 0, 1), (copy_probs, 1, 1),
                             (mask_values, 0, 0), (copy_update, 0, 1), (copy_x1, 0, -1), (mask_values, 1, 0),
                             (copy_update, 1, 1), (copy_x1, 1, -1), (exps, 0, 0))

        @block.vector
        def _(dve):
            dve.memset(val[:, :, :, XD:XD + 1], 1.0).then_inc(ones_set, 1)
            dve.wait_ge(weights_in, 8 * 16)
            def masks(j, u):
                dve.wait_ge(loaded[u], 48 * (j + 1))
                dve.tensor_scalar(shut[:, u, :], mrow[:, u, :], 0.0, -1e30, ALU.is_equal, ALU.mult).then_inc(mask_made[u], 1)

            def keep_keys(j, u):
                dve.wait_ge(front_mm[u], NF * j + 1)
                dve.wait_ge(scores_mm[u], j)
                for m in range(KD):
                    dve.scalar_tensor_tensor(out=keyT[:, u, m, :], in0=psum[:, u, FRONT, m * L:m * L + L],
                                             scalar=b_key[:, m:m + 1], in1=mrow[:, u, :], op0=ALU.add, op1=ALU.mult)
                dve.tensor_copy(x1T[:, u, :, :], psum[:, u, FRONT, KD * L:2 * KD * L].rearrange("p (k t) -> p k t", t=L)
                                ).then_inc(front_ev[u], 1)

            def keep_queries(j, u):
                dve.wait_ge(front_mm[u], NF * j + 2)
                dve.wait_ge(val_done[u], j)
                for m in range(KD):
                    ins = dve.scalar_tensor_tensor(out=qryT[:, u, m, :], in0=psum[:, u, FRONT, m * L:m * L + L],
                                                   scalar=b_tgt[:, m:m + 1], in1=mrow[:, u, :], op0=ALU.add, op1=ALU.mult)
                ins.then_inc(queries_kept[u], 1)
                dve.tensor_tensor(vraw[:, u, :], psum[:, u, FRONT, D:2 * D], b_val[:, :], ALU.add).then_inc(front_ev[u], 1)

            def keep_residual(j, u):
                n = 2 * j + u
                dve.wait_ge(front_mm[u], NF * j + 3)
                dve.wait_ge(x1_biased[u], j + 1)
                dve.tensor_tensor(M.value[:, bass.ds(n, 1), :].rearrange("p b c -> p (b c)"), psum[:, u, FRONT, 0:D],
                                  x1b[:, u, :], ALU.add).then_inc(front_ev[u], 1)

            def scale_scores(j, u):
                dve.wait_ge(scores_mm[u], j + 1)
                dve.wait_ge(mask_made[u], j + 1)
                if not is_first(j):
                    dve.wait_ge(back_mm[u], NB * j - 5)
                dve.scalar_tensor_tensor(out=sc[:, u, :, :],
                                         in0=spsum[:, :, :].rearrange("p b (a t) -> p (b a) t", t=2 * L)[:, :, 0:L],
                                         scalar=SCALE, in1=wide(shut[:, u, :], [128, XH, L], 1),
                                         op0=ALU.mult, op1=ALU.add).then_inc(scores_ev[u], 1)
                dve.wait_ge(scores_ev[u], j + 1)
                dve.tensor_reduce(mx[:, u, :], sc[:, u, :, :], AX.X, ALU.max).then_inc(max_done[u], 1)

            def copy_probs(j, u):
                dve.wait_ge(back_mm[u], NB * j + 2)
                dve.tensor_copy(scT[:, u, 4:8, :], psum[:, u, BACK, :].rearrange("p (i t) -> p i t", t=L)).then_inc(back_ev[u], 1)

            def divide(j, u):
                dve.wait_ge(back_mm[u], NB * j + 3)
                av = psum[:, u, BACK, 0:XH * (XD + 1)].rearrange("p (h d) -> p h d", d=XD + 1)
                dve.reciprocal(den[:, u, :], av[:, :, XD]).then_inc(den_done[u], 1)
                dve.wait_ge(den_done[u], j + 1)
                dve.tensor_tensor(upd[:, u, :].rearrange("p (h d) -> p h d", d=XD), av[:, :, 0:XD],
                                  wide(den[:, u, :], [128, XH, XD], 2), ALU.mult).then_inc(back_ev[u], 1)

            def residual(j, u):
                n = 2 * j + u
                dve.wait_ge(back_mm[u], NB * j + 5)
                dve.tensor_tensor(y[:, u, :], psum[:, u, BACK, 0:D], M.value[:, bass.ds(n, 1), :].rearrange("p b c -> p (b c)"),
                                  ALU.add).then_inc(back_ev[u], 1)
                dve.wait_ge(back_ev[u], NB * j + 5)
                dve.bn_stats(bn[:, u, :], y[:, u, :]).then_inc(ln_step[u], 1)
                dve.wait_ge(ln_step[u], 2 * j + 1)
                dve.memset(carrier[:, :], 0.0)
                dve.bn_aggr(mv[:, u, :], bn[:, u, :]).then_inc(ln_step[u], 1)
                dve.wait_ge(ln_step[u], 2 * j + 2)
                dve.tensor_scalar(mv[:, u, 1:2], mv[:, u, 1:2], 1e-5, None, ALU.add).then_inc(power_asked[u], 1)

            def normalize(j, u):
                dve.wait_ge(power_done[u], j + 1)
                dve.wait_ge(x2_stored[u], 16 * j)
                dve.wait_ge(x2_kept[u], j)
                dve.tensor_scalar(x2[:, u, :], y[:, u, :], mv[:, u, 0:1], bn[:, u, 0:1], ALU.subtract,
                                  ALU.mult).then_inc(x2_done[u], 1)

            def keep_logits(j, u):
                n = 2 * j + u
                dve.wait_ge(back_mm[u], NB * j + 7)
                dve.tensor_copy(M.logits[:, bass.ds(n, 1), :].rearrange("p b e -> p (b e)"), psum[:, u, BACK, 0:NE]
                                ).then_inc(back_ev[u], 1)

            overlapped_pairs(dve, B, (keep_keys, 0, 0), (keep_logits, 0, 2), (keep_logits, 1, 2), (copy_probs, 0, 1),
                             (keep_keys, 1, 0), (copy_probs, 1, 1), (keep_queries, 0, 0),
                             (divide, 0, 1), (divide, 1, 1), (keep_queries, 1, 0), (residual, 0, 1),
                             (scale_scores, 0, 0), (residual, 1, 1), (keep_residual, 0, 0), (normalize, 0, 1),
                             (normalize, 1, 1), (scale_scores, 1, 0), (keep_residual, 1, 0), (masks, 0, -1), (masks, 1, -1))

        @block.gpsimd
        def _(pool):
            pool.wait_ge(weights_in, 8 * 16)

            def bias_x1(j, u):
                pool.wait_ge(x1_copied[u], j + 1)
                pool.wait_ge(front_ev[u], NF * j)
                pool.tensor_tensor(x1b[:, u, :], x1[:, u, :], b_out[:, :], ALU.add).then_inc(x1_biased[u], 1)

            def shift(j, u):
                pool.wait_ge(max_done[u], j + 1)
                pool.tensor_tensor(sc[:, u, :, :], sc[:, u, :, :], wide(mx[:, u, :], [128, XH, L], 2),
                                   ALU.subtract).then_inc(shifted[u], 1)

            def power(j, u):
                pool.wait_ge(power_asked[u], j + 1)
                pool.tensor_tensor(bn[:, u, 0:1], mv[:, u, 1:2], M.minus_half[:, 0:1], ALU.pow).then_inc(power_done[u], 1)

            overlapped_pairs(pool, B, (power, 0, 1), (shift, 0, 0), (power, 1, 1), (shift, 1, 0),
                             (bias_x1, 0, -1), (bias_x1, 1, -1))


def route(nc, M):
    with signals(nc) as signal, ExitStack() as ctx:
        def sb(name, shape, dt=fp32):
            return ctx.enter_context(nc.sbuf_tensor(name, shape, dt))

        ones = sb("ones", [128, 128])
        before = sb("before", [128, 128])
        rank8 = sb("rank8", [128, NE])
        slots = sb("slots", [128, SLOT_TILES])
        zero_row = sb("zero_row", [128, 8 * D])
        l2 = sb("logits_less_top", [128, B, NE])
        exps = sb("router_exps", [128, B, NE])
        diff = sb("router_diff", [128, B, NE])
        tie = sb("tie", [128, B, NE])
        hot = [sb(f"hot{i}", [128, B, NE]) for i in range(2)]
        both = sb("hot_both", [128, B, NE])
        top = sb("top", [128, 2, B])
        tmax = sb("tie_max", [128, B])
        d2 = sb("top_diff", [128, B])
        pr = sb("top_probs", [128, 2, B])
        rsum = sb("router_rsum", [128, B])
        scan = [sb(f"scan{i}", [128, B, NE]) for i in range(2)]
        base = sb("base", [128, B, NE])
        cnt = sb("counts", [128, NE])
        cnti = sb("counts_int", [128, NE], mybir.dt.int32)
        ends = [sb(f"ends{i}", [128, NE]) for i in range(2)]
        nt = sb("tiles_of", [128, NE])
        posf = sb("posf", [128, B])
        past = sb("past", [128, SLOT_TILES, NE])
        ef = sb("expert_f", [128, SLOT_TILES])
        prefix = ctx.enter_context(nc.psum_tensor("prefix_psum", [128, 512], fp32))
        totals = ctx.enter_context(nc.psum_tensor("totals_psum", [128, 512], fp32))
        made = signal("route_constants")
        zero_set = signal("zero_set")
        dve_step = signal("route_step")
        asked = signal("router_exps_asked")
        answered = signal("router_exps_done")
        both_done = signal("both_done")
        counted = signal("counted")
        placed = signal("placed")
        scattered = signal("scattered")
        cleared = signal("cleared")
        block = ctx.enter_context(nc.Block())

        @block.sync
        def _(sp):
            sp.wait_ge(zero_set, 1)
            for i in range(SLOT_TILES // 8):
                r0 = B * L + i * 8 * L
                sp.dma_start(M.rows_dram[r0:r0 + 8 * L, :].rearrange("(p a) c -> p (a c)", a=8), zero_row[:, :]
                             ).then_inc(cleared, 16)

        @block.tensor
        def _(pe):
            pe.wait_ge(made, 4)
            pe.wait_ge(both_done, 1)
            flat = both[:, :, :].rearrange("p b e -> p (b e)")
            pe.matmul(prefix[:, 0:B * NE], before[:, :], flat, start=True, stop=True)
            pe.matmul(totals[:, 0:B * NE], ones[:, :], flat, start=True, stop=True).then_inc(counted, 1)

        @block.vector
        def _(dve):
            steps = [0]

            def link(ins):
                steps[0] += 1
                ins.then_inc(dve_step, 1)
                dve.wait_ge(dve_step, steps[0])

            def eights(ap):
                return wide(ap, [128, B, NE], 2)

            dve.memset(zero_row[:, :], 0.0).then_inc(zero_set, 1)
            dve.wait_ge(made, 4)
            lg = M.logits[:, :, :]
            for i in range(2):
                src = lg if i == 0 else l2[:, :, :]
                link(dve.tensor_reduce(top[:, i, :], src, AX.X, ALU.max))
                link(dve.tensor_tensor(tie[:, :, :], src, eights(top[:, i, :]), ALU.is_equal))
                link(dve.tensor_tensor(tie[:, :, :], tie[:, :, :], wide(rank8[:, :], [128, B, NE], 1), ALU.mult))
                link(dve.tensor_reduce(tmax[:, :], tie[:, :, :], AX.X, ALU.max))
                link(dve.tensor_tensor(hot[i][:, :, :], tie[:, :, :], eights(tmax[:, :]), ALU.is_equal))
                if i == 0:
                    link(dve.scalar_tensor_tensor(out=l2[:, :, :], in0=hot[0][:, :, :], scalar=-1e30, in1=lg,
                                                  op0=ALU.mult, op1=ALU.add))
            link(dve.tensor_tensor(diff[:, :, :], lg, eights(top[:, 0, :]), ALU.subtract))
            dve.tensor_tensor(d2[:, :], top[:, 1, :], top[:, 0, :], ALU.subtract).then_inc(asked, 1)
            dve.tensor_tensor(both[:, :, :], hot[0][:, :, :], hot[1][:, :, :], ALU.add).then_inc(both_done, 1)
            dve.wait_ge(answered, 2)
            link(dve.tensor_reduce(rsum[:, :], exps[:, :, :], AX.X, ALU.add))
            link(dve.reciprocal(pr[:, 0, :], rsum[:, :]))
            link(dve.tensor_tensor(pr[:, 1, :], pr[:, 1, :], pr[:, 0, :], ALU.mult))
            link(dve.tensor_tensor(rsum[:, :], pr[:, 0, :], pr[:, 1, :], ALU.add))
            link(dve.tensor_scalar(rsum[:, :], rsum[:, :], 1e-20, None, ALU.add))
            link(dve.reciprocal(rsum[:, :], rsum[:, :]))
            for i in range(2):
                link(dve.tensor_tensor(M.weight[:, :, i], pr[:, i, :], rsum[:, :], ALU.mult))
            dve.wait_ge(counted, 1)
            tot = totals[:, 0:B * NE].rearrange("p (b e) -> p b e", e=NE)
            link(dve.tensor_copy(scan[0][:, :, :], tot))
            now, s = 0, 1
            while s < B:
                a, c = scan[now], scan[1 - now]
                link(dve.tensor_copy(c[:, 0:s, :], a[:, 0:s, :]))
                link(dve.tensor_tensor(c[:, s:B, :], a[:, s:B, :], a[:, 0:B - s, :], ALU.add))
                now, s = 1 - now, 2 * s
            incl = scan[now]
            link(dve.tensor_tensor(base[:, :, :], incl[:, :, :], tot, ALU.subtract))
            link(dve.tensor_tensor(base[:, :, :], base[:, :, :], prefix[:, 0:B * NE].rearrange("p (b e) -> p b e", e=NE), ALU.add))
            link(dve.tensor_scalar(cnt[:, :], incl[:, B - 1, :], float(L - 1), None, ALU.add))
            link(dve.tensor_copy(cnti[:, :], cnt[:, :]))
            link(dve.tensor_scalar(cnti[:, :], cnti[:, :], 7, None, ALU.arith_shift_right))
            link(dve.tensor_copy(nt[:, :], cnti[:, :]))
            link(dve.tensor_copy(ends[0][:, :], nt[:, :]))
            now, s = 0, 1
            while s < NE:
                a, c = ends[now], ends[1 - now]
                link(dve.tensor_copy(c[:, 0:s], a[:, 0:s]))
                link(dve.tensor_tensor(c[:, s:NE], a[:, s:NE], a[:, 0:NE - s], ALU.add))
                now, s = 1 - now, 2 * s
            end = ends[now]
            link(dve.tensor_tensor(cnt[:, :], end[:, :], nt[:, :], ALU.subtract))
            link(dve.tensor_scalar(cnt[:, :], cnt[:, :], float(L), float(B * L), ALU.mult, ALU.add))
            link(dve.tensor_tensor(base[:, :, :], base[:, :, :], wide(cnt[:, :], [128, B, NE], 1), ALU.add))
            for i in range(2):
                link(dve.tensor_tensor(tie[:, :, :], hot[i][:, :, :], base[:, :, :], ALU.mult))
                link(dve.tensor_reduce(posf[:, :], tie[:, :, :], AX.X, ALU.add))
                link(dve.tensor_copy(M.place[:, i, :], posf[:, :]))
            link(dve.tensor_tensor(past[:, :, :], wide(slots[:, :], [128, SLOT_TILES, NE], 2),
                                   wide(end[:, :], [128, SLOT_TILES, NE], 1), ALU.is_ge))
            link(dve.tensor_reduce(ef[:, :], past[:, :, :], AX.X, ALU.add))
            link(dve.tensor_scalar(ef[:, :], ef[:, :], float(NE - 1), None, ALU.min))
            link(dve.memset(M.expert_of[:, 0:B], NE))
            dve.tensor_copy(M.expert_of[:, B:UNITS], ef[:, :]).then_inc(placed, 1)

        @block.gpsimd
        def _(pool):
            pool.memset(ones[:, :], 1.0).then_inc(made, 1)
            pool.memset(before[:, :], 1.0).then_inc(made, 1)
            pool.iota(rank8[:, :], pattern=[[-1, NE]], base=NE, channel_multiplier=0,
                      allow_small_or_imprecise_dtypes=True)
            pool.iota(slots[:, :], pattern=[[1, SLOT_TILES]], base=0, channel_multiplier=0,
                      allow_small_or_imprecise_dtypes=True).then_inc(made, 1)
            pool.wait_ge(made, 3)
            pool.affine_select(out=before[:, :], in_=before[:, :], compare_op=ALU.is_gt, fill=0.0,
                               base=0, pattern=[[1, 128]], channel_multiplier=-1).then_inc(made, 1)
            pool.wait_ge(asked, 1)
            pool.tensor_tensor(exps[:, :, :].rearrange("p b e -> p (b e)"), M.euler[:, 0:1].broadcast_to([128, B * NE]),
                               diff[:, :, :].rearrange("p b e -> p (b e)"), ALU.pow).then_inc(answered, 1)
            pool.tensor_tensor(pr[:, 1, :], M.euler[:, 0:1].broadcast_to([128, B]), d2[:, :], ALU.pow).then_inc(answered, 1)
            pool.wait_ge(placed, 1)
            pool.wait_ge(cleared, 16 * (SLOT_TILES // 8))
            for b in range(B):
                for i in range(2):
                    pool.indirect_dma_start(out=M.rows_dram[:, :],
                                            out_offset=bass.IndirectOffsetOnAxis(ap=M.place[:, i, b:b + 1], axis=0),
                                            in_=M.value[:, b, :], in_offset=None).then_inc(scattered, 16)
            pool.wait_ge(scattered, 16 * 2 * B)


def experts(nc, M):
    HT = -(-EH // 128)
    HR = [min(128, EH - 128 * t) for t in range(HT)]
    with signals(nc) as signal, ExitStack() as ctx:
        def sb(name, shape):
            return ctx.enter_context(nc.sbuf_tensor(name, shape, fp32))

        def pair(name):
            return [signal(f"{name}{u}") for u in range(2)]

        rows = sb("unit_rows", [128, 2, D])
        rowsT = sb("rowsT", [128, 2, KD, L])
        gate = sb("gate", [128, 2, EH])
        hid = sb("hidden", [128, 2, EH])
        hidT = sb("hiddenT", [128, 2, HT, L])
        done = sb("unit_out", [128, 2, D])
        psum = ctx.enter_context(nc.psum_tensor("unit_psum", [128, 2, 4, 512], fp32))
        TURN, GATE, UP, DOWN = range(4)
        rows_in = pair("rows_in")
        turned = pair("rows_turned")
        rowsT_done = pair("rowsT_done")
        gate_mm = pair("unit_gate_mm")
        gate_done = pair("unit_gate_done")
        hid_done = pair("unit_hid_done")
        hidT_mm = pair("unit_hidT_mm")
        hidT_done = pair("unit_hidT_done")
        down_mm = pair("unit_down_mm")
        down_done = pair("unit_down_done")
        stored = pair("unit_stored")
        block = ctx.enter_context(nc.Block())

        @block.sync
        def _(sp):
            def load(j, u):
                sp.wait_ge(turned[u], j)
                sp.dma_start(rows[:, u, :], M.rows_dram[bass.ds((2 * j + u) * L, L), :]).then_inc(rows_in[u], 16)

            pair_loop(sp, UNITS, load)

        @block.tensor
        def _(pe):
            def turn_rows(j, u):
                pe.wait_ge(rows_in[u], 16 * (j + 1))
                pe.wait_ge(hidT_done[u], j)
                for k in range(KD):
                    mm = pe.transpose(psum[:, u, TURN, k * L:k * L + L], rows[:, u, k * 128:k * 128 + 128], M.ident[:, :])
                mm.then_inc(turned[u], 1)

            def gate_up(j, u):
                e = pe.value_load(M.expert_of[0:1, bass.ds(2 * j + u, 1)], min_val=0, max_val=NE)
                pe.wait_ge(rowsT_done[u], j + 1)
                pe.wait_ge(hid_done[u], j)
                for bank, w in ((GATE, M.wg), (UP, M.wu)):
                    for k in range(KD):
                        mm = pe.matmul(psum[:, u, bank, 0:EH], rowsT[:, u, k, :],
                                       w[:, bass.ds(e, 1), k, :].rearrange("p e n -> p (e n)"),
                                       start=(k == 0), stop=(k == KD - 1))
                mm.then_inc(gate_mm[u], 1)

            def turn_hidden(j, u):
                pe.wait_ge(hid_done[u], j + 1)
                for t in range(HT):
                    mm = pe.transpose(psum[0:HR[t], u, TURN, t * L:t * L + L], hid[:, u, t * 128:t * 128 + HR[t]],
                                      M.ident[:, :])
                mm.then_inc(hidT_mm[u], 1)

            def down(j, u):
                e = pe.value_load(M.expert_of[0:1, bass.ds(2 * j + u, 1)], min_val=0, max_val=NE)
                pe.wait_ge(hidT_done[u], j + 1)
                pe.wait_ge(down_done[u], j)
                for t in range(HT):
                    mm = pe.matmul(psum[:, u, DOWN, 0:D], hidT[0:HR[t], u, t, :],
                                   M.wd[0:HR[t], bass.ds(e, 1), t, :].rearrange("p e n -> p (e n)"),
                                   start=(t == 0), stop=(t == HT - 1))
                mm.then_inc(down_mm[u], 1)

            staged_pair_loop(pe, UNITS, (turn_hidden, 2), (gate_up, 1), (turn_rows, 0), (down, 2))

        @block.scalar
        def _(act):
            def copy_rows(j, u):
                act.wait_ge(turned[u], j + 1)
                act.wait_ge(gate_mm[u], j)
                act.activation(rowsT[:, u, :, :], psum[:, u, TURN, 0:D].rearrange("p (k t) -> p k t", t=L), ACT.Copy
                               ).then_inc(rowsT_done[u], 1)

            def silu(j, u):
                act.wait_ge(gate_mm[u], j + 1)
                act.wait_ge(hid_done[u], j)
                act.activation(gate[:, u, :], psum[:, u, GATE, 0:EH], ACT.Silu).then_inc(gate_done[u], 1)

            def copy_hidden(j, u):
                act.wait_ge(hidT_mm[u], j + 1)
                act.wait_ge(down_mm[u], j)
                act.activation(hidT[:, u, 0:HT - 1, :], psum[:, u, TURN, 0:(HT - 1) * L].rearrange("p (k t) -> p k t", t=L),
                               ACT.Copy)
                act.activation(hidT[0:HR[-1], u, HT - 1, :], psum[0:HR[-1], u, TURN, (HT - 1) * L:HT * L],
                               ACT.Copy).then_inc(hidT_done[u], 1)

            def store(j, u):
                act.wait_ge(down_done[u], j + 1)
                act.dma_start(M.outs_dram[bass.ds((2 * j + u) * L, L), :], done[:, u, :]).then_inc(stored[u], 16)

            staged_pair_loop(act, UNITS, (copy_hidden, 2), (silu, 1), (copy_rows, 0), (store, 3))
            for u in range(2):
                act.wait_ge(stored[u], 16 * (UNITS // 2))

        @block.vector
        def _(dve):
            def multiply(j, u):
                dve.wait_ge(gate_done[u], j + 1)
                dve.wait_ge(hidT_mm[u], j)
                dve.tensor_tensor(hid[:, u, :], psum[:, u, UP, 0:EH], gate[:, u, :], ALU.mult).then_inc(hid_done[u], 1)

            def copy_out(j, u):
                dve.wait_ge(down_mm[u], j + 1)
                dve.wait_ge(stored[u], 16 * j)
                dve.tensor_copy(done[:, u, :], psum[:, u, DOWN, 0:D]).then_inc(down_done[u], 1)

            staged_pair_loop(dve, UNITS, (multiply, 1), (copy_out, 2))


def combine(nc, M, out):
    NBUF = 4
    with signals(nc) as signal, ExitStack() as ctx:
        def sb(name, shape):
            return ctx.enter_context(nc.sbuf_tensor(name, shape, fp32))

        got = sb("gathered", [128, NBUF, 2, D])
        shared = sb("shared_out", [128, NBUF, D])
        acc = sb("sum_out", [128, NBUF, D])
        bn = sb("ln_stats3", [128, B, 6])
        mv = sb("ln_mean_var3", [128, B, 2])
        rstd = sb("ln_rstd3", [128, B])
        gathered = [signal(f"gathered{i}") for i in range(NBUF)]
        shared_in = [signal(f"shared_in{i}") for i in range(NBUF)]
        summed = signal("summed")
        steps = signal("combine_step")
        var_done = signal("var_done")
        rstd_done = signal("rstd_done")
        normed = signal("normed")
        out_stored = signal("out_stored")
        block = ctx.enter_context(nc.Block())

        @block.gpsimd
        def _(pool):
            for b in range(B):
                if b >= NBUF:
                    pool.wait_ge(summed, b - NBUF + 1)
                for i in range(2):
                    pool.indirect_dma_start(out=got[:, b % NBUF, i, :], out_offset=None, in_=M.outs_dram[:, :],
                                            in_offset=bass.IndirectOffsetOnAxis(ap=M.place[:, i, b:b + 1], axis=0)
                                            ).then_inc(gathered[b % NBUF], 16)
                if b >= 2:
                    pool.wait_ge(var_done, b - 1)
                    pool.tensor_tensor(rstd[:, b - 2:b - 1], mv[:, b - 2, 1:2], M.minus_half[:, 0:1], ALU.pow).then_inc(rstd_done, 1)
            for b in (B - 2, B - 1):
                pool.wait_ge(var_done, b + 1)
                pool.tensor_tensor(rstd[:, b:b + 1], mv[:, b, 1:2], M.minus_half[:, 0:1], ALU.pow).then_inc(rstd_done, 1)

        @block.sync
        def _(sp):
            for b in range(B):
                if b >= NBUF:
                    sp.wait_ge(summed, b - NBUF + 1)
                sp.dma_start(shared[:, b % NBUF, :], M.outs_dram[b * L:b * L + L, :]).then_inc(shared_in[b % NBUF], 16)
                if b >= 3:
                    sp.wait_ge(normed, b - 2)
                    sp.dma_start(out[(b - 3) * L:(b - 2) * L, :], M.value[:, b - 3, :]).then_inc(out_stored, 16)
            for b in (B - 3, B - 2, B - 1):
                sp.wait_ge(normed, b + 1)
                sp.dma_start(out[b * L:b * L + L, :], M.value[:, b, :]).then_inc(out_stored, 16)
            sp.wait_ge(out_stored, 16 * B)

        @block.vector
        def _(dve):
            count = [0]

            def link(ins):
                count[0] += 1
                ins.then_inc(steps, 1)
                dve.wait_ge(steps, count[0])

            def normalize(b):
                dve.wait_ge(rstd_done, b + 1)
                dve.tensor_scalar(M.value[:, b, :], M.value[:, b, :], mv[:, b, 0:1], rstd[:, b:b + 1], ALU.subtract,
                                  ALU.mult).then_inc(normed, 1)

            for b in range(B):
                v = M.value[:, b, :]
                r = b % NBUF
                dve.wait_ge(shared_in[r], 16 * (b // NBUF + 1))
                link(dve.tensor_tensor(acc[:, r, :], v, shared[:, r, :], ALU.add))
                dve.wait_ge(gathered[r], 32 * (b // NBUF + 1))
                link(dve.scalar_tensor_tensor(out=acc[:, r, :], in0=got[:, r, 0, :], scalar=M.weight[:, b, 0:1],
                                              in1=acc[:, r, :], op0=ALU.mult, op1=ALU.add))
                dve.scalar_tensor_tensor(out=v, in0=got[:, r, 1, :], scalar=M.weight[:, b, 1:2],
                                         in1=acc[:, r, :], op0=ALU.mult, op1=ALU.add).then_inc(summed, 1)
                dve.wait_ge(summed, b + 1)
                link(dve.bn_stats(bn[:, b, :], v))
                link(dve.bn_aggr(mv[:, b, :], bn[:, b, :]))
                dve.tensor_scalar(mv[:, b, 1:2], mv[:, b, 1:2], 1e-5, None, ALU.add).then_inc(var_done, 1)
                if b >= 3:
                    normalize(b - 3)
            for b in (B - 3, B - 2, B - 1):
                normalize(b)


def program(nc, M, out):
    with ExitStack() as ctx:
        def sb(name, shape, dt=fp32):
            return ctx.enter_context(nc.sbuf_tensor(name, shape, dt))

        M.value = sb("value", [128, B, D])
        M.ident = sb("ident", [128, 128])
        M.causal = sb("causal", [128, 128])
        M.reverse = sb("reverse", [128, 128])
        M.reverse_first = sb("reverse_first", [128, 128])
        M.off32 = sb("off32", [128, 128])
        M.off64 = sb("off64", [128, 128])
        M.blockdiag = sb("blockdiag", [128, 128])
        M.minus_half = sb("minus_half", [128, 1])
        M.plus_half = sb("plus_half", [128, 1])
        M.euler = sb("euler", [128, 1])
        M.rq = sb("rq", [128, B, H])
        M.beta_r = sb("beta_r", [128, B, H])
        M.decay = sb("decay", [128, B, H])
        M.inv_tau = sb("inv_tau", [128, H])
        M.floor = sb("floor", [128, H, NP])
        M.keep = sb("keep", [128, H])
        M.gb2 = sb("gb2", [128, H * NP])
        M.gb1 = sb("gb1", [128, GH // 128])
        M.stat_scale = sb("stat_scale", [80, 1])
        M.wo = sb("wo", [128, KD, D])
        M.gw1x = sb("gw1x", [128, KD, GH])
        M.gw1s = sb("gw1s", [80, GH])
        M.gw2 = sb("gw2", [128, GH // 128, H * NP])
        M.logits = sb("router_logits", [128, B, NE])
        M.weight = sb("expert_weight", [128, B, 2])
        M.place = sb("row_of_token", [128, 2, B], mybir.dt.uint32)
        M.expert_of = sb("expert_of_unit", [128, UNITS], mybir.dt.uint32)
        build_constants(nc, M)
        project(nc, M)
        with ExitStack() as mixing:
            M.filtered = mixing.enter_context(nc.sbuf_tensor("filtered", [128, B, len(FIRS), D], fp32))
            invert_and_filter(nc, M)
            mix_paths(nc, M)
        M.wg = sb("wg", [128, NE + 1, KD, EH])
        M.wu = sb("wu", [128, NE + 1, KD, EH])
        M.wd = sb("wd", [128, NE + 1, -(-EH // 128), D])
        load_experts(nc, M)
        attend(nc, M)
        route(nc, M)
        experts(nc, M)
        combine(nc, M, out)


def kernel(**inputs):
    import numpy as np
    import concourse.bacc as bacc
    from concourse.bass_utils import run_bass_kernel_spmd

    a = {k: np.asarray(v) for k, v in inputs.items()}
    f = {k[len("L0_"):]: v for k, v in a.items() if k.startswith("L0_")}
    tokens = B * L
    x = a["x"].reshape(tokens, D)
    fir = np.zeros((FIR_PAD, len(FIRS), D), np.float32)
    for i, (name, taps) in enumerate(zip(("attn_fir_s", "attn_fir_m", "attn_fir_l"), FIRS)):
        fir[HALF - 1:HALF - 1 + taps, i, :] = f[name][:, ::-1].T
    fir = fir.reshape(FIR_PAD, len(FIRS), NFC, FC).transpose(2, 1, 0, 3)
    stat_scale = np.array([[1 / DV], [1 / DV], [1 / DV], [1.0]] * (H * NP), np.float32)
    arrays = dict(
        x=x, xT=x.T, ctxT=a["ctx_2048"].reshape(tokens, CTX).T, mask=a["mask_BxS2_fk1"],
        wq=f["attn_Wq"], wk=f["attn_Wk"], wv=f["attn_Wv"], wb=f["attn_Wb"],
        conv_q=f["attn_conv_q"], conv_k=f["attn_conv_k"], conv_v=f["attn_conv_v"],
        fir=fir, gw1=f["attn_gW1"], gw1s=f["attn_gW1"][D:].reshape(H * NP * 4, DV, GH),
        gb1=f["attn_gb1"].reshape(GH // 128, 128).T, gw2=f["attn_gW2"], gb2=f["attn_gb2"],
        log_tau=f["attn_log_tau"], eps_logit=f["attn_eps_logit"],
        norm_w=f["attn_norm_w"].reshape(DV, 1), wo=f["attn_Wo"], stat_scale=stat_scale,
        w_srcT=f["xattn_W_src"].T, b_src=f["xattn_b_src"], w_tgtT=f["xattn_W_tgt"].T, b_tgt=f["xattn_b_tgt"].reshape(KD, 128).T,
        b_key=f["xattn_b_src"][0:D].reshape(KD, 128).T, mask_col=a["mask_BxS2_fk1"].reshape(tokens, 1),
        w_outT=f["xattn_W_out"].T, b_out=f["xattn_b_out"], w_routerT=f["ffn_w_router"].T,
        wg=f["ffn_wg"], wu=f["ffn_wu"], wd=f["ffn_wd"], wg_s=f["ffn_wg_s"], wu_s=f["ffn_wu_s"], wd_s=f["ffn_wd_s"],
    )
    nc = bacc.Bacc("TRN2", target_bir_lowering=False, num_devices=1)
    M = Memory()
    given = {}
    ap = {}
    for name, v in arrays.items():
        v = np.ascontiguousarray(v)
        given[f"in_{name}"] = v
        ap[name] = nc.dram_tensor(f"in_{name}", v.shape, mybir.dt.from_np(v.dtype), kind="ExternalInput").ap()
    M.x_dram, M.xT_dram, M.ctxT_dram, M.mask_dram = ap["x"], ap["xT"], ap["ctxT"], ap["mask"]
    M.mask_col_dram, M.b_key_dram = ap["mask_col"], ap["b_key"]
    M.wq_dram, M.wk_dram, M.wv_dram, M.wb_dram = ap["wq"], ap["wk"], ap["wv"], ap["wb"]
    M.conv_q_dram, M.conv_k_dram, M.conv_v_dram = ap["conv_q"], ap["conv_k"], ap["conv_v"]
    M.fir_dram, M.gw1_dram, M.gw1s_dram, M.gb1_dram = ap["fir"], ap["gw1"], ap["gw1s"], ap["gb1"]
    M.gw2_dram, M.gb2_dram, M.log_tau, M.eps_logit = ap["gw2"], ap["gb2"], ap["log_tau"], ap["eps_logit"]
    M.norm_w_dram, M.wo_dram, M.stat_scale_dram = ap["norm_w"], ap["wo"], ap["stat_scale"]
    M.w_srcT_dram, M.b_src_dram, M.w_tgtT_dram, M.b_tgt_dram = ap["w_srcT"], ap["b_src"], ap["w_tgtT"], ap["b_tgt"]
    M.w_outT_dram, M.b_out_dram, M.w_routerT_dram = ap["w_outT"], ap["b_out"], ap["w_routerT"]
    M.wg_dram, M.wu_dram, M.wd_dram = ap["wg"], ap["wu"], ap["wd"]
    M.wg_s_dram, M.wu_s_dram, M.wd_s_dram = ap["wg_s"], ap["wu_s"], ap["wd_s"]
    M.qT_dram = nc.dram_tensor("qT", [D, tokens], fp32).ap()
    M.kT_dram = nc.dram_tensor("kT", [D, tokens], fp32).ap()
    M.nd_dram = nc.dram_tensor("nd", [B, H, L, CB], fp32).ap()
    M.inv_dram = nc.dram_tensor("inv", [B, H, L, CB], fp32).ap()
    M.rows_dram = nc.dram_tensor("rows", [UNITS * L, D], fp32).ap()
    M.outs_dram = nc.dram_tensor("outs", [UNITS * L, D], fp32).ap()
    out = nc.dram_tensor("out", [tokens, D], fp32, kind="ExternalOutput").ap()
    program(nc, M, out)
    r = run_bass_kernel_spmd(nc, [given], core_ids=[0])
    return r.results[0]["out"].reshape(B, L, D)
```
